# Optimizing a Trainium2 kernel written in Bass

```python
import numpy as np
import jax
import jax.numpy as jnp

def _softmax(x, axis=-1):
    return jax.nn.softmax(x, axis=axis)

def _gelu(x):
    return jax.nn.gelu(x, approximate=True)

def _silu(x):
    return jax.nn.silu(x)

def _sigmoid(x):
    return jax.nn.sigmoid(x)

def _layernorm(x, axis=-1, eps=1e-05):
    m = jnp.mean(x, axis=axis, keepdims=True)
    v = jnp.var(x, axis=axis, keepdims=True)
    return (x - m) / jnp.sqrt(v + eps)

def _scatter_add(tgt, idx, src, axis=0):
    return tgt.at[idx].add(src)

def _segment_sum(src, seg, n):
    return jax.ops.segment_sum(src, seg, n)
kernel_name = 'mk_adaln_ffn_d2_seqx_r8_603bf7'

def setup_inputs(seed: int=0):
    np.random.seed(seed)
    _w = jnp.asarray

    def _rec_inputs():
        import jax
        import jax.numpy as jnp
        _rk = jax.random.key(seed)
        x = -0.000125 + 0.9999 * jax.random.normal(jax.random.fold_in(_rk, 1), (64, 32, 512), jnp.float32)
        _lenS = 32 - jax.random.randint(jax.random.fold_in(_rk, 7), (64,), 0, max(1, 32 // 4) + 1, jnp.int32)
        _lenS2 = 32 - jax.random.randint(jax.random.fold_in(_rk, 8), (64,), 0, max(1, 32 // 4) + 1, jnp.int32)
        itok_B_0_23 = jax.random.randint(jax.random.fold_in(_rk, 11), (64,), 0, 24, jnp.int32)
        itok_B_2_6 = jax.random.randint(jax.random.fold_in(_rk, 12), (64,), 2, 7, jnp.int32)
        return (x, itok_B_0_23, itok_B_2_6)
    x, itok_B_0_23, itok_B_2_6 = _rec_inputs()

    def _L0_cond_setup():
        import jax, jax.numpy as jnp
        import numpy as np
        R = 16
        ALPHA = 32
        SCALING = ALPHA / R
        SLOTS = 32
        IN_F = 512
        OUT_F = 512
        B, T = (8, 128)
        key = jax.random.key(seed)
        k1, k2, k3, k4, k5, k6 = jax.random.split(key, 6)
        x = jax.random.normal(k1, (B, T, IN_F), dtype=jnp.float32)
        adapter_mapping = jax.random.randint(k2, (B,), 0, SLOTS, dtype=jnp.int32)
        W = jax.random.normal(k3, (OUT_F, IN_F), dtype=jnp.float32) * 0.02
        b = jax.random.normal(k4, (OUT_F,), dtype=jnp.float32) * 0.02
        lora_As = jax.random.normal(k5, (SLOTS, IN_F, R), dtype=jnp.float32) * 0.02
        lora_Bs = jax.random.normal(k6, (SLOTS, R, OUT_F), dtype=jnp.float32) * 0.02
        return {'x': x, 'adapter_mapping': adapter_mapping, 'W': W, 'b': b, 'lora_As': lora_As, 'lora_Bs': lora_Bs}
    _L0_cond_all = _L0_cond_setup()
    _L0_cond_in = {k: v for k, v in _L0_cond_all.items() if k in ('W', 'b', 'lora_As', 'lora_Bs')}
    del _L0_cond_all

    def _L0_ffn_setup():
        import jax, jax.numpy as jnp
        import numpy as np
        GROUP_SIZE = 64
        BITS = 4
        VALS_PER_WORD = 32 // BITS

        def _dequantize(qweight, scales, zeros):
            O, packed = qweight.shape
            shifts = jnp.arange(VALS_PER_WORD, dtype=jnp.uint32) * BITS
            wq = qweight[:, :, None] >> shifts[None, None, :] & jnp.uint32((1 << BITS) - 1)
            wq = wq.reshape(O, packed * VALS_PER_WORD).astype(jnp.float32)
            s = jnp.repeat(scales, GROUP_SIZE, axis=1)
            z = jnp.repeat(zeros, GROUP_SIZE, axis=1)
            return wq * s + z
        key = jax.random.key(seed)
        ks = jax.random.split(key, 7)
        B, S, I, O = (4, 256, 512, 512)
        G = I // GROUP_SIZE
        x = jax.random.normal(ks[0], (B, S, I), dtype=jnp.float32)
        channel_scale = jax.random.uniform(ks[1], (1, 1, I), dtype=jnp.float32, minval=0.5, maxval=1.5)
        qweight = jax.random.randint(ks[2], (O, I // VALS_PER_WORD), 0, 2147483647, dtype=jnp.int32).astype(jnp.uint32)
        q_perm = jax.random.permutation(ks[3], I).astype(jnp.int32)
        scales = jax.random.uniform(ks[4], (O, G), dtype=jnp.float32, minval=0.001, maxval=0.02)
        zeros = jax.random.normal(ks[5], (O, G), dtype=jnp.float32) * 0.05
        bias = jax.random.normal(ks[6], (O,), dtype=jnp.float32) * 0.02
        return {'x': x, 'channel_scale': channel_scale, 'qweight': qweight, 'q_perm': q_perm, 'scales': scales, 'zeros': zeros, 'bias': bias}
    _L0_ffn_all = _L0_ffn_setup()
    _L0_ffn_in = {k: v for k, v in _L0_ffn_all.items() if k in ('channel_scale', 'qweight', 'q_perm', 'scales', 'zeros', 'bias')}
    del _L0_ffn_all

    def _L1_cond_setup():
        import jax, jax.numpy as jnp
        import numpy as np
        B, N, H, F = (4, 64, 512, 1376)
        L, R, RANK = (1, 16, 16)
        SCALE = 0.5
        key = jax.random.key(seed)
        ks = jax.random.split(key, 12)
        nrm = lambda k, shape, fan: jax.random.normal(k, shape, jnp.float32) * fan ** (-0.5)
        inp = {'x': jax.random.normal(ks[0], (B, N, H), jnp.float32), 'W_gate': nrm(ks[1], (F, H), H), 'W_up': nrm(ks[2], (F, H), H), 'W_down': nrm(ks[3], (H, F), F), 'A_gate': nrm(ks[4], (L, R, RANK, H), H), 'B_gate': nrm(ks[5], (L, R, F, RANK), RANK), 'A_up': nrm(ks[6], (L, R, RANK, H), H), 'B_up': nrm(ks[7], (L, R, F, RANK), RANK), 'A_down': nrm(ks[8], (L, R, RANK, F), F), 'B_down': nrm(ks[9], (L, R, H, RANK), RANK), 'lora_indices': jax.random.randint(ks[10], (B,), 0, R), 'layer_idx': 0}
        return inp
    _L1_cond_all = _L1_cond_setup()
    _L1_cond_in = {k: v for k, v in _L1_cond_all.items() if k in ('W_gate', 'W_up', 'W_down', 'A_gate', 'B_gate', 'A_up', 'B_up', 'A_down', 'B_down')}
    del _L1_cond_all

    def _L1_ffn_setup():
        import jax, jax.numpy as jnp
        import numpy as np
        N_STREAMS = 4
        DIM = 128
        SINKHORN_ITERS = 50
        SINKHORN_TAU = 0.1
        RMS_EPS = 1.1920929e-07

        def sinkhorn_log(logits, num_iters=SINKHORN_ITERS, tau=SINKHORN_TAU):
            Z = logits / tau
            u0 = jnp.zeros(Z.shape[:-1], Z.dtype)
            v0 = jnp.zeros_like(u0)

            def step(carry, _):
                u, v = carry
                u = -jax.nn.logsumexp(Z + v[..., None, :], axis=-1)
                v = -jax.nn.logsumexp(Z + u[..., :, None], axis=-2)
                return ((u, v), None)
            (u, v), _ = jax.lax.scan(step, (u0, v0), None, length=num_iters)
            return jnp.exp(Z + u[..., :, None] + v[..., None, :])
        key = jax.random.key(seed)
        ks = jax.random.split(key, 6)
        B, T = (4, 256)
        n, C = (N_STREAMS, DIM)
        wd = n * C
        x = jax.random.normal(ks[0], (B, T, wd), dtype=jnp.float32)
        W_res = 0.01 * jax.random.normal(ks[1], (n * n, wd), dtype=jnp.float32)
        W_pre = 0.01 * jax.random.normal(ks[2], (n, wd), dtype=jnp.float32)
        W_post = 0.01 * jax.random.normal(ks[3], (n, wd), dtype=jnp.float32)
        H_res_base = jnp.full((n, n), -0.5, dtype=jnp.float32)
        H_res_base = H_res_base.at[jnp.arange(n), jnp.arange(n)].set(0.0)
        H_pre_base = jnp.zeros((n,), dtype=jnp.float32).at[0].set(1.0)
        H_post_base = jnp.zeros((n,), dtype=jnp.float32)
        gate = jnp.array([5.0], dtype=jnp.float32)
        W_branch = 1.0 / np.sqrt(C) * jax.random.normal(ks[4], (C, C), dtype=jnp.float32)
        return {'x': x, 'W_res': W_res, 'W_pre': W_pre, 'W_post': W_post, 'H_res_base': H_res_base, 'H_pre_base': H_pre_base, 'H_post_base': H_post_base, 'gate': gate, 'W_branch': W_branch}
    _L1_ffn_all = _L1_ffn_setup()
    _L1_ffn_in = {k: v for k, v in _L1_ffn_all.items() if k in ('W_res', 'W_pre', 'W_post', 'H_res_base', 'H_pre_base', 'H_post_base', 'gate', 'W_branch')}
    del _L1_ffn_all
    return {'x': x, 'itok_B_0_23': itok_B_0_23, 'itok_B_2_6': itok_B_2_6, 'L0_cond_W': _L0_cond_in['W'], 'L0_cond_b': _L0_cond_in['b'], 'L0_cond_lora_As': _L0_cond_in['lora_As'], 'L0_cond_lora_Bs': _L0_cond_in['lora_Bs'], 'L0_ffn_channel_scale': _L0_ffn_in['channel_scale'], 'L0_ffn_qweight': _L0_ffn_in['qweight'], 'L0_ffn_q_perm': _L0_ffn_in['q_perm'], 'L0_ffn_scales': _L0_ffn_in['scales'], 'L0_ffn_zeros': _L0_ffn_in['zeros'], 'L0_ffn_bias': _L0_ffn_in['bias'], 'L1_cond_W_gate': _L1_cond_in['W_gate'], 'L1_cond_W_up': _L1_cond_in['W_up'], 'L1_cond_W_down': _L1_cond_in['W_down'], 'L1_cond_A_gate': _L1_cond_in['A_gate'], 'L1_cond_B_gate': _L1_cond_in['B_gate'], 'L1_cond_A_up': _L1_cond_in['A_up'], 'L1_cond_B_up': _L1_cond_in['B_up'], 'L1_cond_A_down': _L1_cond_in['A_down'], 'L1_cond_B_down': _L1_cond_in['B_down'], 'L1_ffn_W_res': _L1_ffn_in['W_res'], 'L1_ffn_W_pre': _L1_ffn_in['W_pre'], 'L1_ffn_W_post': _L1_ffn_in['W_post'], 'L1_ffn_H_res_base': _L1_ffn_in['H_res_base'], 'L1_ffn_H_pre_base': _L1_ffn_in['H_pre_base'], 'L1_ffn_H_post_base': _L1_ffn_in['H_post_base'], 'L1_ffn_gate': _L1_ffn_in['gate'], 'L1_ffn_W_branch': _L1_ffn_in['W_branch']}

def reference(x, itok_B_0_23, itok_B_2_6, L0_cond_W, L0_cond_b, L0_cond_lora_As, L0_cond_lora_Bs, L0_ffn_channel_scale, L0_ffn_qweight, L0_ffn_q_perm, L0_ffn_scales, L0_ffn_zeros, L0_ffn_bias, L1_cond_W_gate, L1_cond_W_up, L1_cond_W_down, L1_cond_A_gate, L1_cond_B_gate, L1_cond_A_up, L1_cond_B_up, L1_cond_A_down, L1_cond_B_down, L1_ffn_W_res, L1_ffn_W_pre, L1_ffn_W_post, L1_ffn_H_res_base, L1_ffn_H_pre_base, L1_ffn_H_post_base, L1_ffn_gate, L1_ffn_W_branch):
    import jax
    import jax.numpy as jnp

    def _L0_cond_ref(x, adapter_mapping, W, b, lora_As, lora_Bs):
        import jax, jax.numpy as jnp
        import numpy as np
        R = 16
        ALPHA = 32
        SCALING = ALPHA / R
        SLOTS = 32
        IN_F = 512
        OUT_F = 512
        B, T = (8, 128)
        base_out = jnp.einsum('bti,oi->bto', x, W) + b
        A = lora_As[adapter_mapping]
        Bm = lora_Bs[adapter_mapping]
        lora_h = jnp.einsum('bti,bir->btr', x, A)
        lora_out = jnp.einsum('btr,bro->bto', lora_h, Bm)
        return base_out + lora_out * SCALING

    def _L0_ffn_ref(x, channel_scale, qweight, q_perm, scales, zeros, bias):
        import jax, jax.numpy as jnp
        import numpy as np
        GROUP_SIZE = 64
        BITS = 4
        VALS_PER_WORD = 32 // BITS

        def _dequantize(qweight, scales, zeros):
            O, packed = qweight.shape
            shifts = jnp.arange(VALS_PER_WORD, dtype=jnp.uint32) * BITS
            wq = qweight[:, :, None] >> shifts[None, None, :] & jnp.uint32((1 << BITS) - 1)
            wq = wq.reshape(O, packed * VALS_PER_WORD).astype(jnp.float32)
            s = jnp.repeat(scales, GROUP_SIZE, axis=1)
            z = jnp.repeat(zeros, GROUP_SIZE, axis=1)
            return wq * s + z
        x = x * channel_scale
        x = jnp.take(x, q_perm, axis=-1)
        W = _dequantize(qweight, scales, zeros)
        out = jnp.einsum('bsi,oi->bso', x, W)
        return out + bias

    def _L1_cond_ref(x, W_gate, W_up, W_down, A_gate, B_gate, A_up, B_up, A_down, B_down, lora_indices, layer_idx):
        import jax, jax.numpy as jnp
        import numpy as np
        B, N, H, F = (4, 64, 512, 1376)
        L, R, RANK = (1, 16, 16)
        SCALE = 0.5

        def lora_add(base, inp, A, B):
            Ab = A[layer_idx][lora_indices]
            Bb = B[layer_idx][lora_indices]
            t = jnp.einsum('bri,bni->bnr', Ab, inp)
            return base + jnp.einsum('bor,bnr->bno', Bb, t) * SCALE
        gate = lora_add(jnp.einsum('bnh,fh->bnf', x, W_gate), x, A_gate, B_gate)
        up = lora_add(jnp.einsum('bnh,fh->bnf', x, W_up), x, A_up, B_up)
        act = jax.nn.silu(gate) * up
        down = lora_add(jnp.einsum('bnf,hf->bnh', act, W_down), act, A_down, B_down)
        return down

    def _L1_ffn_ref(x, W_res, W_pre, W_post, H_res_base, H_pre_base, H_post_base, gate, W_branch):
        import jax, jax.numpy as jnp
        import numpy as np
        N_STREAMS = 4
        DIM = 128
        SINKHORN_ITERS = 50
        SINKHORN_TAU = 0.1
        RMS_EPS = 1.1920929e-07

        def sinkhorn_log(logits, num_iters=SINKHORN_ITERS, tau=SINKHORN_TAU):
            Z = logits / tau
            u0 = jnp.zeros(Z.shape[:-1], Z.dtype)
            v0 = jnp.zeros_like(u0)

            def step(carry, _):
                u, v = carry
                u = -jax.nn.logsumexp(Z + v[..., None, :], axis=-1)
                v = -jax.nn.logsumexp(Z + u[..., :, None], axis=-2)
                return ((u, v), None)
            (u, v), _ = jax.lax.scan(step, (u0, v0), None, length=num_iters)
            return jnp.exp(Z + u[..., :, None] + v[..., None, :])
        B, T, nC = x.shape
        n = N_STREAMS
        C = nC // n
        x_norm = x * jax.lax.rsqrt(jnp.mean(x * x, axis=-1, keepdims=True) + RMS_EPS)
        H_res_logits = (x_norm @ W_res.T).reshape(B, T, n, n) + H_res_base
        H_pre_logits = x_norm @ W_pre.T + H_pre_base
        H_post_logits = x_norm @ W_post.T + H_post_base
        H_res = sinkhorn_log(H_res_logits)
        H_pre = jax.nn.softmax(H_pre_logits, axis=-1)
        H_post = jax.nn.softmax(H_post_logits, axis=-1)
        g = jax.nn.sigmoid(gate)[0]
        I = jnp.eye(n, dtype=H_res.dtype)
        H_res = (1.0 - g) * I + g * H_res
        x_streams = x.reshape(B, T, n, C)
        x_pre = jnp.einsum('btnc,btn->btc', x_streams, H_pre)
        y = x_pre @ W_branch
        x_mixed = jnp.einsum('btij,btjc->btic', H_res, x_streams)
        y_distributed = jnp.einsum('btc,btn->btnc', y, H_post)
        return (x_mixed + y_distributed).reshape(B, T, nC)
    x = x + _L0_ffn_ref(_L0_cond_ref(x, itok_B_0_23, L0_cond_W, L0_cond_b, L0_cond_lora_As, L0_cond_lora_Bs), L0_ffn_channel_scale, L0_ffn_qweight, L0_ffn_q_perm, L0_ffn_scales, L0_ffn_zeros, L0_ffn_bias)
    x = x + _L1_ffn_ref(_L1_cond_ref(x, L1_cond_W_gate, L1_cond_W_up, L1_cond_W_down, L1_cond_A_gate, L1_cond_B_gate, L1_cond_A_up, L1_cond_B_up, L1_cond_A_down, L1_cond_B_down, itok_B_2_6, 0), L1_ffn_W_res, L1_ffn_W_pre, L1_ffn_W_post, L1_ffn_H_res_base, L1_ffn_H_pre_base, L1_ffn_H_post_base, L1_ffn_gate, L1_ffn_W_branch)
    return x

_drawn_inputs = setup_inputs


def setup_inputs(seed=0):
    import zlib

    import numpy as np

    out = dict(_drawn_inputs(seed))
    spreads = {'L1_ffn_H_post_base': (0.0, 0.432)}
    factors = {'L0_ffn_bias': 3.273}
    for name, (base, spread) in spreads.items():
        noise = np.random.default_rng([zlib.crc32(name.encode()), seed]).standard_normal(out[name].shape)
        drawn = base * np.exp(spread * noise) if base else spread * noise
        out[name] = jnp.asarray(drawn.astype(out[name].dtype))
    for name, factor in factors.items():
        out[name] = (out[name] * factor).astype(out[name].dtype)
    return out
```

```python
from contextlib import ExitStack

import concourse.bass as bass
from concourse import mybir

F32 = mybir.dt.float32
F16 = mybir.dt.float16
I32 = mybir.dt.int32
U32 = mybir.dt.uint32
ALU = mybir.AluOpType
ACT = mybir.ActivationFunctionType
AX = mybir.AxisListType

P = 128
BATCH, SEQ, D = 64, 32, 512
TOK = BATCH * SEQ
KT = D // P
RANK = 16
SLOTS0, SLOTS1 = 32, 16
F = 1376
FT = -(-F // P)
FL = F - (FT - 1) * P
NGROUP = 8
C0 = 512
N0 = TOK // C0
T0 = C0 // P
B0 = C0 // SEQ
G0 = B0 // 2
C1 = 256
N1 = TOK // C1
T1 = C1 // P
B1 = C1 // SEQ
G1 = B1 // 2
PAIR = 2 * SEQ
PIECES = 4
DT_PIECE = 3
A1W = KT * 2 * RANK + FT * RANK
GUW = KT * 2 * RANK
B1W = 2 * F + D
GU = 2 * F
NPROJ = 24
ROUNDS = 50
RMS_EPS = 1.1920929e-07

SCALE = 256.0
INV = 1.0 / SCALE
LORA0 = 2.0 * INV
LORA1 = 0.5 * INV
PASSES = ((0, 0), (1, 0), (0, 1))


def wait(eng, sem, value):
    if not isinstance(value, int) or value > 0:
        eng.wait_ge(sem, value)


def build(nc, a, out):
    ctx = ExitStack()
    with ctx:
        def maker(stack):
            return lambda name, shape, dt: stack.enter_context(nc.sbuf_tensor(name, shape, dt))

        sb = maker(ctx)

        xT = sb("xT", [P, KT, TOK + C1], F32)
        ident32 = sb("ident32", [P, P], F32)
        ident16 = sb("ident16", [P, P], F16)
        mask0 = sb("mask0", [P, 4, RANK], F32)
        mask1 = sb("mask1", [P, 4, RANK], F32)
        slot0 = sb("slot0", [1, BATCH], I32)
        slot1 = sb("slot1", [1, BATCH + B1], I32)
        proj = sb("proj", [P, KT, NPROJ], F32)
        base = sb("base", [P, NPROJ], F32)
        gate = sb("gate", [P, 2], F32)
        branch = sb("branch", [P, P], F32)
        chan = sb("chan", [P, KT], F32)
        b0 = sb("b0", [P, KT], F32)
        b0s = sb("b0s", [P, KT, 2], F16)
        fbias = sb("fbias", [P, KT], F32)
        csum = sb("csum", [P, KT], F32)
        cvec = sb("cvec", [P, KT], F32)
        perm_i = sb("perm_i", [P, KT], I32)
        perm_f = sb("perm_f", [P, KT], F32)
        shift = sb("shift", [P, 1], I32)
        shift4 = sb("shift4", [P, 1], I32)

        setup = ExitStack()
        st = maker(setup)
        q = st("q", [P, KT, D], U32)
        q4 = st("q4", [P, KT, D], U32)
        sc = st("sc", [P, KT, D], F32)
        zr = st("zr", [P, KT, D], F32)
        w_in = st("w_in", [P, KT, D], F32)
        a0_in = st("a0_in", [P, SLOTS0, KT * RANK], F32)
        a0_out = st("a0_out", [P, SLOTS0, 2, KT * RANK], F16)
        b0_in = st("b0_in", [P, KT, D], F32)
        b0_out = st("b0_out", [P, 2, KT, D], F16)
        onehot = st("onehot", [P, KT, D], F16)
        col_i = st("col_i", [P, D], I32)
        setup.close()

        wg = sb("wg", [P, 2, KT, F], F16)
        wu = sb("wu", [P, 2, KT, F], F16)
        wd = sb("wd", [P, 2, PIECES * DT_PIECE, D], F16)

        layer0 = ExitStack()
        l0 = maker(layer0)
        sb_out = l0("sb_out", [P, 2, B1W // 2], F16)
        sa_out = l0("sa_out", [P, SLOTS1 // 4, 2, A1W], F16)
        s_g = l0("s_g", [P, F], F32)
        w0 = l0("w0", [P, 2, KT, D], F16)
        mw = l0("mw", [P, 2, KT, D], F16)
        xs = l0("xs", [P, 2, KT, C0], F16)
        hs = l0("hs", [P, 2, KT, C0], F16)
        o_sb = l0("o_sb", [P, 2, C0], F32)
        a0g = l0("a0g", [P, B0, 2, KT * RANK], F16)
        b0g = l0("b0g", [P, G0, D], F16)
        t0_f = l0("t0_f", [P, T0 * 4, RANK], F32)
        t0_s = l0("t0_s", [P, T0 * 4, 4, RANK], F16)
        t0_t = l0("t0_t", [P, C0], F16)
        wq16 = l0("wq16", [P, 2, KT, D], F16)
        s_u = l0("s_u", [P, F], F32)
        s_d = l0("s_d", [P, DT_PIECE, D], F32)
        s_a = l0("s_a", [P, SLOTS1 // 4, A1W], F32)
        s_b = l0("s_b", [P, B1W // 2], F32)
        layer0.close()

        a0_tab = nc.dram_tensor("a0_tab", [SLOTS0, P, 2 * KT * RANK], F16, kind="Internal")
        b0_tab = nc.dram_tensor("b0_tab", [SLOTS0, 2, RANK, D], F16, kind="Internal")
        a1_tab = nc.dram_tensor("a1_tab", [SLOTS1, P, 2 * A1W], F16, kind="Internal")
        b1_tab = nc.dram_tensor("b1_tab", [SLOTS1, 2, RANK, B1W], F16, kind="Internal")

        psum0 = ExitStack()

        def ps(name, shape, dt=F32, stack=psum0):
            return stack.enter_context(nc.psum_tensor(name, shape, dt))

        p_h = ps("p_h", [P, 4, D])
        p_t = ps("p_t", [P, 2 * T0 * 4, RANK])
        p_tt = ps("p_tt", [P, 2 * C0], F16)
        p_o = ps("p_o", [P, 2, D])
        psum0.close()

        with ExitStack() as sems0:
            def sem(name):
                return sems0.enter_context(nc.semaphore(name))

            ld_small, ld_q, ld_w, ld_a0, ld_b0, ld_x, ld_const = (
                sem(n) for n in "ld_small ld_q ld_w ld_a0 ld_b0 ld_x ld_const".split())
            ld_g, ld_u, ld_d, ld_a1, ld_b1 = (sem(n) for n in "ld_g ld_u ld_d ld_a1 ld_b1".split())
            consts, z_ready = sem("consts"), sem("z_ready")
            deq = sem("deq")
            w_hi, w_lo = sem("w_hi"), sem("w_lo")
            m_ps, m_hi, m_lo = sem("m_ps"), sem("m_hi"), sem("m_lo")
            c_ps, c_done = sem("c_ps"), sem("c_done")
            wr_a0, wr_b0, wr_a1, wr_b1, got_a, got_b = (
                sem(n) for n in "wr_a0 wr_b0 wr_a1 wr_b1 got_a got_b".split())
            x_hi, x_lo, a_ps, t_f, t_hi, t_lo, tt_ps, tt_sb, base_done = (
                sem(n) for n in "x_hi x_lo a_ps t_f t_hi t_lo tt_ps tt_sb base_done".split())
            h_ps, h_hi, h_lo, o_ps, o_up, x1 = (sem(n) for n in "h_ps h_hi h_lo o_ps o_up x1".split())
            s_hi, s_lo = sem("s_hi"), sem("s_lo")

            block = sems0.enter_context(nc.Block())

            @block.sync
            def _(sp):
                sp.dma_start(perm_i[:], a["perm"]).then_inc(ld_small, 16)
                sp.dma_start(slot0[:], a["slot0"]).then_inc(ld_small, 16)
                sp.dma_start(slot1[:, 0:BATCH], a["slot1"]).then_inc(ld_small, 16)
                sp.dma_start(chan[:], a["chan"]).then_inc(ld_small, 16)
                sp.dma_start(b0[:], a["b0"]).then_inc(ld_small, 16)
                sp.dma_start(fbias[:], a["fbias"]).then_inc(ld_small, 16)
                for t in range(KT):
                    words = a["qT"][t * 16:(t + 1) * 16, :]
                    sp.dma_start(q[:, t, :], words.unsqueeze(1).broadcast_to([16, 8, D])).then_inc(ld_q, 16)
                for table, dst in (("scT", sc), ("zrT", zr)):
                    halves = a[table].rearrange("(t h) o -> h t o", h=2)
                    for h in range(2):
                        sp.dma_start(dst[64 * h:64 * h + 64, :, :],
                                     halves[h].unsqueeze(0).broadcast_to([64, KT, D])).then_inc(ld_q, 16)
                sp.dma_start(a0_in[:], a["a0"].rearrange("p (s n) -> p s n", s=SLOTS0)).then_inc(ld_a0, 16)
                sp.dma_start(w_in[:], a["w0T"].rearrange("(t p) o -> p t o", p=P)).then_inc(ld_w, 16)
                xv = a["xT"].rearrange("(t p) n -> p t n", p=P)
                for c in range(N0):
                    sp.dma_start(xT[:, :, c * C0:(c + 1) * C0], xv[:, :, c * C0:(c + 1) * C0]).then_inc(ld_x, 16)
                sp.dma_start(b0_in[:], a["b0t"].rearrange("(t p) o -> p t o", p=P)).then_inc(ld_b0, 16)
                sp.dma_start(proj[:], a["proj"].rearrange("(t p) n -> p t n", p=P)).then_inc(ld_const, 16)
                sp.dma_start(base[:], a["base"].broadcast_to([P, NPROJ])).then_inc(ld_const, 16)
                sp.dma_start(gate[:, 0:1], a["gate"].broadcast_to([P, 1])).then_inc(ld_const, 16)
                sp.dma_start(branch[:], a["branch"]).then_inc(ld_const, 16)
                sp.wait_ge(w_lo, 1)
                sp.dma_start(a0_tab.rearrange("s p n -> p s n"),
                             a0_out[:].rearrange("p s h n -> p s (h n)")).then_inc(wr_a0, 16)
                sp.wait_ge(w_lo, 3)
                for t in range(KT):
                    for part in range(2):
                        sp.dma_start(b0_tab[8 * t:8 * t + 8, part], b0_out[:, part, t, :]).then_inc(wr_b0, 16)

                def gather_a(c):
                    for b in range(B0):
                        s = sp.value_load(slot0[0:1, bass.ds(c * B0 + b, 1)], min_val=0, max_val=SLOTS0 - 1)
                        if b == 0:
                            wait(sp, a_ps, c * 1)
                        sp.dma_start(a0g[:, b, :, :].rearrange("p h n -> p (h n)"),
                                     a0_tab[bass.ds(s, 1)].rearrange("a p n -> (a p) n")).then_inc(got_a, 16)

                def gather_b(c):
                    for b in range(B0):
                        s = sp.value_load(slot0[0:1, bass.ds(c * B0 + b, 1)], min_val=0, max_val=SLOTS0 - 1)
                        if b == 0:
                            wait(sp, h_ps, c * KT)
                        sp.dma_start(b0g[64 * (b % 2):64 * (b % 2) + 64, b // 2, :],
                                     b0_tab[bass.ds(s, 1)].rearrange("a h r n -> a (h r) n")
                                     .broadcast_to([2, 2 * RANK, D])).then_inc(got_b, 16)

                def load_pieces(c):
                    wait(sp, s_lo, c * 5)
                    sp.dma_start(s_g[:], a["wgT"][bass.ds(c * P, P), :]).then_inc(ld_g, 16)
                    sp.dma_start(s_u[:], a["wuT"][bass.ds(c * P, P), :]).then_inc(ld_u, 16)
                    sp.dma_start(s_d[:], a["wdT"][bass.ds(c * DT_PIECE * P, DT_PIECE * P), :]
                                 .rearrange("(t p) n -> p t n", p=P)).then_inc(ld_d, 16)
                    sp.dma_start(s_a[:], a["a1"][bass.ds(c * P, P), :]
                                 .rearrange("p (s n) -> p s n", n=A1W)).then_inc(ld_a1, 16)
                    sp.dma_start(s_b[:], a["b1t"][bass.ds(c * P, P), :]).then_inc(ld_b1, 16)

                def store_pieces(c):
                    sp.wait_ge(s_lo, c * 5 + 4)
                    sp.dma_start(a1_tab[bass.ds(c * 4, 4)].rearrange("s p n -> p s n"),
                                 sa_out[:].rearrange("p s h n -> p s (h n)")).then_inc(wr_a1, 16)
                    sp.wait_ge(s_lo, c * 5 + 5)
                    for part in range(2):
                        sp.dma_start(b1_tab[bass.ds(4 * c, 4), part].rearrange("s r (k n) -> s (r k) n", k=2), sb_out[:, part, :]).then_inc(wr_b1, 16)

                sp.wait_ge(ld_small, 6 * 16)
                sp.wait_ge(wr_a0, 16)
                gather_a(0)
                sp.wait_ge(wr_b0, 2 * KT * 16)
                gather_b(0)
                load_pieces(0)
                with sp.Fori(1, N0) as c:
                    store_pieces(c - 1)
                    load_pieces(c)
                    gather_a(c)
                    gather_b(c)
                store_pieces(N0 - 1)
                sp.wait_ge(wr_a1, N0 * 16)
                sp.wait_ge(wr_b1, N0 * 2 * 16)
                for s, n in ((ld_q, 8), (ld_const, 4), (got_a, BATCH), (got_b, BATCH)):
                    sp.wait_ge(s, n * 16)

            @block.gpsimd
            def _(pool):
                pool.iota(shift4[:], [[0, 1]], base=0, channel_multiplier=4).then_inc(consts, 1)
                pool.iota(col_i[:], [[1, D]], base=0, channel_multiplier=0).then_inc(consts, 1)
                pool.memset(ident32[:], 0.0).then_inc(z_ready, 1)
                pool.memset(mask0[:], LORA0).then_inc(z_ready, 1)
                pool.memset(mask1[:], LORA1).then_inc(z_ready, 1)
                pool.memset(slot1[:, BATCH:BATCH + B1], 0).then_inc(z_ready, 1)
                pool.memset(xT[:, :, TOK:TOK + C1], 0.0).then_inc(z_ready, 1)
                pool.wait_ge(z_ready, 5)
                pool.affine_select(out=ident32[:], in_=ident32[:], compare_op=ALU.not_equal, fill=1.0, base=0,
                                   pattern=[[-1, P]], channel_multiplier=1).then_inc(z_ready, 1)
                for m in (mask0, mask1):
                    pool.affine_select(out=m[:], in_=m[:], compare_op=ALU.is_ge, fill=0.0, base=0,
                                       pattern=[[-SEQ, 4], [0, RANK]], channel_multiplier=1).then_inc(z_ready, 1)
                pool.wait_ge(z_ready, 8)
                pool.tensor_copy(ident16[:], ident32[:]).then_inc(consts, 1)
                for m in (mask0, mask1):
                    pool.affine_select(out=m[:], in_=m[:], compare_op=ALU.is_ge, fill=0.0, base=SEQ - 1,
                                       pattern=[[SEQ, 4], [0, RANK]], channel_multiplier=-1).then_inc(consts, 1)

                def residual(c):
                    for o in range(KT):
                        pool.wait_ge(o_up, c * KT + o + 1)
                        xo = xT[:, o, bass.ds(c * C0, C0)]
                        pool.tensor_tensor(xo, xo, o_sb[:, o % 2, :], ALU.add).then_inc(x1, 1)

                pool.wait_ge(ld_x, N0 * 16)
                residual(0)
                with pool.Fori(1, N0) as c:
                    residual(c)

            @block.scalar
            def _(act):
                def hi(out, in_, done, scale=SCALE):
                    nc.scalar.activation(out, in_, ACT.Identity, scale=scale).then_inc(done, 1)

                act.wait_ge(ld_a0, 16)
                hi(a0_out[:, :, 0, :], a0_in[:], w_hi)
                act.wait_ge(ld_w, 16)
                hi(w0[:, 0], w_in[:], w_hi)
                act.wait_ge(ld_b0, 16)
                hi(b0_out[:, 0], b0_in[:], w_hi)
                act.wait_ge(ld_small, 6 * 16)
                hi(b0s[:, :, 0], b0[:], w_hi)
                act.wait_ge(deq, 5)
                hi(wq16[:, 0], sc[:], w_hi)

                def x_part(c):
                    wait(act, base_done, c * 1)
                    hi(xs[:, 0], xT[:, :, bass.ds(c * C0, C0)], x_hi, scale=1.0)

                def body(c):
                    x_part(c)
                    act.wait_ge(t_f, c + 1)
                    wait(act, tt_ps, c * 1)
                    for copy in range(2):
                        nc.scalar.copy(t0_s[:, :, copy, :], t0_f[:]).then_inc(t_hi, 1)
                    for k, (ready, out, in_) in enumerate((
                            (ld_g, wg[:, 0, bass.ds(c, 1), :], s_g[:].unsqueeze(1)),
                            (ld_u, wu[:, 0, bass.ds(c, 1), :], s_u[:].unsqueeze(1)),
                            (ld_d, wd[:, 0, bass.ds(c * DT_PIECE, DT_PIECE), :], s_d[:]),
                            (ld_a1, sa_out[:, :, 0, :], s_a[:]),
                            (ld_b1, sb_out[:, 0, :], s_b[:]))):
                        act.wait_ge(ready, c * 16 + 16)
                        if k == 3:
                            wait(act, wr_a1, c * 16)
                        if k == 4:
                            wait(act, wr_b1, c * 32)
                        hi(out, in_, s_hi)
                    act.wait_ge(tt_ps, c + 1)
                    wait(act, h_ps, c * KT)
                    nc.scalar.copy(t0_t[:].rearrange("p (t n) -> p t n", t=T0),
                                   p_tt[:].rearrange("p (t n) -> p t n", t=T0)[:, :, 64:64 + P]).then_inc(tt_sb, 1)
                    for o in range(KT):
                        act.wait_ge(h_ps, c * KT + o + 1)
                        if o == 0:
                            wait(act, o_ps, c * KT)
                        hi(hs[:, 0, o, :], p_h[:, o, :], h_hi, scale=INV)
                    for o in range(KT):
                        act.wait_ge(o_ps, c * KT + o + 1)
                        wait(act, x1, c * KT + o - 1)
                        nc.scalar.activation(o_sb[:, o % 2, :], p_o[:, o % 2, :], ACT.Identity,
                                             bias=cvec[:, o:o + 1], scale=INV).then_inc(o_up, 1)

                for o in range(KT):
                    act.wait_ge(m_ps, o + 1)
                    hi(mw[:, 0, o, :], p_h[:, o, :], m_hi, scale=chan[:, o:o + 1])
                act.wait_ge(ld_x, N0 * 16)
                act.wait_ge(c_done, 2)
                body(0)
                with act.Fori(1, N0) as c:
                    body(c)

            @block.vector
            def _(dve):
                def lo(out, in_, high, done, scale=SCALE):
                    nc.vector.scalar_tensor_tensor(out, in_, scale, high, ALU.mult, ALU.subtract).then_inc(done, 1)

                dve.wait_ge(consts, 2)
                dve.wait_ge(ld_small, 6 * 16)
                nc.vector.tensor_scalar(shift[:], shift4[:], 31, None, ALU.bitwise_and).then_inc(deq, 1)
                nc.vector.tensor_copy(perm_f[:], perm_i[:]).then_inc(deq, 1)
                dve.wait_ge(deq, 2)
                dve.wait_ge(w_hi, 1)
                lo(a0_out[:, :, 1, :], a0_in[:], a0_out[:, :, 0, :], w_lo)
                for t in range(KT):
                    nc.vector.tensor_scalar(onehot[:, t, :], col_i[:], perm_f[:, t:t + 1], None,
                                            ALU.is_equal).then_inc(m_lo, 1)
                dve.wait_ge(ld_q, 8 * 16)
                nc.vector.tensor_scalar(q4[:], q[:], shift[:, 0:1].bitcast(U32), 15, ALU.logical_shift_right,
                                        ALU.bitwise_and).then_inc(deq, 1)
                dve.wait_ge(deq, 3)
                nc.vector.tensor_tensor(sc[:], q4[:], sc[:], ALU.mult).then_inc(deq, 1)
                dve.wait_ge(deq, 4)
                nc.vector.tensor_tensor(sc[:], sc[:], zr[:], ALU.add).then_inc(deq, 1)
                dve.wait_ge(w_hi, 2)
                lo(w0[:, 1], w_in[:], w0[:, 0], w_lo)
                dve.wait_ge(w_hi, 3)
                lo(b0_out[:, 1], b0_in[:], b0_out[:, 0], w_lo)
                dve.wait_ge(w_hi, 4)
                lo(b0s[:, :, 1], b0[:], b0s[:, :, 0], w_lo)
                dve.wait_ge(w_hi, 5)
                dve.wait_ge(deq, 5)
                lo(wq16[:, 1], sc[:], wq16[:, 0], w_lo)
                for o in range(KT):
                    dve.wait_ge(m_hi, o + 1)
                    nc.vector.scalar_tensor_tensor(mw[:, 1, o, :], p_h[:, o, :], chan[:, o:o + 1], mw[:, 0, o, :],
                                                   ALU.mult, ALU.subtract).then_inc(m_lo, 1)
                dve.wait_ge(c_ps, 1)
                nc.vector.tensor_reduce(csum[:], p_t[:, 0:KT, 0:2], AX.X, ALU.add).then_inc(c_done, 1)
                dve.wait_ge(c_done, 1)
                nc.vector.scalar_tensor_tensor(cvec[:], csum[:], INV * INV, fbias[:], ALU.mult,
                                               ALU.add).then_inc(c_done, 1)
                dve.wait_ge(consts, 5)

                def body(c):
                    dve.wait_ge(x_hi, c + 1)
                    nc.vector.tensor_tensor(xs[:, 1], xT[:, :, bass.ds(c * C0, C0)], xs[:, 0],
                                            ALU.subtract).then_inc(x_lo, 1)
                    dve.wait_ge(a_ps, c + 1)
                    wait(dve, t_hi, 2 * c)
                    nc.vector.tensor_tensor(
                        t0_f[:].rearrange("p (t b) r -> p t b r", b=4),
                        p_t[:, 0:T0 * 4, :].rearrange("p (t b) r -> p t b r", b=4),
                        mask0[:].unsqueeze(1).broadcast_to([P, T0, 4, RANK]), ALU.mult).then_inc(t_f, 1)
                    dve.wait_ge(t_hi, 2 * c + 2)
                    dve.wait_ge(t_f, c + 1)
                    for copy in range(2):
                        nc.vector.tensor_tensor(t0_s[:, :, 2 + copy, :], t0_f[:], t0_s[:, :, 0, :],
                                                ALU.subtract).then_inc(t_lo, 1)
                    for k, (out, in_, high) in enumerate((
                            (wg[:, 1, bass.ds(c, 1), :], s_g[:].unsqueeze(1), wg[:, 0, bass.ds(c, 1), :]),
                            (wu[:, 1, bass.ds(c, 1), :], s_u[:].unsqueeze(1), wu[:, 0, bass.ds(c, 1), :]),
                            (wd[:, 1, bass.ds(c * DT_PIECE, DT_PIECE), :], s_d[:],
                             wd[:, 0, bass.ds(c * DT_PIECE, DT_PIECE), :]),
                            (sa_out[:, :, 1, :], s_a[:], sa_out[:, :, 0, :]),
                            (sb_out[:, 1, :], s_b[:], sb_out[:, 0, :]))):
                        dve.wait_ge(s_hi, c * 5 + k + 1)
                        lo(out, in_, high, s_lo)
                    for o in range(KT):
                        dve.wait_ge(h_hi, c * KT + o + 1)
                        lo(hs[:, 1, o, :], p_h[:, o, :], hs[:, 0, o, :], h_lo, scale=INV)

                body(0)
                with dve.Fori(1, N0) as c:
                    body(c)

            @block.tensor
            def _(pe):
                pe.wait_ge(w_lo, 5)
                pe.wait_ge(m_lo, KT)
                for i in range(KT):
                    for part in range(2):
                        for t in range(KT):
                            mm = nc.tensor.matmul(p_h[:, i, :], onehot[:, t, i * P:(i + 1) * P], wq16[:, part, t, :],
                                                  start=(part == 0 and t == 0), stop=(part == 1 and t == KT - 1))
                    mm.then_inc(m_ps, 1)
                pe.wait_ge(m_lo, 2 * KT)
                for o in range(KT):
                    for part in range(2):
                        for i in range(KT):
                            mm = nc.tensor.matmul(p_t[:, o, 0:2], mw[:, part, i, o * P:(o + 1) * P], b0s[:, i, :],
                                                  start=(part == 0 and i == 0), stop=(part == 1 and i == KT - 1))
                mm.then_inc(c_ps, 1)
                pe.wait_ge(consts, 5)
                pe.wait_ge(c_done, 1)

                def body(c):
                    pe.wait_ge(x_lo, c + 1)
                    pe.wait_ge(got_a, c * (B0 * 16) + B0 * 16)
                    wait(pe, t_f, c * 1)
                    for t in range(T0):
                        for n, (sx, sa) in enumerate(PASSES):
                            for i in range(KT):
                                mm = nc.tensor.matmul(p_t[:, 4 * t:4 * t + 4, :], xs[:, sx, i, t * P:(t + 1) * P],
                                                      a0g[:, 4 * t:4 * t + 4, sa, i * RANK:(i + 1) * RANK],
                                                      start=(n == 0 and i == 0), stop=(n == 2 and i == KT - 1))
                    mm.then_inc(a_ps, 1)
                    for o in range(KT):
                        wait(pe, h_lo, c * KT - KT + o + 1)
                        if o == KT - 1:
                            pe.wait_ge(t_lo, 2 * c + 2)
                            wait(pe, tt_sb, c * 1)
                        for n, (sw, sx) in enumerate(PASSES):
                            for i in range(KT):
                                mm = nc.tensor.matmul(p_h[:, o, :], w0[:, sw, i, o * P:(o + 1) * P], xs[:, sx, i, :],
                                                      start=(n == 0 and i == 0), stop=(n == 2 and i == KT - 1))
                    mm.then_inc(base_done, 1)
                    for t in range(T0):
                        for g in range(2):
                            at = (2 * t + 1 - g) * P
                            mm = nc.tensor.transpose(
                                p_tt[:, at:at + P],
                                t0_s[:, 4 * t + 2 * g:4 * t + 2 * g + 2, :, :].rearrange("p b s r -> p (b s r)"),
                                ident16[:])
                    mm.then_inc(tt_ps, 1)
                    pe.wait_ge(tt_sb, c + 1)
                    pe.wait_ge(got_b, c * (B0 * 16) + B0 * 16)
                    for o in range(KT):
                        for g in range(G0):
                            cols = slice(g * PAIR, (g + 1) * PAIR)
                            rows = slice((g ^ 1) * PAIR, ((g ^ 1) + 1) * PAIR)
                            mm = nc.tensor.matmul(p_h[:, o, cols], b0g[:, g, o * P:(o + 1) * P], t0_t[:, rows],
                                                  start=False, stop=True, skip_group_check=True)
                        mm.then_inc(h_ps, 1)
                    pe.wait_ge(h_lo, c * KT + KT)
                    for o in range(KT):
                        wait(pe, o_up, c * KT + o - 1)
                        for n, (sw, sx) in enumerate(PASSES):
                            for i in range(KT):
                                mm = nc.tensor.matmul(p_o[:, o % 2, :], mw[:, sw, i, o * P:(o + 1) * P], hs[:, sx, i, :],
                                                      start=(n == 0 and i == 0), stop=(n == 2 and i == KT - 1))
                        mm.then_inc(o_ps, 1)

                body(0)
                with pe.Fori(1, N0) as c:
                    body(c)

        l1 = maker(ctx)
        xs1 = l1("xs1", [P, 2, 2, KT, C1], F16)
        acts = l1("acts", [P, 2, FT, C1], F16)
        sil = l1("sil", [P, 3, C1], F32)
        prod = l1("prod", [P, 3, C1], F32)
        y1 = l1("y1", [P, 2, T1, D], F32)
        yT = l1("yT", [P, T1, KT, P], F32)
        xc = l1("xc", [P, KT, C1], F32)
        ag = l1("ag", [P, B1, 2, GUW], F16)
        ad = l1("ad", [P, B1, 2, FT * RANK], F16)
        bg = l1("bg", [P, G1, GU], F16)
        bd = l1("bd", [P, G1, D], F16)
        ta_f = l1("ta_f", [P, T1 * 2 * 4, RANK], F32)
        ta_s = l1("ta_s", [P, T1 * 2 * 4, 4, RANK], F16)
        ta_t = l1("ta_t", [P, 2, T1 * 2, P], F16)
        td_f = l1("td_f", [P, T1 * 4, RANK], F32)
        td_s = l1("td_s", [P, T1 * 4, 4, RANK], F16)
        td_t = l1("td_t", [P, T1 * 2, P], F16)
        out_sb = l1("out_sb", [P, T1, D], F32)
        xpre = l1("xpre", [P, T1, P], F32)
        xpreT = l1("xpreT", [P, T1, P], F32)
        yb = l1("yb", [P, T1, P], F32)
        ssq = l1("ssq", [P, 2, T1], F32)
        sq_junk = l1("sq_junk", [P, T1, D], F32)
        ms = l1("ms", [P, T1], F32)
        lnms = l1("lnms", [P, T1], F32)
        rs0 = l1("rs0", [P, T1], F32)
        rs1 = l1("rs1", [P, T1], F32)
        rstd = l1("rstd", [P, T1], F32)
        lg = l1("lg", [P, T1 * 6, 4], F32)
        mx = l1("mx", [P, T1 * 6], F32)
        ex = l1("ex", [P, T1 * 6, 4], F32)
        rsum = l1("rsum", [P, T1 * 6], F32)
        rinv = l1("rinv", [P, T1 * 6], F32)
        lnr = l1("lnr", [P, T1 * 4], F32)
        hpp = l1("hpp", [P, T1, 2, 4], F32)
        lu = l1("lu", [P, T1, 4, 4], F32)
        cmax = l1("cmax", [P, T1, 4], F32)
        hr = l1("hr", [P, T1, 4, 4], F32)
        sums = l1("sums", [P, T1, 4], F32)
        inv = l1("inv", [P, T1, 4], F32)
        hg = l1("hg", [P, T1, 16], F32)
        eye = l1("eye", [P, 16], F32)
        gsig = l1("gsig", [P, 4], F32)

        psum1 = ExitStack()
        p_gu = ps("p_gu", [P, 2, 2, C1], stack=psum1)
        p_y = ps("p_y", [P, T1, D], stack=psum1)
        p_a = ps("p_a", [P, D], stack=psum1)
        p_at = ps("p_at", [P, 2 * D], F16, stack=psum1)
        p_m1 = ps("p_m1", [P, D], stack=psum1)
        p_m2 = ps("p_m2", [P, D], stack=psum1)

        with ExitStack() as sems1:
            def sem(name):
                return sems1.enter_context(nc.semaphore(name))

            got_ag, got_ad, got_bg, got_bd = (sem(n) for n in "got_ag got_ad got_bg got_bd".split())
            x_hi, x_lo = sem("x1_hi"), sem("x1_lo")
            ta_ps, ta_up, ta_hi, ta_lo, tat_ps, tat_sb = (
                sem(n) for n in "ta_ps ta_up ta_hi ta_lo tat_ps tat_sb".split())
            td_ps, td_up, td_hi, td_lo, tdt_ps, tdt_sb = (
                sem(n) for n in "td_ps td_up td_hi td_lo tdt_ps tdt_sb".split())
            gu_ps, sil_up, prods, act_hi, act_lo = (sem(n) for n in "gu_ps sil_up prods act_hi act_lo".split())
            y_ps, y_up, yt_ps, yt_sb, lg_ps = (sem(n) for n in "y_ps y_up yt_ps yt_sb lg_ps".split())
            to_act, from_act, chain = (sem(n) for n in "to_act from_act chain".split())
            xp_up, xp_ps, xp_sb, yb_ps, yb_sb = (sem(n) for n in "xp_up xp_ps xp_sb yb_ps yb_sb".split())
            xb_ps, xc_up, mixed = (sem(n) for n in "xb_ps xc_up mixed".split())
            stored = [sem(f"stored{t}") for t in range(T1)]
            gate_e, gate_d, eye_up = (sem(n) for n in "gate_e gate_d eye_up".split())

            block = sems1.enter_context(nc.Block())

            def rows_of(f):
                return P if f < FT - 1 else FL

            @block.sync
            def _(sp):
                def gather(n, dst, table, slices, done, free, freed):
                    for b in range(B1):
                        s = sp.value_load(slot1[0:1, bass.ds(n * B1 + b, 1)], min_val=0, max_val=SLOTS1 - 1)
                        if b == 0:
                            wait(sp, free, freed)
                        sp.dma_start(dst(b), table(s, slices)).then_inc(done, 16)

                def a_rows(s, cols):
                    return (a1_tab[bass.ds(s, 1)].rearrange("a p (h n) -> (a p) h n", h=2)[:, :, cols])

                def b_rows(s, cols):
                    rows = b1_tab[bass.ds(s, 1)].rearrange("a h r n -> a (h r) n")[:, :, cols]
                    return rows.broadcast_to([2, 2 * RANK, cols.stop - cols.start])

                def pair_rows(dst):
                    return lambda b: dst[64 * (b % 2):64 * (b % 2) + 64, b // 2, :]

                def gather_ag(n):
                    gather(n, lambda b: ag[:, b, :, :], a_rows, slice(0, GUW), got_ag, ta_ps, n)

                def gather_ad(n):
                    gather(n, lambda b: ad[:, b, :, :], a_rows, slice(GUW, A1W), got_ad, td_ps, n)

                def gather_bg(n):
                    gather(n, pair_rows(bg), b_rows, slice(0, GU), got_bg, gu_ps, n * FT)

                def gather_bd(n):
                    gather(n, pair_rows(bd), b_rows, slice(GU, B1W), got_bd, y_ps, n * T1)

                def store(n):
                    for t in range(T1):
                        sp.wait_ge(mixed, n * T1 + t + 1)
                        sp.dma_start(out[bass.ds(n * C1 + t * P, P), :], out_sb[:, t, :]).then_inc(stored[t], 16)

                def step(n, first=False, last=False):
                    gather_ag(n + 1)
                    gather_ad(n)
                    gather_bd(n)
                    if not last:
                        gather_bg(n + 1)
                    if not first:
                        store(n - 1)

                gather_ag(0)
                gather_bg(0)
                step(0, first=True)
                step(1)
                with sp.Fori(1, N1 // 2 - 1) as s:
                    step(2 * s)
                    step(2 * s + 1)
                step(N1 - 2)
                step(N1 - 1, last=True)
                store(N1 - 1)
                sp.wait_ge(got_ag, (N1 + 1) * B1 * 16)
                for t in range(T1):
                    sp.wait_ge(stored[t], N1 * 16)

            @block.gpsimd
            def _(pool):
                pool.memset(eye[:], 0.0).then_inc(eye_up, 1)
                pool.wait_ge(eye_up, 1)
                pool.affine_select(out=eye[:].rearrange("p (i j) -> p i j", j=4),
                                   in_=eye[:].rearrange("p (i j) -> p i j", j=4), compare_op=ALU.not_equal,
                                   fill=1.0, base=0, pattern=[[1, 4], [-1, 4]],
                                   channel_multiplier=0).then_inc(eye_up, 1)

                def x_low(n, par):
                    pool.wait_ge(x_hi, n + 1)
                    pool.tensor_tensor(xs1[:, par, 1], xT[:, :, bass.ds(n * C1, C1)], xs1[:, par, 0],
                                       ALU.subtract).then_inc(x_lo, 1)

                def step(n, par, first=False):
                    for f in range(FT):
                        m = rows_of(f)
                        if f == FT - 1 and not first:
                            pool.wait_ge(xb_ps, n * T1)
                        pool.wait_ge(act_hi, n * FT + f + 1)
                        pool.tensor_tensor(acts[0:m, 1, f, :], prod[0:m, f % 3, :], acts[0:m, 0, f, :],
                                           ALU.subtract).then_inc(act_lo, 1)
                        if f == 5:
                            x_low(n + 1, 1 - par)
                    pool.tensor_copy(xc[:], xT[:, :, bass.ds(n * C1, C1)]).then_inc(xc_up, 1)

                x_low(0, 0)
                step(0, 0, first=True)
                step(1, 1)
                with pool.Fori(1, N1 // 2) as s:
                    step(2 * s, 0)
                    step(2 * s + 1, 1)

            @block.scalar
            def _(act):
                def split_x(n, par):
                    nc.scalar.copy(xs1[:, par, 0], xT[:, :, bass.ds(n * C1, C1)]).then_inc(x_hi, 1)

                def a_high(n):
                    act.wait_ge(ta_up, n + 1)
                    for copy in range(2):
                        if copy == 0:
                            wait(act, tat_ps, n)
                        nc.scalar.copy(ta_s[:, :, copy, :], ta_f[:]).then_inc(ta_hi, 1)

                def a_rows(n, par):
                    act.wait_ge(tat_ps, n + 1)
                    nc.scalar.copy(ta_t[:, par], p_at[:].rearrange("p (u n) -> p u n", u=2 * T1)
                                   [:, :, 64:64 + P]).then_inc(tat_sb, 1)

                def high(n, f):
                    m = rows_of(f)
                    act.wait_ge(prods, n * FT + f + 1)
                    if f == 0:
                        wait(act, y_ps, n * T1)
                    nc.scalar.copy(acts[0:m, 0, f, :], prod[0:m, f % 3, :]).then_inc(act_hi, 1)

                def y_transposed(n):
                    act.wait_ge(yt_ps, n + 1)
                    wait(act, lg_ps, n)
                    for t, p in enumerate((p_m1, p_a)):
                        nc.scalar.copy(yT[:, t].rearrange("p k n -> p (k n)"), p[:]).then_inc(yt_sb, 1)

                def root(n):
                    act.wait_ge(to_act, 4 * n + 1)
                    nc.scalar.activation(lnms[:], ms[:], ACT.Ln).then_inc(from_act, 1)
                    act.wait_ge(from_act, 5 * n + 1)
                    nc.scalar.activation(rs0[:], lnms[:], ACT.Exp, scale=-0.5).then_inc(from_act, 1)

                def exps(n):
                    act.wait_ge(to_act, 4 * n + 2)
                    v = ex[:].rearrange("p (t k) j -> p t (k j)", t=T1)
                    w = lg[:].rearrange("p (t k) j -> p t (k j)", t=T1)
                    nc.scalar.activation(v[:, :, 0:16], w[:, :, 0:16], ACT.Exp, scale=10.0)
                    nc.scalar.activation(v[:, :, 16:24], w[:, :, 16:24], ACT.Exp).then_inc(from_act, 1)
                    act.wait_ge(to_act, 4 * n + 3)
                    nc.scalar.activation(lnr[:].rearrange("p (t k) -> p t k", t=T1),
                                         rsum[:].rearrange("p (t k) -> p t k", t=T1)[:, :, 0:4],
                                         ACT.Ln).then_inc(from_act, 1)
                    act.wait_ge(to_act, 4 * n + 4)
                    nc.scalar.activation(ex[:].rearrange("p (t k) j -> p t (k j)", t=T1)[:, :, 0:16],
                                         lu[:].rearrange("p t i j -> p t (i j)"), ACT.Exp).then_inc(from_act, 1)

                def x_pre_out(n):
                    act.wait_ge(xp_ps, n + 1)
                    wait(act, yb_ps, n)
                    nc.scalar.copy(xpreT[:].rearrange("p t c -> p (t c)"), p_m2[:, 0:C1]).then_inc(xp_sb, 1)

                def y_out(n):
                    act.wait_ge(yb_ps, n + 1)
                    wait(act, mixed, n * T1)
                    nc.scalar.copy(yb[:].rearrange("p t c -> p (t c)"), p_m2[:, C1:2 * C1]).then_inc(yb_sb, 1)

                def step(n, par, first=False):
                    for f in range(FT):
                        m = rows_of(f)
                        act.wait_ge(gu_ps, n * FT + f + 1)
                        wait(act, prods, n * FT + f - 2)
                        nc.scalar.activation(sil[0:m, f % 3, :], p_gu[0:m, (par * FT + f) % 2, 0, :], ACT.Silu,
                                             scale=INV).then_inc(sil_up, 1)
                        if f:
                            high(n, f - 1)
                        if not first:
                            if f == 0:
                                root(n - 1)
                                y_transposed(n - 1)
                            if f == 1:
                                exps(n - 1)
                            if f == 5:
                                x_pre_out(n - 1)
                            if f == 7:
                                y_out(n - 1)
                        if f == 4:
                            split_x(n + 1, 1 - par)
                        if f == 9:
                            a_high(n + 1)
                    high(n, FT - 1)
                    a_rows(n + 1, 1 - par)
                    act.wait_ge(td_up, n + 1)
                    for copy in range(2):
                        if copy == 0:
                            wait(act, tdt_ps, n)
                        nc.scalar.copy(td_s[:, :, copy, :], td_f[:]).then_inc(td_hi, 1)
                    act.wait_ge(tdt_ps, n + 1)
                    nc.scalar.copy(td_t[:].rearrange("p u n -> p (u n)"), p_at[:, 0:D]).then_inc(tdt_sb, 1)
                    for t in range(T1):
                        act.wait_ge(y_ps, n * T1 + t + 1)
                        if t == 0:
                            wait(act, y_up, 2 * T1 * n)
                        wait(act, mixed, (n - 1) * T1)
                        nc.scalar.activation(y1[:, par, t, :], p_y[:, t, :], ACT.Identity, scale=INV).then_inc(y_up, 1)
                        nc.scalar.activation(sq_junk[:, t, :], p_y[:, t, :], ACT.Square, scale=INV,
                                             accum_out=ssq[:, par, t:t + 1]).then_inc(y_up, 1)

                nc.scalar.activation(gsig[:, 0:1], gate[:, 0:1], ACT.Exp, scale=-1.0).then_inc(gate_e, 1)
                split_x(0, 0)
                a_high(0)
                a_rows(0, 0)
                step(0, 0, first=True)
                step(1, 1)
                with act.Fori(1, N1 // 2) as s:
                    step(2 * s, 0)
                    step(2 * s + 1, 1)
                root(N1 - 1)
                y_transposed(N1 - 1)
                exps(N1 - 1)
                x_pre_out(N1 - 1)
                y_out(N1 - 1)

            @block.vector
            def _(dve):
                count = [0]

                def link(ins):
                    count[0] += 1
                    ins.then_inc(chain, 1)
                    dve.wait_ge(chain, count[0])

                def restart():
                    dve.sem_clear(chain)
                    count[0] = 0

                def take_a(n):
                    dve.wait_ge(ta_ps, n + 1)
                    wait(dve, ta_hi, 2 * n)
                    nc.vector.tensor_tensor(
                        ta_f[:].rearrange("p (u b) r -> p u (b r)", b=4),
                        p_a[:, 0:C1].rearrange("p (u m) -> p u m", u=2 * T1),
                        mask1[:].rearrange("p b r -> p (b r)").unsqueeze(1).broadcast_to([P, 2 * T1, 4 * RANK]),
                        ALU.mult).then_inc(ta_up, 1)

                def low_a(n):
                    dve.wait_ge(ta_hi, 2 * n + 2)
                    for copy in range(2):
                        nc.vector.tensor_tensor(ta_s[:, :, 2 + copy, :], ta_f[:], ta_s[:, :, 0, :],
                                                ALU.subtract).then_inc(ta_lo, 1)

                def logits(m, par):
                    link(nc.vector.tensor_scalar(rs1[:], rs0[:], 1.0, None, ALU.mult))
                    link(nc.vector.tensor_tensor(rs1[:], rs0[:], rs0[:], ALU.mult))
                    link(nc.vector.tensor_tensor(rs1[:], rs1[:], ms[:], ALU.mult))
                    link(nc.vector.tensor_scalar(rs1[:], rs1[:], -0.5, 1.5, ALU.mult, ALU.add))
                    link(nc.vector.tensor_tensor(rstd[:], rs0[:], rs1[:], ALU.mult))
                    dve.wait_ge(lg_ps, m + 1)
                    for t in range(T1):
                        last = nc.vector.scalar_tensor_tensor(
                            lg[:].rearrange("p (t k) j -> p t (k j)", t=T1)[:, t, :],
                            p_m2[:, t * NPROJ:(t + 1) * NPROJ], rstd[:, t:t + 1], base[:], ALU.mult, ALU.add)
                    link(last)
                    link(nc.vector.tensor_reduce(mx[:], lg[:], AX.X, ALU.max))
                    nc.vector.tensor_tensor(lg[:], lg[:], mx[:].unsqueeze(2).broadcast_to([P, T1 * 6, 4]),
                                            ALU.subtract).then_inc(to_act, 1)
                    dve.wait_ge(from_act, 5 * m + 3)
                    nc.vector.tensor_reduce(rsum[:], ex[:], AX.X, ALU.add).then_inc(to_act, 1)
                    dve.wait_ge(to_act, 4 * m + 3)
                    link(nc.vector.reciprocal(rinv[:], rsum[:]))
                    link(nc.vector.tensor_tensor(
                        hpp[:], ex[:].rearrange("p (t k) j -> p t k j", t=T1)[:, :, 4:6, :],
                        rinv[:].rearrange("p (t k) -> p t k", t=T1)[:, :, 4:6].unsqueeze(3)
                        .broadcast_to([P, T1, 2, 4]), ALU.mult))
                    dve.wait_ge(from_act, 5 * m + 4)
                    for t in range(T1):
                        last = nc.vector.scalar_tensor_tensor(
                            lu[:, t], lg[:, 6 * t:6 * t + 4, :], 10.0,
                            lnr[:, 4 * t:4 * t + 4].unsqueeze(2).broadcast_to([P, 4, 4]), ALU.mult, ALU.subtract)
                    link(last)
                    link(nc.vector.tensor_reduce(cmax[:], lu[:].rearrange("p t i j -> p t j i"), AX.X, ALU.max))
                    nc.vector.tensor_tensor(lu[:], lu[:], cmax[:].unsqueeze(2).broadcast_to([P, T1, 4, 4]),
                                            ALU.subtract).then_inc(to_act, 1)
                    dve.wait_ge(from_act, 5 * m + 5)
                    e2 = ex[:].rearrange("p (t k) j -> p t k j", t=T1)[:, :, 0:4, :]
                    link(nc.vector.tensor_reduce(sums[:], e2.rearrange("p t i j -> p t j i"), AX.X, ALU.add))
                    link(nc.vector.reciprocal(inv[:], sums[:]))
                    link(nc.vector.tensor_tensor(hr[:], e2, inv[:].unsqueeze(2).broadcast_to([P, T1, 4, 4]),
                                                 ALU.mult))

                def mean_square(m, par):
                    dve.wait_ge(y_up, 2 * T1 * (m + 1))
                    nc.vector.tensor_scalar(ms[:], ssq[:, par, :], 1.0 / D, RMS_EPS, ALU.mult,
                                            ALU.add).then_inc(to_act, 1)
                    dve.wait_ge(from_act, 5 * m + 2)

                def rounds(k):
                    for _ in range(k):
                        link(nc.vector.tensor_reduce(sums[:], hr[:], AX.X, ALU.add))
                        link(nc.vector.reciprocal(inv[:], sums[:]))
                        link(nc.vector.tensor_tensor(hr[:], hr[:], inv[:].unsqueeze(3).broadcast_to([P, T1, 4, 4]),
                                                     ALU.mult))
                        link(nc.vector.tensor_reduce(sums[:], hr[:].rearrange("p t i j -> p t j i"), AX.X, ALU.add))
                        link(nc.vector.reciprocal(inv[:], sums[:]))
                        link(nc.vector.tensor_tensor(hr[:], hr[:], inv[:].unsqueeze(2).broadcast_to([P, T1, 4, 4]),
                                                     ALU.mult))

                def x_pre(m, par):
                    wait(dve, xp_ps, m)
                    for k in range(4):
                        for t in range(T1):
                            s_k = y1[:, par, t, k * P:(k + 1) * P]
                            if k == 0:
                                last = nc.vector.tensor_scalar(xpre[:, t, :], s_k, hpp[:, t, 0, 0:1], None, ALU.mult)
                            else:
                                last = nc.vector.scalar_tensor_tensor(xpre[:, t, :], s_k, hpp[:, t, 0, k:k + 1],
                                                                      xpre[:, t, :], ALU.mult, ALU.add)
                        if k < 3:
                            link(last)
                    last.then_inc(xp_up, 1)

                def mix(m, par):
                    link(nc.vector.scalar_tensor_tensor(hg[:], hr[:].rearrange("p t i j -> p t (i j)"), gsig[:, 2:3],
                                                        eye[:].unsqueeze(1).broadcast_to([P, T1, 16]),
                                                        ALU.mult, ALU.add))
                    dve.wait_ge(yb_sb, m + 1)
                    dve.wait_ge(xb_ps, m * T1 + T1)
                    for t, back in enumerate((p_m1, p_m2)):
                        wait(dve, stored[t], m * 16)
                        for k in range(5):
                            for i in range(4):
                                o = out_sb[:, t, i * P:(i + 1) * P]
                                src = yb[:, t, :] if k == 4 else y1[:, par, t, k * P:(k + 1) * P]
                                by = hpp[:, t, 1, i:i + 1] if k == 4 else hg[:, t, 4 * i + k:4 * i + k + 1]
                                last = nc.vector.scalar_tensor_tensor(
                                    o, src, by, back[:, i * P:(i + 1) * P] if k == 0 else o, ALU.mult, ALU.add)
                            if k < 4:
                                link(last)
                        last.then_inc(mixed, 1)

                def step(n, par, first=False):
                    restart()
                    for f in range(FT):
                        m = rows_of(f)
                        dve.wait_ge(sil_up, n * FT + f + 1)
                        wait(dve, act_lo, n * FT + f - 2)
                        nc.vector.scalar_tensor_tensor(prod[0:m, f % 3, :], p_gu[0:m, (par * FT + f) % 2, 1, :], INV,
                                                       sil[0:m, f % 3, :], ALU.mult, ALU.mult).then_inc(prods, 1)
                        if not first:
                            if f == 0:
                                mean_square(n - 1, 1 - par)
                            elif f == 1:
                                logits(n - 1, 1 - par)
                            elif f == 3:
                                x_pre(n - 1, 1 - par)
                            else:
                                rounds(4)
                        if f == 8:
                            take_a(n + 1)
                        if f == 9:
                            low_a(n + 1)
                    dve.wait_ge(td_ps, n + 1)
                    wait(dve, td_hi, 2 * n)
                    nc.vector.tensor_tensor(
                        td_f[:].rearrange("p (u b) r -> p u (b r)", b=4),
                        p_a[:, 0:P].rearrange("p (u m) -> p u m", u=T1),
                        mask1[:].rearrange("p b r -> p (b r)").unsqueeze(1).broadcast_to([P, T1, 4 * RANK]),
                        ALU.mult).then_inc(td_up, 1)
                    dve.wait_ge(td_hi, 2 * n + 2)
                    for copy in range(2):
                        nc.vector.tensor_tensor(td_s[:, :, 2 + copy, :], td_f[:], td_s[:, :, 0, :],
                                                ALU.subtract).then_inc(td_lo, 1)
                    if not first:
                        rounds(ROUNDS - 1 - 4 * 8)
                        mix(n - 1, 1 - par)

                restart()
                dve.wait_ge(gate_e, 1)
                dve.wait_ge(eye_up, 2)
                link(nc.vector.tensor_scalar(gsig[:, 1:2], gsig[:, 0:1], 1.0, None, ALU.add))
                link(nc.vector.reciprocal(gsig[:, 2:3], gsig[:, 1:2]))
                link(nc.vector.tensor_scalar(gsig[:, 3:4], gsig[:, 2:3], -1.0, 1.0, ALU.mult, ALU.add))
                link(nc.vector.tensor_scalar(eye[:], eye[:], gsig[:, 3:4], None, ALU.mult))
                take_a(0)
                low_a(0)
                step(0, 0, first=True)
                step(1, 1)
                with dve.Fori(1, N1 // 2) as s:
                    step(2 * s, 0)
                    step(2 * s + 1, 1)
                restart()
                mean_square(N1 - 1, 1)
                logits(N1 - 1, 1)
                x_pre(N1 - 1, 1)
                rounds(ROUNDS - 1)
                mix(N1 - 1, 1)

            @block.tensor
            def _(pe):
                def x_a(n, par):
                    pe.wait_ge(x_lo, n + 1)
                    pe.wait_ge(got_ag, (n + 1) * (B1 * 16))
                    wait(pe, td_up, n - 1)
                    for t in range(T1):
                        for k, (sx, sa) in enumerate(PASSES):
                            for i in range(KT):
                                mm = nc.tensor.matmul(
                                    p_a[:, t * P:(t + 1) * P], xs1[:, par, sx, i, t * P:(t + 1) * P],
                                    ag[:, 4 * t:4 * t + 4, sa, i * 2 * RANK:(i + 1) * 2 * RANK]
                                    .rearrange("p b (a r) -> p a b r", a=2),
                                    start=(k == 0 and i == 0), stop=(k == 2 and i == KT - 1))
                    mm.then_inc(ta_ps, 1)

                def a_rows(n):
                    pe.wait_ge(ta_lo, 2 * n + 2)
                    wait(pe, tdt_sb, n - 1)
                    for u in range(2 * T1):
                        for g in range(2):
                            at = (2 * u + 1 - g) * P
                            mm = nc.tensor.transpose(
                                p_at[:, at:at + P],
                                ta_s[:, 4 * u + 2 * g:4 * u + 2 * g + 2, :, :].rearrange("p b s r -> p (b s r)"),
                                ident16[:])
                    mm.then_inc(tat_ps, 1)

                def gate_up(n, par, f):
                    m = rows_of(f)
                    bank = (par * FT + f) % 2
                    wait(pe, prods, n * FT + f - 1)
                    for tab, w in enumerate((wg, wu)):
                        for k, (sw, sx) in enumerate(PASSES):
                            for i in range(KT):
                                nc.tensor.matmul(p_gu[0:m, bank, tab, :], w[:, sw, i, f * P:f * P + m],
                                                 xs1[:, par, sx, i, :], start=(k == 0 and i == 0),
                                                 stop=(k == 2 and i == KT - 1))
                        for t in range(T1):
                            for g in range(2):
                                at = t * P + g * PAIR
                                mm = nc.tensor.matmul(
                                    p_gu[0:m, bank, tab, at:at + PAIR],
                                    bg[:, 2 * t + g, tab * F + f * P:tab * F + f * P + m],
                                    ta_t[:, par, 2 * t + tab, (1 - g) * PAIR:(2 - g) * PAIR],
                                    start=False, stop=True, skip_group_check=True)
                    mm.then_inc(gu_ps, 1)

                def y_transposes(m, par):
                    pe.wait_ge(y_up, 2 * T1 * (m + 1))
                    wait(pe, mixed, m * T1)
                    for t, p in enumerate((p_m1, p_a)):
                        for i in range(KT):
                            mm = nc.tensor.transpose(p[:, i * P:(i + 1) * P], y1[:, par, t, i * P:(i + 1) * P],
                                                     ident32[:])
                    mm.then_inc(yt_ps, 1)

                def project(m):
                    pe.wait_ge(yt_sb, 2 * m + 2)
                    for t in range(T1):
                        for i in range(KT):
                            mm = nc.tensor.matmul(p_m2[:, t * NPROJ:(t + 1) * NPROJ], yT[:, t, i, :], proj[:, i, :],
                                                  start=(i == 0), stop=(i == KT - 1))
                    mm.then_inc(lg_ps, 1)

                def pre_transposes(m):
                    pe.wait_ge(xp_up, m + 1)
                    for t in range(T1):
                        mm = nc.tensor.transpose(p_m2[:, t * P:(t + 1) * P], xpre[:, t, :], ident32[:])
                    mm.then_inc(xp_ps, 1)

                def branch_product(m):
                    pe.wait_ge(xp_sb, m + 1)
                    for t in range(T1):
                        mm = nc.tensor.matmul(p_m2[:, C1 + t * P:C1 + (t + 1) * P], xpreT[:, t, :], branch[:],
                                              start=True, stop=True)
                    mm.then_inc(yb_ps, 1)

                def x_back(m, t):
                    if t == 0:
                        pe.wait_ge(xc_up, m + 1)
                    else:
                        pe.wait_ge(yb_sb, m + 1)
                    for i in range(KT):
                        mm = nc.tensor.transpose((p_m1, p_m2)[t][:, i * P:(i + 1) * P],
                                                 xc[:, i, t * P:(t + 1) * P], ident32[:])
                    mm.then_inc(xb_ps, 1)

                def down(n, par):
                    pe.wait_ge(got_ad, (n + 1) * (B1 * 16))
                    pe.wait_ge(ta_up, n + 2)
                    for t in range(T1):
                        for i in range(FT):
                            m = rows_of(i)
                            if t == 0:
                                pe.wait_ge(act_lo, n * FT + i + 1)
                            for k, (sx, sa) in enumerate(PASSES):
                                mm = nc.tensor.matmul(
                                    p_a[:, t * 64:(t + 1) * 64], acts[0:m, sx, i, t * P:(t + 1) * P],
                                    ad[0:m, 4 * t:4 * t + 4, sa, i * RANK:(i + 1) * RANK],
                                    start=(i == 0 and k == 0), stop=(i == FT - 1 and k == 2))
                    mm.then_inc(td_ps, 1)
                    for t in range(T1):
                        if t == 0:
                            wait(pe, y_up, 2 * T1 * n)
                        for i in range(FT):
                            m = rows_of(i)
                            if t == 1 and i == 5:
                                pe.wait_ge(td_lo, 2 * n + 2)
                                pe.wait_ge(tat_sb, n + 2)
                                for u in range(2 * T1):
                                    mm = nc.tensor.transpose(
                                        p_at[:, u * P:(u + 1) * P],
                                        td_s[:, 2 * u:2 * u + 2, :, :].rearrange("p b s r -> p (b s r)"), ident16[:])
                                mm.then_inc(tdt_ps, 1)
                            for k, (sx, sw) in enumerate(PASSES):
                                nc.tensor.matmul(p_y[:, t, :], acts[0:m, sx, i, t * P:(t + 1) * P],
                                                 wd[0:m, sw, i, :], start=(i == 0 and k == 0), stop=False)
                    pe.wait_ge(tdt_sb, n + 1)
                    pe.wait_ge(got_bd, (n + 1) * (B1 * 16))
                    for t in range(T1):
                        for g in range(2):
                            mm = nc.tensor.matmul(p_y[:, t, :], td_t[:, 2 * t + g, :], bd[:, 2 * t + g, :],
                                                  start=False, stop=(g == 1))
                        mm.then_inc(y_ps, 1)

                def step(n, par, first=False):
                    pe.wait_ge(tat_sb, n + 1)
                    pe.wait_ge(got_bg, (n + 1) * (B1 * 16))
                    for f in range(FT):
                        gate_up(n, par, f)
                        if f == 7:
                            x_a(n + 1, 1 - par)
                        if f == 9:
                            a_rows(n + 1)
                        if not first:
                            if f == 0:
                                y_transposes(n - 1, 1 - par)
                            if f == 1:
                                project(n - 1)
                            if f == 4:
                                pre_transposes(n - 1)
                            if f == 5:
                                branch_product(n - 1)
                            if f == 7:
                                x_back(n - 1, 0)
                            if f == 8:
                                x_back(n - 1, 1)
                    down(n, par)

                x_a(0, 0)
                a_rows(0)
                step(0, 0, first=True)
                step(1, 1)
                with pe.Fori(1, N1 // 2) as s:
                    step(2 * s, 0)
                    step(2 * s + 1, 1)
                y_transposes(N1 - 1, 1)
                project(N1 - 1)
                pre_transposes(N1 - 1)
                branch_product(N1 - 1)
                x_back(N1 - 1, 0)
                x_back(N1 - 1, 1)


def kernel(**inputs):
    import numpy as np
    import concourse.bacc as bacc
    from concourse.bass_utils import run_bass_kernel_spmd as run

    def get(name):
        return np.asarray(inputs[name])

    def columns(v):
        return v.reshape(KT, P).T

    def slots_a(t, slots, tiles):
        return t.reshape(slots, tiles, P, -1).transpose(2, 0, 1, 3)

    a_gu = np.stack([get("L1_cond_A_gate")[0], get("L1_cond_A_up")[0]], 1)
    a_gu = slots_a(a_gu.transpose(0, 3, 1, 2), SLOTS1, KT).reshape(P, SLOTS1, -1)
    a_d = np.zeros((SLOTS1, FT * P, RANK), np.float32)
    a_d[:, :F] = get("L1_cond_A_down")[0].transpose(0, 2, 1)
    a_d = slots_a(a_d, SLOTS1, FT).reshape(P, SLOTS1, -1)
    a1 = np.concatenate([a_gu, a_d], 2)
    wd = np.zeros((PIECES * DT_PIECE * P, D), np.float32)
    wd[:F] = get("L1_cond_W_down").T
    rows = [get(n)[0].transpose(0, 2, 1) for n in ("L1_cond_B_gate", "L1_cond_B_up", "L1_cond_B_down")]
    x = get("x").reshape(TOK, D)
    arrays = {
        "xT": x.T,
        "slot0": get("itok_B_0_23").reshape(1, BATCH),
        "slot1": get("itok_B_2_6").reshape(1, BATCH),
        "w0T": get("L0_cond_W").T,
        "b0": columns(get("L0_cond_b")),
        "a0": slots_a(get("L0_cond_lora_As"), SLOTS0, KT).reshape(P, -1),
        "b0t": get("L0_cond_lora_Bs").reshape(SLOTS0 * RANK, D),
        "chan": columns(get("L0_ffn_channel_scale").reshape(D)),
        "qT": get("L0_ffn_qweight").T,
        "perm": columns(get("L0_ffn_q_perm")),
        "scT": get("L0_ffn_scales").T,
        "zrT": get("L0_ffn_zeros").T,
        "fbias": columns(get("L0_ffn_bias")),
        "wgT": get("L1_cond_W_gate").T,
        "wuT": get("L1_cond_W_up").T,
        "wdT": wd,
        "a1": a1.reshape(P, PIECES, -1).transpose(1, 0, 2).reshape(PIECES * P, -1),
        "b1t": np.concatenate(rows, 2).reshape(2 * SLOTS1 * RANK, B1W // 2),
        "proj": np.concatenate([get("L1_ffn_W_res"), get("L1_ffn_W_pre"), get("L1_ffn_W_post")], 0).T,
        "base": np.concatenate([get("L1_ffn_H_res_base").reshape(-1), get("L1_ffn_H_pre_base"),
                                get("L1_ffn_H_post_base")]).reshape(1, NPROJ),
        "gate": get("L1_ffn_gate").reshape(1, 1),
        "branch": get("L1_ffn_W_branch"),
    }
    nc = bacc.Bacc("TRN2", target_bir_lowering=False, num_devices=1)
    arrays = {"in_" + n: np.ascontiguousarray(v) for n, v in arrays.items()}
    aps = {n[3:]: nc.dram_tensor(n, v.shape, mybir.dt.from_np(v.dtype), kind="ExternalInput").ap()
           for n, v in arrays.items()}
    out = nc.dram_tensor("out", (TOK, D), F32, kind="ExternalOutput").ap()
    build(nc, aps, out)
    r = run(nc, [arrays], core_ids=[0])
    return r.results[0]["out"].reshape(BATCH, SEQ, D)
```

```python
from contextlib import ExitStack

import concourse.bass as bass
from concourse import mybir

F32 = mybir.dt.float32
F16 = mybir.dt.float16
I32 = mybir.dt.int32
U32 = mybir.dt.uint32
ALU = mybir.AluOpType
ACT = mybir.ActivationFunctionType
AX = mybir.AxisListType

P = 128
BATCH, SEQ, D = 64, 32, 512
TOK = BATCH * SEQ
KT = D // P
RANK = 16
SLOTS0, SLOTS1 = 32, 16
F = 1376
FT = -(-F // P)
FL = F - (FT - 1) * P
NGROUP = 8
C0 = 512
N0 = TOK // C0
T0 = C0 // P
B0 = C0 // SEQ
G0 = B0 // 2
C1 = 256
N1 = TOK // C1
T1 = C1 // P
B1 = C1 // SEQ
G1 = B1 // 2
PAIR = 2 * SEQ
PIECES = 4
DT_PIECE = 3
A1W = KT * 2 * RANK + FT * RANK
GUW = KT * 2 * RANK
B1W = 2 * F + D
GU = 2 * F
NPROJ = 24
ROUNDS = 50
NT = TOK // P
GROUPS = ((0, 6), (6, 12), (12, 16))
CHAIN_STEPS = ((3, 4, 5), (6, 7))
CHAIN_F = (2, 0, 2, 1, 2, 2, 2, 1, 2, 1, 2)
CHAIN_DOWN = 17
TAIL_BOTH = 6
RMS_EPS = 1.1920929e-07

SCALE = 256.0
INV = 1.0 / SCALE
LORA0 = 2.0 * INV
LORA1 = 0.5 * INV
PASSES = ((0, 0), (1, 0), (0, 1))


def wait(eng, sem, value):
    if not isinstance(value, int) or value > 0:
        eng.wait_ge(sem, value)


def build(nc, a, out):
    ctx = ExitStack()
    with ctx:
        def maker(stack):
            return lambda name, shape, dt: stack.enter_context(nc.sbuf_tensor(name, shape, dt))

        sb = maker(ctx)

        xT = sb("xT", [P, KT, TOK + C1], F32)
        ident32 = sb("ident32", [P, P], F32)
        ident16 = sb("ident16", [P, P], F16)
        mask0 = sb("mask0", [P, 4, RANK], F32)
        mask1 = sb("mask1", [P, 4, RANK], F32)
        slot0 = sb("slot0", [1, BATCH], I32)
        slot1 = sb("slot1", [1, BATCH + B1], I32)
        proj = sb("proj", [P, KT, NPROJ], F32)
        base = sb("base", [P, NPROJ], F32)
        gate = sb("gate", [P, 2], F32)
        branch = sb("branch", [P, P], F32)
        chan = sb("chan", [P, KT], F32)
        b0 = sb("b0", [P, KT], F32)
        b0s = sb("b0s", [P, KT, 2], F16)
        fbias = sb("fbias", [P, KT], F32)
        csum = sb("csum", [P, KT], F32)
        cvec = sb("cvec", [P, KT], F32)
        perm_i = sb("perm_i", [P, KT], I32)
        perm_f = sb("perm_f", [P, KT], F32)
        shift = sb("shift", [P, 1], I32)
        shift4 = sb("shift4", [P, 1], I32)

        setup = ExitStack()
        st = maker(setup)
        q = st("q", [P, KT, D], U32)
        q4 = st("q4", [P, KT, D], U32)
        sc = st("sc", [P, KT, D], F32)
        zr = st("zr", [P, KT, D], F32)
        w_in = st("w_in", [P, KT, D], F32)
        a0_in = st("a0_in", [P, SLOTS0, KT * RANK], F32)
        a0_out = st("a0_out", [P, SLOTS0, 2, KT * RANK], F16)
        b0_in = st("b0_in", [P, KT, D], F32)
        b0_out = st("b0_out", [P, 2, KT, D], F16)
        onehot = st("onehot", [P, KT, D], F16)
        col_i = st("col_i", [P, D], I32)
        setup.close()

        wg = sb("wg", [P, 2, KT, F], F16)
        wu = sb("wu", [P, 2, KT, F], F16)
        wd = sb("wd", [P, 2, PIECES * DT_PIECE, D], F16)

        layer0 = ExitStack()
        l0 = maker(layer0)
        sb_out = l0("sb_out", [P, 2, B1W // 2], F16)
        sa_out = l0("sa_out", [P, SLOTS1 // 4, 2, A1W], F16)
        s_g = l0("s_g", [P, F], F32)
        w0 = l0("w0", [P, 2, KT, D], F16)
        mw = l0("mw", [P, 2, KT, D], F16)
        xs = l0("xs", [P, 2, KT, C0], F16)
        hs = l0("hs", [P, 2, KT, C0], F16)
        o_sb = l0("o_sb", [P, 2, C0], F32)
        a0g = l0("a0g", [P, B0, 2, KT * RANK], F16)
        b0g = l0("b0g", [P, G0, D], F16)
        t0_f = l0("t0_f", [P, T0 * 4, RANK], F32)
        t0_s = l0("t0_s", [P, T0 * 4, 4, RANK], F16)
        t0_t = l0("t0_t", [P, C0], F16)
        wq16 = l0("wq16", [P, 2, KT, D], F16)
        s_u = l0("s_u", [P, F], F32)
        s_d = l0("s_d", [P, DT_PIECE, D], F32)
        s_a = l0("s_a", [P, SLOTS1 // 4, A1W], F32)
        s_b = l0("s_b", [P, B1W // 2], F32)
        layer0.close()

        a0_tab = nc.dram_tensor("a0_tab", [SLOTS0, P, 2 * KT * RANK], F16, kind="Internal")
        b0_tab = nc.dram_tensor("b0_tab", [SLOTS0, 2, RANK, D], F16, kind="Internal")
        a1_tab = nc.dram_tensor("a1_tab", [SLOTS1, P, 2 * A1W], F16, kind="Internal")
        b1_tab = nc.dram_tensor("b1_tab", [SLOTS1, 2, RANK, B1W], F16, kind="Internal")

        psum0 = ExitStack()

        def ps(name, shape, dt=F32, stack=psum0):
            return stack.enter_context(nc.psum_tensor(name, shape, dt))

        p_h = ps("p_h", [P, 4, D])
        p_t = ps("p_t", [P, 2 * T0 * 4, RANK])
        p_tt = ps("p_tt", [P, 2 * C0], F16)
        p_o = ps("p_o", [P, 2, D])
        psum0.close()

        with ExitStack() as sems0:
            def sem(name):
                return sems0.enter_context(nc.semaphore(name))

            ld_small, ld_q, ld_w, ld_a0, ld_b0, ld_x, ld_const = (
                sem(n) for n in "ld_small ld_q ld_w ld_a0 ld_b0 ld_x ld_const".split())
            ld_g, ld_u, ld_d, ld_a1, ld_b1 = (sem(n) for n in "ld_g ld_u ld_d ld_a1 ld_b1".split())
            consts, z_ready = sem("consts"), sem("z_ready")
            deq = sem("deq")
            w_hi, w_lo = sem("w_hi"), sem("w_lo")
            m_ps, m_hi, m_lo = sem("m_ps"), sem("m_hi"), sem("m_lo")
            c_ps, c_done = sem("c_ps"), sem("c_done")
            wr_a0, wr_b0, wr_a1, wr_b1, got_a, got_b = (
                sem(n) for n in "wr_a0 wr_b0 wr_a1 wr_b1 got_a got_b".split())
            x_hi, x_lo, a_ps, t_f, t_hi, t_lo, tt_ps, tt_sb, base_done = (
                sem(n) for n in "x_hi x_lo a_ps t_f t_hi t_lo tt_ps tt_sb base_done".split())
            h_ps, h_hi, h_lo, o_ps, o_up, x1 = (sem(n) for n in "h_ps h_hi h_lo o_ps o_up x1".split())
            s_hi, s_lo = sem("s_hi"), sem("s_lo")

            block = sems0.enter_context(nc.Block())

            @block.sync
            def _(sp):
                sp.dma_start(perm_i[:], a["perm"]).then_inc(ld_small, 16)
                sp.dma_start(slot0[:], a["slot0"]).then_inc(ld_small, 16)
                sp.dma_start(slot1[:, 0:BATCH], a["slot1"]).then_inc(ld_small, 16)
                sp.dma_start(chan[:], a["chan"]).then_inc(ld_small, 16)
                sp.dma_start(b0[:], a["b0"]).then_inc(ld_small, 16)
                sp.dma_start(fbias[:], a["fbias"]).then_inc(ld_small, 16)
                for t in range(KT):
                    words = a["qT"][t * 16:(t + 1) * 16, :]
                    sp.dma_start(q[:, t, :], words.unsqueeze(1).broadcast_to([16, 8, D])).then_inc(ld_q, 16)
                for table, dst in (("scT", sc), ("zrT", zr)):
                    halves = a[table].rearrange("(t h) o -> h t o", h=2)
                    for h in range(2):
                        sp.dma_start(dst[64 * h:64 * h + 64, :, :],
                                     halves[h].unsqueeze(0).broadcast_to([64, KT, D])).then_inc(ld_q, 16)
                sp.dma_start(a0_in[:], a["a0"].rearrange("p (s n) -> p s n", s=SLOTS0)).then_inc(ld_a0, 16)
                sp.dma_start(w_in[:], a["w0T"].rearrange("(t p) o -> p t o", p=P)).then_inc(ld_w, 16)
                xv = a["xT"].rearrange("(t p) n -> p t n", p=P)
                for c in range(N0):
                    sp.dma_start(xT[:, :, c * C0:(c + 1) * C0], xv[:, :, c * C0:(c + 1) * C0]).then_inc(ld_x, 16)
                sp.dma_start(b0_in[:], a["b0t"].rearrange("(t p) o -> p t o", p=P)).then_inc(ld_b0, 16)
                sp.dma_start(proj[:], a["proj"].rearrange("(t p) n -> p t n", p=P)).then_inc(ld_const, 16)
                sp.dma_start(base[:], a["base"].broadcast_to([P, NPROJ])).then_inc(ld_const, 16)
                sp.dma_start(gate[:, 0:1], a["gate"].broadcast_to([P, 1])).then_inc(ld_const, 16)
                sp.dma_start(branch[:], a["branch"]).then_inc(ld_const, 16)
                sp.wait_ge(w_lo, 1)
                sp.dma_start(a0_tab.rearrange("s p n -> p s n"),
                             a0_out[:].rearrange("p s h n -> p s (h n)")).then_inc(wr_a0, 16)
                sp.wait_ge(w_lo, 3)
                for t in range(KT):
                    for part in range(2):
                        sp.dma_start(b0_tab[8 * t:8 * t + 8, part], b0_out[:, part, t, :]).then_inc(wr_b0, 16)

                def gather_a(c):
                    for b in range(B0):
                        s = sp.value_load(slot0[0:1, bass.ds(c * B0 + b, 1)], min_val=0, max_val=SLOTS0 - 1)
                        if b == 0:
                            wait(sp, a_ps, c * 1)
                        sp.dma_start(a0g[:, b, :, :].rearrange("p h n -> p (h n)"),
                                     a0_tab[bass.ds(s, 1)].rearrange("a p n -> (a p) n")).then_inc(got_a, 16)

                def gather_b(c):
                    for b in range(B0):
                        s = sp.value_load(slot0[0:1, bass.ds(c * B0 + b, 1)], min_val=0, max_val=SLOTS0 - 1)
                        if b == 0:
                            wait(sp, h_ps, c * KT)
                        sp.dma_start(b0g[64 * (b % 2):64 * (b % 2) + 64, b // 2, :],
                                     b0_tab[bass.ds(s, 1)].rearrange("a h r n -> a (h r) n")
                                     .broadcast_to([2, 2 * RANK, D])).then_inc(got_b, 16)

                def load_pieces(c):
                    wait(sp, s_lo, c * 5)
                    sp.dma_start(s_g[:], a["wgT"][bass.ds(c * P, P), :]).then_inc(ld_g, 16)
                    sp.dma_start(s_u[:], a["wuT"][bass.ds(c * P, P), :]).then_inc(ld_u, 16)
                    sp.dma_start(s_d[:], a["wdT"][bass.ds(c * DT_PIECE * P, DT_PIECE * P), :]
                                 .rearrange("(t p) n -> p t n", p=P)).then_inc(ld_d, 16)
                    sp.dma_start(s_a[:], a["a1"][bass.ds(c * P, P), :]
                                 .rearrange("p (s n) -> p s n", n=A1W)).then_inc(ld_a1, 16)
                    sp.dma_start(s_b[:], a["b1t"][bass.ds(c * P, P), :]).then_inc(ld_b1, 16)

                def store_pieces(c):
                    sp.wait_ge(s_lo, c * 5 + 4)
                    sp.dma_start(a1_tab[bass.ds(c * 4, 4)].rearrange("s p n -> p s n"),
                                 sa_out[:].rearrange("p s h n -> p s (h n)")).then_inc(wr_a1, 16)
                    sp.wait_ge(s_lo, c * 5 + 5)
                    for part in range(2):
                        sp.dma_start(b1_tab[bass.ds(4 * c, 4), part].rearrange("s r (k n) -> s (r k) n", k=2), sb_out[:, part, :]).then_inc(wr_b1, 16)

                sp.wait_ge(ld_small, 6 * 16)
                sp.wait_ge(wr_a0, 16)
                gather_a(0)
                sp.wait_ge(wr_b0, 2 * KT * 16)
                gather_b(0)
                load_pieces(0)
                with sp.Fori(1, N0) as c:
                    store_pieces(c - 1)
                    load_pieces(c)
                    gather_a(c)
                    gather_b(c)
                store_pieces(N0 - 1)
                sp.wait_ge(wr_a1, N0 * 16)
                sp.wait_ge(wr_b1, N0 * 2 * 16)
                for s, n in ((ld_q, 8), (ld_const, 4), (got_a, BATCH), (got_b, BATCH)):
                    sp.wait_ge(s, n * 16)

            @block.gpsimd
            def _(pool):
                pool.iota(shift4[:], [[0, 1]], base=0, channel_multiplier=4).then_inc(consts, 1)
                pool.iota(col_i[:], [[1, D]], base=0, channel_multiplier=0).then_inc(consts, 1)
                pool.memset(ident32[:], 0.0).then_inc(z_ready, 1)
                pool.memset(mask0[:], LORA0).then_inc(z_ready, 1)
                pool.memset(mask1[:], LORA1).then_inc(z_ready, 1)
                pool.memset(slot1[:, BATCH:BATCH + B1], 0).then_inc(z_ready, 1)
                pool.memset(xT[:, :, TOK:TOK + C1], 0.0).then_inc(z_ready, 1)
                pool.wait_ge(z_ready, 5)
                pool.affine_select(out=ident32[:], in_=ident32[:], compare_op=ALU.not_equal, fill=1.0, base=0,
                                   pattern=[[-1, P]], channel_multiplier=1).then_inc(z_ready, 1)
                for m in (mask0, mask1):
                    pool.affine_select(out=m[:], in_=m[:], compare_op=ALU.is_ge, fill=0.0, base=0,
                                       pattern=[[-SEQ, 4], [0, RANK]], channel_multiplier=1).then_inc(z_ready, 1)
                pool.wait_ge(z_ready, 8)
                pool.tensor_copy(ident16[:], ident32[:]).then_inc(consts, 1)
                for m in (mask0, mask1):
                    pool.affine_select(out=m[:], in_=m[:], compare_op=ALU.is_ge, fill=0.0, base=SEQ - 1,
                                       pattern=[[SEQ, 4], [0, RANK]], channel_multiplier=-1).then_inc(consts, 1)

                def residual(c):
                    for o in range(KT):
                        pool.wait_ge(o_up, c * KT + o + 1)
                        xo = xT[:, o, bass.ds(c * C0, C0)]
                        pool.tensor_tensor(xo, xo, o_sb[:, o % 2, :], ALU.add).then_inc(x1, 1)

                pool.wait_ge(ld_x, N0 * 16)
                residual(0)
                with pool.Fori(1, N0) as c:
                    residual(c)

            @block.scalar
            def _(act):
                def hi(out, in_, done, scale=SCALE):
                    nc.scalar.activation(out, in_, ACT.Identity, scale=scale).then_inc(done, 1)

                act.wait_ge(ld_a0, 16)
                hi(a0_out[:, :, 0, :], a0_in[:], w_hi)
                act.wait_ge(ld_w, 16)
                hi(w0[:, 0], w_in[:], w_hi)
                act.wait_ge(ld_b0, 16)
                hi(b0_out[:, 0], b0_in[:], w_hi)
                act.wait_ge(ld_small, 6 * 16)
                hi(b0s[:, :, 0], b0[:], w_hi)
                act.wait_ge(deq, 5)
                hi(wq16[:, 0], sc[:], w_hi)

                def x_part(c):
                    wait(act, base_done, c * 1)
                    hi(xs[:, 0], xT[:, :, bass.ds(c * C0, C0)], x_hi, scale=1.0)

                def body(c):
                    x_part(c)
                    act.wait_ge(t_f, c + 1)
                    wait(act, tt_ps, c * 1)
                    for copy in range(2):
                        nc.scalar.copy(t0_s[:, :, copy, :], t0_f[:]).then_inc(t_hi, 1)
                    for k, (ready, out, in_) in enumerate((
                            (ld_g, wg[:, 0, bass.ds(c, 1), :], s_g[:].unsqueeze(1)),
                            (ld_u, wu[:, 0, bass.ds(c, 1), :], s_u[:].unsqueeze(1)),
                            (ld_d, wd[:, 0, bass.ds(c * DT_PIECE, DT_PIECE), :], s_d[:]),
                            (ld_a1, sa_out[:, :, 0, :], s_a[:]),
                            (ld_b1, sb_out[:, 0, :], s_b[:]))):
                        act.wait_ge(ready, c * 16 + 16)
                        if k == 3:
                            wait(act, wr_a1, c * 16)
                        if k == 4:
                            wait(act, wr_b1, c * 32)
                        hi(out, in_, s_hi)
                    act.wait_ge(tt_ps, c + 1)
                    wait(act, h_ps, c * KT)
                    nc.scalar.copy(t0_t[:].rearrange("p (t n) -> p t n", t=T0),
                                   p_tt[:].rearrange("p (t n) -> p t n", t=T0)[:, :, 64:64 + P]).then_inc(tt_sb, 1)
                    for o in range(KT):
                        act.wait_ge(h_ps, c * KT + o + 1)
                        if o == 0:
                            wait(act, o_ps, c * KT)
                        hi(hs[:, 0, o, :], p_h[:, o, :], h_hi, scale=INV)
                    for o in range(KT):
                        act.wait_ge(o_ps, c * KT + o + 1)
                        wait(act, x1, c * KT + o - 1)
                        nc.scalar.activation(o_sb[:, o % 2, :], p_o[:, o % 2, :], ACT.Identity,
                                             bias=cvec[:, o:o + 1], scale=INV).then_inc(o_up, 1)

                for o in range(KT):
                    act.wait_ge(m_ps, o + 1)
                    hi(mw[:, 0, o, :], p_h[:, o, :], m_hi, scale=chan[:, o:o + 1])
                act.wait_ge(ld_x, N0 * 16)
                act.wait_ge(c_done, 2)
                body(0)
                with act.Fori(1, N0) as c:
                    body(c)

            @block.vector
            def _(dve):
                def lo(out, in_, high, done, scale=SCALE):
                    nc.vector.scalar_tensor_tensor(out, in_, scale, high, ALU.mult, ALU.subtract).then_inc(done, 1)

                dve.wait_ge(consts, 2)
                dve.wait_ge(ld_small, 6 * 16)
                nc.vector.tensor_scalar(shift[:], shift4[:], 31, None, ALU.bitwise_and).then_inc(deq, 1)
                nc.vector.tensor_copy(perm_f[:], perm_i[:]).then_inc(deq, 1)
                dve.wait_ge(deq, 2)
                dve.wait_ge(w_hi, 1)
                lo(a0_out[:, :, 1, :], a0_in[:], a0_out[:, :, 0, :], w_lo)
                for t in range(KT):
                    nc.vector.tensor_scalar(onehot[:, t, :], col_i[:], perm_f[:, t:t + 1], None,
                                            ALU.is_equal).then_inc(m_lo, 1)
                dve.wait_ge(ld_q, 8 * 16)
                nc.vector.tensor_scalar(q4[:], q[:], shift[:, 0:1].bitcast(U32), 15, ALU.logical_shift_right,
                                        ALU.bitwise_and).then_inc(deq, 1)
                dve.wait_ge(deq, 3)
                nc.vector.tensor_tensor(sc[:], q4[:], sc[:], ALU.mult).then_inc(deq, 1)
                dve.wait_ge(deq, 4)
                nc.vector.tensor_tensor(sc[:], sc[:], zr[:], ALU.add).then_inc(deq, 1)
                dve.wait_ge(w_hi, 2)
                lo(w0[:, 1], w_in[:], w0[:, 0], w_lo)
                dve.wait_ge(w_hi, 3)
                lo(b0_out[:, 1], b0_in[:], b0_out[:, 0], w_lo)
                dve.wait_ge(w_hi, 4)
                lo(b0s[:, :, 1], b0[:], b0s[:, :, 0], w_lo)
                dve.wait_ge(w_hi, 5)
                dve.wait_ge(deq, 5)
                lo(wq16[:, 1], sc[:], wq16[:, 0], w_lo)
                for o in range(KT):
                    dve.wait_ge(m_hi, o + 1)
                    nc.vector.scalar_tensor_tensor(mw[:, 1, o, :], p_h[:, o, :], chan[:, o:o + 1], mw[:, 0, o, :],
                                                   ALU.mult, ALU.subtract).then_inc(m_lo, 1)
                dve.wait_ge(c_ps, 1)
                nc.vector.tensor_reduce(csum[:], p_t[:, 0:KT, 0:2], AX.X, ALU.add).then_inc(c_done, 1)
                dve.wait_ge(c_done, 1)
                nc.vector.scalar_tensor_tensor(cvec[:], csum[:], INV * INV, fbias[:], ALU.mult,
                                               ALU.add).then_inc(c_done, 1)
                dve.wait_ge(consts, 5)

                def body(c):
                    dve.wait_ge(x_hi, c + 1)
                    nc.vector.tensor_tensor(xs[:, 1], xT[:, :, bass.ds(c * C0, C0)], xs[:, 0],
                                            ALU.subtract).then_inc(x_lo, 1)
                    dve.wait_ge(a_ps, c + 1)
                    wait(dve, t_hi, 2 * c)
                    nc.vector.tensor_tensor(
                        t0_f[:].rearrange("p (t b) r -> p t b r", b=4),
                        p_t[:, 0:T0 * 4, :].rearrange("p (t b) r -> p t b r", b=4),
                        mask0[:].unsqueeze(1).broadcast_to([P, T0, 4, RANK]), ALU.mult).then_inc(t_f, 1)
                    dve.wait_ge(t_hi, 2 * c + 2)
                    dve.wait_ge(t_f, c + 1)
                    for copy in range(2):
                        nc.vector.tensor_tensor(t0_s[:, :, 2 + copy, :], t0_f[:], t0_s[:, :, 0, :],
                                                ALU.subtract).then_inc(t_lo, 1)
                    for k, (out, in_, high) in enumerate((
                            (wg[:, 1, bass.ds(c, 1), :], s_g[:].unsqueeze(1), wg[:, 0, bass.ds(c, 1), :]),
                            (wu[:, 1, bass.ds(c, 1), :], s_u[:].unsqueeze(1), wu[:, 0, bass.ds(c, 1), :]),
                            (wd[:, 1, bass.ds(c * DT_PIECE, DT_PIECE), :], s_d[:],
                             wd[:, 0, bass.ds(c * DT_PIECE, DT_PIECE), :]),
                            (sa_out[:, :, 1, :], s_a[:], sa_out[:, :, 0, :]),
                            (sb_out[:, 1, :], s_b[:], sb_out[:, 0, :]))):
                        dve.wait_ge(s_hi, c * 5 + k + 1)
                        lo(out, in_, high, s_lo)
                    for o in range(KT):
                        dve.wait_ge(h_hi, c * KT + o + 1)
                        lo(hs[:, 1, o, :], p_h[:, o, :], hs[:, 0, o, :], h_lo, scale=INV)

                body(0)
                with dve.Fori(1, N0) as c:
                    body(c)

            @block.tensor
            def _(pe):
                pe.wait_ge(w_lo, 5)
                pe.wait_ge(m_lo, KT)
                for i in range(KT):
                    for part in range(2):
                        for t in range(KT):
                            mm = nc.tensor.matmul(p_h[:, i, :], onehot[:, t, i * P:(i + 1) * P], wq16[:, part, t, :],
                                                  start=(part == 0 and t == 0), stop=(part == 1 and t == KT - 1))
                    mm.then_inc(m_ps, 1)
                pe.wait_ge(m_lo, 2 * KT)
                for o in range(KT):
                    for part in range(2):
                        for i in range(KT):
                            mm = nc.tensor.matmul(p_t[:, o, 0:2], mw[:, part, i, o * P:(o + 1) * P], b0s[:, i, :],
                                                  start=(part == 0 and i == 0), stop=(part == 1 and i == KT - 1))
                mm.then_inc(c_ps, 1)
                pe.wait_ge(consts, 5)
                pe.wait_ge(c_done, 1)

                def body(c):
                    pe.wait_ge(x_lo, c + 1)
                    pe.wait_ge(got_a, c * (B0 * 16) + B0 * 16)
                    wait(pe, t_f, c * 1)
                    for t in range(T0):
                        for n, (sx, sa) in enumerate(PASSES):
                            for i in range(KT):
                                mm = nc.tensor.matmul(p_t[:, 4 * t:4 * t + 4, :], xs[:, sx, i, t * P:(t + 1) * P],
                                                      a0g[:, 4 * t:4 * t + 4, sa, i * RANK:(i + 1) * RANK],
                                                      start=(n == 0 and i == 0), stop=(n == 2 and i == KT - 1))
                    mm.then_inc(a_ps, 1)
                    for o in range(KT):
                        wait(pe, h_lo, c * KT - KT + o + 1)
                        if o == KT - 1:
                            pe.wait_ge(t_lo, 2 * c + 2)
                            wait(pe, tt_sb, c * 1)
                        for n, (sw, sx) in enumerate(PASSES):
                            for i in range(KT):
                                mm = nc.tensor.matmul(p_h[:, o, :], w0[:, sw, i, o * P:(o + 1) * P], xs[:, sx, i, :],
                                                      start=(n == 0 and i == 0), stop=(n == 2 and i == KT - 1))
                    mm.then_inc(base_done, 1)
                    for t in range(T0):
                        for g in range(2):
                            at = (2 * t + 1 - g) * P
                            mm = nc.tensor.transpose(
                                p_tt[:, at:at + P],
                                t0_s[:, 4 * t + 2 * g:4 * t + 2 * g + 2, :, :].rearrange("p b s r -> p (b s r)"),
                                ident16[:])
                    mm.then_inc(tt_ps, 1)
                    pe.wait_ge(tt_sb, c + 1)
                    pe.wait_ge(got_b, c * (B0 * 16) + B0 * 16)
                    for o in range(KT):
                        for g in range(G0):
                            cols = slice(g * PAIR, (g + 1) * PAIR)
                            rows = slice((g ^ 1) * PAIR, ((g ^ 1) + 1) * PAIR)
                            mm = nc.tensor.matmul(p_h[:, o, cols], b0g[:, g, o * P:(o + 1) * P], t0_t[:, rows],
                                                  start=False, stop=True, skip_group_check=True)
                        mm.then_inc(h_ps, 1)
                    pe.wait_ge(h_lo, c * KT + KT)
                    for o in range(KT):
                        wait(pe, o_up, c * KT + o - 1)
                        for n, (sw, sx) in enumerate(PASSES):
                            for i in range(KT):
                                mm = nc.tensor.matmul(p_o[:, o % 2, :], mw[:, sw, i, o * P:(o + 1) * P], hs[:, sx, i, :],
                                                      start=(n == 0 and i == 0), stop=(n == 2 and i == KT - 1))
                        mm.then_inc(o_ps, 1)

                body(0)
                with pe.Fori(1, N0) as c:
                    body(c)

        l1 = maker(ctx)
        xs1 = l1("xs1", [P, 2, 2, KT, C1], F16)
        acts = l1("acts", [P, 2, FT, C1], F16)
        sil = l1("sil", [P, 2, C1], F32)
        prod = l1("prod", [P, 2, C1], F32)
        y1 = l1("y1", [P, 2, T1, D], F32)
        yT = l1("yT", [P, T1, KT, P], F32)
        xc = l1("xc", [P, KT, C1], F32)
        ag = l1("ag", [P, B1, 2, GUW], F16)
        ad = l1("ad", [P, B1, 2, FT * RANK], F16)
        bg = l1("bg", [P, G1, GU], F16)
        bd = l1("bd", [P, G1, D], F16)
        ta_f = l1("ta_f", [P, T1 * 2 * 4, RANK], F32)
        ta_s = l1("ta_s", [P, T1 * 2 * 4, 4, RANK], F16)
        ta_t = l1("ta_t", [P, 2, T1 * 2, P], F16)
        td_f = l1("td_f", [P, T1 * 4, RANK], F32)
        td_s = l1("td_s", [P, T1 * 4, 4, RANK], F16)
        td_t = l1("td_t", [P, T1 * 2, P], F16)
        base_sb = l1("base_sb", [P, T1, D], F32)
        y_in = l1("y_in", [P, 2, D], F32)
        mix_sb = l1("mix_sb", [P, 2, D], F32)
        xpre = l1("xpre", [P, T1, P], F32)
        yb = l1("yb", [P, T1, P], F32)
        ssq = l1("ssq", [P, 2, T1], F32)
        sq_junk = l1("sq_junk", [P, T1, D], F16)
        ms = l1("ms", [P, T1], F32)
        lnms = l1("lnms", [P, T1], F32)
        rs0 = l1("rs0", [P, T1], F32)
        rs1 = l1("rs1", [P, T1], F32)
        rstd = l1("rstd", [P, T1], F32)
        lg = l1("lg", [P, T1 * 6, 4], F32)
        mx = l1("mx", [P, T1 * 6], F32)
        ex = l1("ex", [P, T1 * 6, 4], F32)
        rsum = l1("rsum", [P, T1 * 6], F32)
        rinv = l1("rinv", [P, T1 * 6], F32)
        lnr = l1("lnr", [P, T1 * 4], F32)
        hpp = l1("hpp", [P, T1, 2, 4], F32)
        lu = l1("lu", [P, T1, 4, 4], F32)
        cmax = l1("cmax", [P, T1, 4], F32)
        hr = l1("hr", [P, NT, 4, 4], F32)
        sums = l1("sums", [P, NT, 4], F32)
        inv = l1("inv", [P, NT, 4], F32)
        csums = l1("csums", [P, T1, 4], F32)
        cinv = l1("cinv", [P, T1, 4], F32)
        hg = l1("hg", [P, NT, 16], F32)
        eye = l1("eye", [P, 16], F32)
        gsig = l1("gsig", [P, 4], F32)

        y_tok = nc.dram_tensor("y_tok", [TOK, D], F32, kind="Internal")
        base_tok = nc.dram_tensor("base_tok", [TOK, D], F32, kind="Internal")

        psum1 = ExitStack()
        p_gu = ps("p_gu", [P, 2, 2, C1], stack=psum1)
        p_y = ps("p_y", [P, T1, D], stack=psum1)
        p_a = ps("p_a", [P, D], stack=psum1)
        p_at = ps("p_at", [P, 2 * D], F16, stack=psum1)
        p_m1 = ps("p_m1", [P, D], stack=psum1)
        p_m2 = ps("p_m2", [P, D], stack=psum1)

        with ExitStack() as sems1:
            def sem(name):
                return sems1.enter_context(nc.semaphore(name))

            got_ag, got_ad, got_bg, got_bd = (sem(n) for n in "got_ag got_ad got_bg got_bd".split())
            x_hi, x_lo = sem("x1_hi"), sem("x1_lo")
            ta_ps, ta_up, ta_hi, ta_lo, tat_ps, tat_sb = (
                sem(n) for n in "ta_ps ta_up ta_hi ta_lo tat_ps tat_sb".split())
            td_ps, td_up, td_hi, td_lo, tdt_ps, tdt_sb = (
                sem(n) for n in "td_ps td_up td_hi td_lo tdt_ps tdt_sb".split())
            gu_ps, sil_up, prods, act_hi, act_lo = (sem(n) for n in "gu_ps sil_up prods act_hi act_lo".split())
            y_ps, y_up, yt_ps, yt_sb, lg_ps = (sem(n) for n in "y_ps y_up yt_ps yt_sb lg_ps".split())
            to_act, from_act, chain = (sem(n) for n in "to_act from_act chain".split())
            round_step = [sem(f"round_step{g}") for g in range(len(GROUPS))]
            xp_up, xp_ps, xp_sb, yb_ps, yb_sb = (sem(n) for n in "xp_up xp_ps xp_sb yb_ps yb_sb".split())
            xb_ps, xc_up, mixed = (sem(n) for n in "xb_ps xc_up mixed".split())
            y_kept = [sem(f"y_kept{p}") for p in range(2)]
            base_up, base_kept = sem("base_up"), sem("base_kept")
            mix_in = [sem(f"mix_in{b}") for b in range(2)]
            stored = [sem(f"stored{b}") for b in range(2)]
            gate_e, gate_d, eye_up = (sem(n) for n in "gate_e gate_d eye_up".split())

            block = sems1.enter_context(nc.Block())

            def rows_of(f):
                return P if f < FT - 1 else FL


            @block.sync
            def _(sp):
                def gather(n, *tables):
                    with sp.Fori(0, G1) as g:
                        for b in range(2):
                            s = sp.value_load(slot1[0:1, bass.ds(2 * g + (n * B1 + b), 1)],
                                              min_val=0, max_val=SLOTS1 - 1)
                            for dst, table, cols, done in tables:
                                sp.dma_start(dst(g, b), table(s, cols)).then_inc(done, 16)

                def a_rows(s, cols):
                    return (a1_tab[bass.ds(s, 1)].rearrange("a p (h n) -> (a p) h n", h=2)[:, :, cols])

                def b_rows(s, cols):
                    rows = b1_tab[bass.ds(s, 1)].rearrange("a h r n -> a (h r) n")[:, :, cols]
                    return rows.broadcast_to([2, 2 * RANK, cols.stop - cols.start])

                def pair_rows(dst):
                    return lambda g, b: dst[64 * b:64 * b + 64, bass.ds(g, 1), :].rearrange("p g n -> p (g n)")

                def batch(dst):
                    return lambda g, b: dst[:, bass.ds(2 * g + b, 1), :, :].rearrange("p g h n -> p (g h) n")

                def gather_ag(n):
                    wait(sp, ta_ps, n)
                    gather(n, (batch(ag), a_rows, slice(0, GUW), got_ag))

                def gather_down(n):
                    wait(sp, td_ps, n)
                    wait(sp, y_ps, n * T1)
                    gather(n, (batch(ad), a_rows, slice(GUW, A1W), got_ad),
                           (pair_rows(bd), b_rows, slice(GU, B1W), got_bd))

                def gather_bg(n):
                    wait(sp, gu_ps, n * FT)
                    gather(n, (pair_rows(bg), b_rows, slice(0, GU), got_bg))

                def keep_y(n):
                    sp.wait_ge(y_up, 2 * T1 * (n + 1))
                    for t in range(T1):
                        sp.dma_start(y_tok[(n * T1 + t) * P:(n * T1 + t + 1) * P, :],
                                     y1[:, n % 2, t, :]).then_inc(y_kept[n % 2], 16)

                def keep_base(n):
                    sp.wait_ge(base_up, n + 1)
                    for t in range(T1):
                        sp.dma_start(base_tok[(n * T1 + t) * P:(n * T1 + t + 1) * P, :],
                                     base_sb[:, t, :]).then_inc(base_kept, 16)

                def mix_load(t):
                    b = t % 2
                    wait(sp, stored[b], t // 2 * 16)
                    sp.dma_start(y_in[:, b, :], y_tok[t * P:(t + 1) * P, :]).then_inc(mix_in[b], 16)
                    sp.dma_start(mix_sb[:, b, :], base_tok[t * P:(t + 1) * P, :]).then_inc(mix_in[b], 16)

                def mix_first(first, end):
                    for p in range(2):
                        steps = len(range(p, -(-end // T1), 2))
                        sp.wait_ge(y_kept[p], steps * T1 * 16)
                    sp.wait_ge(base_kept, end * 16)
                    mix_load(first)
                    mix_load(first + 1)

                def mix_next(t, end):
                    sp.wait_ge(mixed, t + 1)
                    sp.dma_start(out[t * P:(t + 1) * P, :], mix_sb[:, t % 2, :]).then_inc(stored[t % 2], 16)
                    if t + 2 < end:
                        mix_load(t + 2)

                gather_ag(0)
                gather_bg(0)
                for n in range(N1):
                    if n:
                        keep_y(n - 1)
                    if n == N1 - 2:
                        mix_first(*GROUPS[0])
                    if n == N1 - 1:
                        mix_next(0, GROUPS[0][1])
                        mix_next(1, GROUPS[0][1])
                    gather_ag(n + 1)
                    gather_down(n)
                    if n == N1 - 1:
                        mix_next(2, GROUPS[0][1])
                        mix_next(3, GROUPS[0][1])
                    if n + 1 < N1:
                        gather_bg(n + 1)
                    if n:
                        keep_base(n - 1)
                for t in range(4, GROUPS[0][1]):
                    mix_next(t, GROUPS[0][1])
                keep_y(N1 - 1)
                mix_first(*GROUPS[1])
                for t in range(*GROUPS[1]):
                    mix_next(t, GROUPS[1][1])
                keep_base(N1 - 1)
                mix_first(*GROUPS[2])
                for t in range(*GROUPS[2]):
                    mix_next(t, GROUPS[2][1])
                sp.wait_ge(got_ag, (N1 + 1) * B1 * 16)
                for b in range(2):
                    sp.wait_ge(stored[b], NT // 2 * 16)

            @block.gpsimd
            def _(pool):
                pool.memset(eye[:], 0.0).then_inc(eye_up, 1)
                pool.wait_ge(eye_up, 1)
                pool.affine_select(out=eye[:].rearrange("p (i j) -> p i j", j=4),
                                   in_=eye[:].rearrange("p (i j) -> p i j", j=4), compare_op=ALU.not_equal,
                                   fill=1.0, base=0, pattern=[[1, 4], [-1, 4]],
                                   channel_multiplier=0).then_inc(eye_up, 1)

                def x_low(n, par):
                    pool.wait_ge(x_hi, n + 1)
                    pool.tensor_tensor(xs1[:, par, 1], xT[:, :, bass.ds(n * C1, C1)], xs1[:, par, 0],
                                       ALU.subtract).then_inc(x_lo, 1)

                def keep_x(n):
                    pool.tensor_copy(xc[:], xT[:, :, bass.ds(n * C1, C1)]).then_inc(xc_up, 1)

                def step(n, par, first=False, second=False):
                    for f in range(FT):
                        m = rows_of(f)
                        if f == 6 and not (first or second):
                            pool.wait_ge(xb_ps, (n - 1) * T1)
                        pool.wait_ge(act_hi, n * FT + f + 1)
                        pool.tensor_tensor(acts[0:m, 1, f, :], prod[0:m, (par * FT + f) % 2, :], acts[0:m, 0, f, :],
                                           ALU.subtract).then_inc(act_lo, 1)
                        if f == 4:
                            x_low(n + 1, 1 - par)
                        if f == 6 and not first:
                            keep_x(n - 1)

                x_low(0, 0)
                step(0, 0, first=True)
                step(1, 1, second=True)
                with pool.Fori(1, N1 // 2) as s:
                    step(2 * s, 0)
                    step(2 * s + 1, 1)
                pool.wait_ge(xb_ps, (N1 - 1) * T1)
                keep_x(N1 - 1)

            @block.scalar
            def _(act):
                def split_x(n, par):
                    nc.scalar.copy(xs1[:, par, 0], xT[:, :, bass.ds(n * C1, C1)]).then_inc(x_hi, 1)

                def a_high(n):
                    act.wait_ge(ta_up, n + 1)
                    for copy in range(2):
                        if copy == 0:
                            wait(act, tat_ps, n)
                        nc.scalar.copy(ta_s[:, :, copy, :], ta_f[:]).then_inc(ta_hi, 1)

                def a_rows(n, par):
                    act.wait_ge(tat_ps, n + 1)
                    nc.scalar.copy(ta_t[:, par], p_at[:].rearrange("p (u n) -> p u n", u=2 * T1)
                                   [:, :, 64:64 + P]).then_inc(tat_sb, 1)

                def high(n, par, f):
                    m = rows_of(f)
                    act.wait_ge(prods, n * FT + f + 1)
                    if f == 0:
                        wait(act, y_ps, n * T1)
                    nc.scalar.copy(acts[0:m, 0, f, :], prod[0:m, (par * FT + f) % 2, :]).then_inc(act_hi, 1)

                def y_transposed(n):
                    act.wait_ge(yt_ps, n + 1)
                    wait(act, lg_ps, n)
                    for t, p in enumerate((p_m1, p_a)):
                        nc.scalar.copy(yT[:, t].rearrange("p k n -> p (k n)"), p[:]).then_inc(yt_sb, 1)

                def root(n):
                    act.wait_ge(to_act, 4 * n + 1)
                    nc.scalar.activation(lnms[:], ms[:], ACT.Ln).then_inc(from_act, 1)
                    act.wait_ge(from_act, 5 * n + 1)
                    nc.scalar.activation(rs0[:], lnms[:], ACT.Exp, scale=-0.5).then_inc(from_act, 1)

                def exps(n):
                    act.wait_ge(to_act, 4 * n + 2)
                    v = ex[:].rearrange("p (t k) j -> p t (k j)", t=T1)
                    w = lg[:].rearrange("p (t k) j -> p t (k j)", t=T1)
                    nc.scalar.activation(v[:, :, 0:16], w[:, :, 0:16], ACT.Exp, scale=10.0)
                    nc.scalar.activation(v[:, :, 16:24], w[:, :, 16:24], ACT.Exp).then_inc(from_act, 1)
                    act.wait_ge(to_act, 4 * n + 3)
                    nc.scalar.activation(lnr[:].rearrange("p (t k) -> p t k", t=T1),
                                         rsum[:].rearrange("p (t k) -> p t k", t=T1)[:, :, 0:4],
                                         ACT.Ln).then_inc(from_act, 1)
                    act.wait_ge(to_act, 4 * n + 4)
                    nc.scalar.activation(ex[:].rearrange("p (t k) j -> p t (k j)", t=T1)[:, :, 0:16],
                                         lu[:].rearrange("p t i j -> p t (i j)"), ACT.Exp).then_inc(from_act, 1)

                def x_pre_out(n):
                    act.wait_ge(xp_ps, n + 1)
                    wait(act, yb_ps, n)
                    nc.scalar.copy(xpre[:].rearrange("p t c -> p (t c)"), p_m2[:, 0:C1]).then_inc(xp_sb, 1)

                def y_out(n):
                    act.wait_ge(yb_ps, n + 1)
                    wait(act, base_up, n)
                    nc.scalar.copy(yb[:].rearrange("p t c -> p (t c)"), p_m2[:, C1:2 * C1]).then_inc(yb_sb, 1)

                def step(n, par, first=False):
                    for f in range(FT):
                        m = rows_of(f)
                        act.wait_ge(gu_ps, n * FT + f + 1)
                        wait(act, prods, n * FT + f - 1)
                        nc.scalar.activation(sil[0:m, (par * FT + f) % 2, :], p_gu[0:m, (par * FT + f) % 2, 0, :], ACT.Silu,
                                             scale=INV).then_inc(sil_up, 1)
                        if f:
                            high(n, par, f - 1)
                        if not first:
                            if f == 0:
                                y_transposed(n - 1)
                            if f == 1:
                                act.preload_act_table_set("natural_log_exp_and_others")
                                root(n - 1)
                                exps(n - 1)
                                act.preload_act_table_set("silu_and_others")
                            if f == 5:
                                x_pre_out(n - 1)
                            if f == 7:
                                y_out(n - 1)
                        if f == 3:
                            split_x(n + 1, 1 - par)
                        if f == 8:
                            a_high(n + 1)
                    high(n, par, FT - 1)
                    a_rows(n + 1, 1 - par)
                    act.wait_ge(td_up, n + 1)
                    for copy in range(2):
                        if copy == 0:
                            wait(act, tdt_ps, n)
                        nc.scalar.copy(td_s[:, :, copy, :], td_f[:]).then_inc(td_hi, 1)
                    act.wait_ge(tdt_ps, n + 1)
                    nc.scalar.copy(td_t[:].rearrange("p u n -> p (u n)"), p_at[:, 0:D]).then_inc(tdt_sb, 1)
                    for t in range(T1):
                        act.wait_ge(y_ps, n * T1 + t + 1)
                        if t == 0:
                            wait(act, y_up, 2 * T1 * n)
                            wait(act, y_kept[par], (n - par) * T1 * 8)
                        nc.scalar.activation(y1[:, par, t, :], p_y[:, t, :], ACT.Identity, scale=INV).then_inc(y_up, 1)
                        nc.scalar.activation(sq_junk[:, t, :], p_y[:, t, :], ACT.Square, scale=INV,
                                             accum_out=ssq[:, par, t:t + 1]).then_inc(y_up, 1)

                nc.scalar.activation(gsig[:, 0:1], gate[:, 0:1], ACT.Exp, scale=-1.0).then_inc(gate_e, 1)
                split_x(0, 0)
                a_high(0)
                a_rows(0, 0)
                step(0, 0, first=True)
                step(1, 1)
                with act.Fori(1, N1 // 2) as s:
                    step(2 * s, 0)
                    step(2 * s + 1, 1)
                act.preload_act_table_set("natural_log_exp_and_others")
                root(N1 - 1)
                y_transposed(N1 - 1)
                exps(N1 - 1)
                x_pre_out(N1 - 1)
                y_out(N1 - 1)

            @block.vector
            def _(dve):
                count = [0]

                def link(ins):
                    count[0] += 1
                    ins.then_inc(chain, 1)
                    dve.wait_ge(chain, count[0])

                def restart():
                    dve.sem_clear(chain)
                    count[0] = 0

                def take_a(n):
                    dve.wait_ge(ta_ps, n + 1)
                    wait(dve, ta_hi, 2 * n)
                    nc.vector.tensor_tensor(
                        ta_f[:].rearrange("p (u b) r -> p u (b r)", b=4),
                        p_a[:, 0:C1].rearrange("p (u m) -> p u m", u=2 * T1),
                        mask1[:].rearrange("p b r -> p (b r)").unsqueeze(1).broadcast_to([P, 2 * T1, 4 * RANK]),
                        ALU.mult).then_inc(ta_up, 1)

                def low_a(n):
                    dve.wait_ge(ta_hi, 2 * n + 2)
                    for copy in range(2):
                        nc.vector.tensor_tensor(ta_s[:, :, 2 + copy, :], ta_f[:], ta_s[:, :, 0, :],
                                                ALU.subtract).then_inc(ta_lo, 1)

                def logits(m, par):
                    link(nc.vector.tensor_scalar(rs1[:], rs0[:], 1.0, None, ALU.mult))
                    link(nc.vector.tensor_tensor(rs1[:], rs0[:], rs0[:], ALU.mult))
                    link(nc.vector.tensor_tensor(rs1[:], rs1[:], ms[:], ALU.mult))
                    link(nc.vector.tensor_scalar(rs1[:], rs1[:], -0.5, 1.5, ALU.mult, ALU.add))
                    link(nc.vector.tensor_tensor(rstd[:], rs0[:], rs1[:], ALU.mult))
                    dve.wait_ge(lg_ps, m + 1)
                    for t in range(T1):
                        last = nc.vector.scalar_tensor_tensor(
                            lg[:].rearrange("p (t k) j -> p t (k j)", t=T1)[:, t, :],
                            p_m2[:, t * NPROJ:(t + 1) * NPROJ], rstd[:, t:t + 1], base[:], ALU.mult, ALU.add)
                    link(last)
                    link(nc.vector.tensor_reduce(mx[:], lg[:], AX.X, ALU.max))
                    nc.vector.tensor_tensor(lg[:], lg[:], mx[:].unsqueeze(2).broadcast_to([P, T1 * 6, 4]),
                                            ALU.subtract).then_inc(to_act, 1)
                    dve.wait_ge(from_act, 5 * m + 3)
                    nc.vector.tensor_reduce(rsum[:], ex[:], AX.X, ALU.add).then_inc(to_act, 1)
                    dve.wait_ge(to_act, 4 * m + 3)
                    link(nc.vector.reciprocal(rinv[:], rsum[:]))
                    link(nc.vector.tensor_tensor(
                        hpp[:], ex[:].rearrange("p (t k) j -> p t k j", t=T1)[:, :, 4:6, :],
                        rinv[:].rearrange("p (t k) -> p t k", t=T1)[:, :, 4:6].unsqueeze(3)
                        .broadcast_to([P, T1, 2, 4]), ALU.mult))
                    dve.wait_ge(from_act, 5 * m + 4)
                    for t in range(T1):
                        last = nc.vector.scalar_tensor_tensor(
                            lu[:, t], lg[:, 6 * t:6 * t + 4, :], 10.0,
                            lnr[:, 4 * t:4 * t + 4].unsqueeze(2).broadcast_to([P, 4, 4]), ALU.mult, ALU.subtract)
                    link(last)
                    link(nc.vector.tensor_reduce(cmax[:], lu[:].rearrange("p t i j -> p t j i"), AX.X, ALU.max))
                    nc.vector.tensor_tensor(lu[:], lu[:], cmax[:].unsqueeze(2).broadcast_to([P, T1, 4, 4]),
                                            ALU.subtract).then_inc(to_act, 1)
                    dve.wait_ge(from_act, 5 * m + 5)
                    e2 = ex[:].rearrange("p (t k) j -> p t k j", t=T1)[:, :, 0:4, :]
                    link(nc.vector.tensor_reduce(csums[:], e2.rearrange("p t i j -> p t j i"), AX.X, ALU.add))
                    link(nc.vector.reciprocal(cinv[:], csums[:]))
                    link(nc.vector.tensor_tensor(hr[:, m * T1:(m + 1) * T1], e2,
                                                 cinv[:].unsqueeze(2).broadcast_to([P, T1, 4, 4]), ALU.mult))

                def mean_square(m, par):
                    dve.wait_ge(y_up, 2 * T1 * (m + 1))
                    nc.vector.tensor_scalar(ms[:], ssq[:, par, :], 1.0 / D, RMS_EPS, ALU.mult,
                                            ALU.add).then_inc(to_act, 1)
                    dve.wait_ge(from_act, 5 * m + 2)

                def half_rounds(group):
                    tiles = slice(*group)
                    h = hr[:, tiles]
                    shape = [P, group[1] - group[0], 4, 4]
                    for r in range(2 * (ROUNDS - 1)):
                        rows = r % 2 == 0
                        yield nc.vector.tensor_reduce(
                            sums[:, tiles], h if rows else h.rearrange("p t i j -> p t j i"), AX.X, ALU.add)
                        yield nc.vector.reciprocal(inv[:, tiles], sums[:, tiles])
                        yield nc.vector.tensor_tensor(
                            h, h, inv[:, tiles].unsqueeze(3 if rows else 2).broadcast_to(shape), ALU.mult)

                rounds = [half_rounds(group) for group in GROUPS]
                issued = [0] * len(GROUPS)

                def advance(which, k, beside=()):
                    for _ in range(3 * k):
                        for g in which:
                            if issued[g]:
                                dve.wait_ge(round_step[g], issued[g])
                            ins = next(rounds[g], None)
                            if ins is not None:
                                ins.then_inc(round_step[g], 1)
                                issued[g] += 1
                        next(iter(beside), None)
                        if all(issued[g] == 6 * (ROUNDS - 1) for g in which):
                            break
                    for g in which:
                        dve.wait_ge(round_step[g], issued[g])

                def x_pre(m, par):
                    wait(dve, yb_ps, m)
                    for k in range(4):
                        for t in range(T1):
                            s_k = y1[:, par, t, k * P:(k + 1) * P]
                            if k == 0:
                                last = nc.vector.tensor_scalar(xpre[:, t, :], s_k, hpp[:, t, 0, 0:1], None, ALU.mult)
                            else:
                                last = nc.vector.scalar_tensor_tensor(xpre[:, t, :], s_k, hpp[:, t, 0, k:k + 1],
                                                                      xpre[:, t, :], ALU.mult, ALU.add)
                        if k < 3:
                            link(last)
                    last.then_inc(xp_up, 1)

                def base_of(m):
                    dve.wait_ge(yb_sb, m + 1)
                    dve.wait_ge(xb_ps, m * T1 + T1)
                    wait(dve, base_kept, m * T1 * 16)
                    for t, back in enumerate((p_m1, p_m2)):
                        for i in range(4):
                            last = nc.vector.scalar_tensor_tensor(
                                base_sb[:, t, i * P:(i + 1) * P], yb[:, t, :], hpp[:, t, 1, i:i + 1],
                                back[:, i * P:(i + 1) * P], ALU.mult, ALU.add)
                    last.then_inc(base_up, 1)

                def gated(group):
                    n = group[1] - group[0]
                    link(nc.vector.scalar_tensor_tensor(
                        hg[:, slice(*group)], hr[:, slice(*group)].rearrange("p t i j -> p t (i j)"), gsig[:, 2:3],
                        eye[:].unsqueeze(1).broadcast_to([P, n, 16]), ALU.mult, ALU.add))

                def mixing(first, end):
                    for t in range(first, end):
                        b = t % 2
                        dve.wait_ge(mix_in[b], (t // 2 + 1) * 32)
                        for k in range(4):
                            for i in range(4):
                                o = mix_sb[:, b, i * P:(i + 1) * P]
                                ins = nc.vector.scalar_tensor_tensor(
                                    o, y_in[:, b, k * P:(k + 1) * P], hg[:, t, 4 * i + k:4 * i + k + 1], o,
                                    ALU.mult, ALU.add)
                                if k == 3 and i == 3:
                                    ins.then_inc(mixed, 1)
                                yield ins if i == 3 and k < 3 else None

                def finish(mixing):
                    for ins in mixing:
                        if ins is not None:
                            link(ins)

                def step(n):
                    par = n % 2
                    restart()
                    for f in range(FT):
                        m = rows_of(f)
                        dve.wait_ge(sil_up, n * FT + f + 1)
                        wait(dve, act_lo, n * FT + f - 1)
                        nc.vector.scalar_tensor_tensor(prod[0:m, (par * FT + f) % 2, :],
                                                       p_gu[0:m, (par * FT + f) % 2, 1, :], INV,
                                                       sil[0:m, (par * FT + f) % 2, :], ALU.mult,
                                                       ALU.mult).then_inc(prods, 1)
                        if n:
                            if f == 1:
                                mean_square(n - 1, 1 - par)
                                logits(n - 1, 1 - par)
                            if f == 3:
                                x_pre(n - 1, 1 - par)
                        chain_slot(n, f)
                        if f == 7:
                            take_a(n + 1)
                        if f == 9:
                            low_a(n + 1)
                    if n:
                        base_of(n - 1)
                    dve.wait_ge(td_ps, n + 1)
                    wait(dve, td_hi, 2 * n)
                    nc.vector.tensor_tensor(
                        td_f[:].rearrange("p (u b) r -> p u (b r)", b=4),
                        p_a[:, 0:P].rearrange("p (u m) -> p u m", u=T1),
                        mask1[:].rearrange("p b r -> p (b r)").unsqueeze(1).broadcast_to([P, T1, 4 * RANK]),
                        ALU.mult).then_inc(td_up, 1)
                    dve.wait_ge(td_hi, 2 * n + 2)
                    for copy in range(2):
                        nc.vector.tensor_tensor(td_s[:, :, 2 + copy, :], td_f[:], td_s[:, :, 0, :],
                                                ALU.subtract).then_inc(td_lo, 1)
                    chain_slot(n, FT)

                mix_late = {N1 - 2: mixing(0, 2), N1 - 1: mixing(2, GROUPS[0][1])}

                def chain_slot(n, f):
                    k = CHAIN_DOWN if f == FT else CHAIN_F[f]
                    for g, steps in enumerate(CHAIN_STEPS):
                        if n in steps and (f >= 2 or n > steps[0]):
                            advance((g,), k, mix_late[n] if g == 1 else ())
                    if n == N1 - 2 and f == 0:
                        advance((0,), 2 * ROUNDS)
                        gated(GROUPS[0])
                    if n in mix_late and f == FT:
                        finish(mix_late[n])

                restart()
                dve.wait_ge(gate_e, 1)
                dve.wait_ge(eye_up, 2)
                link(nc.vector.tensor_scalar(gsig[:, 1:2], gsig[:, 0:1], 1.0, None, ALU.add))
                link(nc.vector.reciprocal(gsig[:, 2:3], gsig[:, 1:2]))
                link(nc.vector.tensor_scalar(gsig[:, 3:4], gsig[:, 2:3], -1.0, 1.0, ALU.mult, ALU.add))
                link(nc.vector.tensor_scalar(eye[:], eye[:], gsig[:, 3:4], None, ALU.mult))
                take_a(0)
                low_a(0)
                for n in range(N1):
                    step(n)
                restart()
                mean_square(N1 - 1, 1)
                logits(N1 - 1, 1)
                x_pre(N1 - 1, 1)
                advance((1, 2), TAIL_BOTH)
                base_of(N1 - 1)
                advance((1, 2), (6 * (ROUNDS - 1) - issued[1]) // 3)
                gated(GROUPS[1])
                beside = mixing(*GROUPS[1])
                advance((2,), 2 * ROUNDS, beside)
                finish(beside)
                gated(GROUPS[2])
                finish(mixing(*GROUPS[2]))

            @block.tensor
            def _(pe):
                def x_a(n, par):
                    pe.wait_ge(x_lo, n + 1)
                    pe.wait_ge(got_ag, (n + 1) * (B1 * 16))
                    wait(pe, td_up, n - 1)
                    for t in range(T1):
                        for k, (sx, sa) in enumerate(PASSES):
                            for i in range(KT):
                                mm = nc.tensor.matmul(
                                    p_a[:, t * P:(t + 1) * P], xs1[:, par, sx, i, t * P:(t + 1) * P],
                                    ag[:, 4 * t:4 * t + 4, sa, i * 2 * RANK:(i + 1) * 2 * RANK]
                                    .rearrange("p b (a r) -> p a b r", a=2),
                                    start=(k == 0 and i == 0), stop=(k == 2 and i == KT - 1))
                    mm.then_inc(ta_ps, 1)

                def a_rows(n):
                    pe.wait_ge(ta_lo, 2 * n + 2)
                    wait(pe, tdt_sb, n - 1)
                    for u in range(2 * T1):
                        for g in range(2):
                            at = (2 * u + 1 - g) * P
                            mm = nc.tensor.transpose(
                                p_at[:, at:at + P],
                                ta_s[:, 4 * u + 2 * g:4 * u + 2 * g + 2, :, :].rearrange("p b s r -> p (b s r)"),
                                ident16[:])
                    mm.then_inc(tat_ps, 1)

                def gate_up(n, par, f):
                    m = rows_of(f)
                    bank = (par * FT + f) % 2
                    wait(pe, prods, n * FT + f - 1)
                    for tab, w in enumerate((wg, wu)):
                        for k, (sw, sx) in enumerate(PASSES):
                            for i in range(KT):
                                nc.tensor.matmul(p_gu[0:m, bank, tab, :], w[:, sw, i, f * P:f * P + m],
                                                 xs1[:, par, sx, i, :], start=(k == 0 and i == 0),
                                                 stop=(k == 2 and i == KT - 1))
                        for t in range(T1):
                            for g in range(2):
                                at = t * P + g * PAIR
                                col = tab * F + f * P
                                mm = nc.tensor.matmul(
                                    p_gu[0:m, bank, tab, at:at + PAIR],
                                    bg[:, 2 * t + g, col:col + m],
                                    ta_t[:, par, 2 * t + tab, (1 - g) * PAIR:(2 - g) * PAIR],
                                    start=False, stop=True, skip_group_check=True)
                    mm.then_inc(gu_ps, 1)

                def y_transposes(m, par):
                    pe.wait_ge(y_up, 2 * T1 * (m + 1))
                    wait(pe, base_up, m)
                    for t, p in enumerate((p_m1, p_a)):
                        for i in range(KT):
                            mm = nc.tensor.transpose(p[:, i * P:(i + 1) * P], y1[:, par, t, i * P:(i + 1) * P],
                                                     ident32[:])
                    mm.then_inc(yt_ps, 1)

                def project(m):
                    pe.wait_ge(yt_sb, 2 * m + 2)
                    for t in range(T1):
                        for i in range(KT):
                            mm = nc.tensor.matmul(p_m2[:, t * NPROJ:(t + 1) * NPROJ], yT[:, t, i, :], proj[:, i, :],
                                                  start=(i == 0), stop=(i == KT - 1))
                    mm.then_inc(lg_ps, 1)

                def pre_transposes(m):
                    pe.wait_ge(xp_up, m + 1)
                    for t in range(T1):
                        mm = nc.tensor.transpose(p_m2[:, t * P:(t + 1) * P], xpre[:, t, :], ident32[:])
                    mm.then_inc(xp_ps, 1)

                def branch_product(m):
                    pe.wait_ge(xp_sb, m + 1)
                    for t in range(T1):
                        mm = nc.tensor.matmul(p_m2[:, C1 + t * P:C1 + (t + 1) * P], xpre[:, t, :], branch[:],
                                              start=True, stop=True)
                    mm.then_inc(yb_ps, 1)

                def x_back(m, t):
                    if t == 0:
                        pe.wait_ge(xc_up, m + 1)
                    else:
                        pe.wait_ge(yb_sb, m + 1)
                    for i in range(KT):
                        mm = nc.tensor.transpose((p_m1, p_m2)[t][:, i * P:(i + 1) * P],
                                                 xc[:, i, t * P:(t + 1) * P], ident32[:])
                    mm.then_inc(xb_ps, 1)

                def down(n, par):
                    pe.wait_ge(got_ad, (n + 1) * (B1 * 16))
                    pe.wait_ge(ta_up, n + 2)
                    for t in range(T1):
                        for i in range(FT):
                            m = rows_of(i)
                            if t == 0:
                                pe.wait_ge(act_lo, n * FT + i + 1)
                            for k, (sx, sa) in enumerate(PASSES):
                                mm = nc.tensor.matmul(
                                    p_a[:, t * 64:(t + 1) * 64], acts[0:m, sx, i, t * P:(t + 1) * P],
                                    ad[0:m, 4 * t:4 * t + 4, sa, i * RANK:(i + 1) * RANK],
                                    start=(i == 0 and k == 0), stop=(i == FT - 1 and k == 2))
                    mm.then_inc(td_ps, 1)
                    for t in range(T1):
                        if t == 0:
                            wait(pe, y_up, 2 * T1 * n)
                        for i in range(FT):
                            m = rows_of(i)
                            if t == 1 and i == 5:
                                pe.wait_ge(td_lo, 2 * n + 2)
                                pe.wait_ge(tat_sb, n + 2)
                                for u in range(2 * T1):
                                    mm = nc.tensor.transpose(
                                        p_at[:, u * P:(u + 1) * P],
                                        td_s[:, 2 * u:2 * u + 2, :, :].rearrange("p b s r -> p (b s r)"), ident16[:])
                                mm.then_inc(tdt_ps, 1)
                            for k, (sx, sw) in enumerate(PASSES):
                                nc.tensor.matmul(p_y[:, t, :], acts[0:m, sx, i, t * P:(t + 1) * P],
                                                 wd[0:m, sw, i, :], start=(i == 0 and k == 0), stop=False)
                    pe.wait_ge(tdt_sb, n + 1)
                    pe.wait_ge(got_bd, (n + 1) * (B1 * 16))
                    for t in range(T1):
                        for g in range(2):
                            mm = nc.tensor.matmul(p_y[:, t, :], td_t[:, 2 * t + g, :], bd[:, 2 * t + g, :],
                                                  start=False, stop=(g == 1))
                        mm.then_inc(y_ps, 1)

                def step(n, par, first=False):
                    pe.wait_ge(tat_sb, n + 1)
                    pe.wait_ge(got_bg, (n + 1) * (B1 * 16))
                    for f in range(FT):
                        gate_up(n, par, f)
                        if f == 6:
                            x_a(n + 1, 1 - par)
                        if f == FT - 1:
                            a_rows(n + 1)
                        if not first:
                            if f == 0:
                                y_transposes(n - 1, 1 - par)
                            if f == 1:
                                project(n - 1)
                            if f == 4:
                                pre_transposes(n - 1)
                            if f == 5:
                                branch_product(n - 1)
                            if f == 8:
                                x_back(n - 1, 0)
                            if f == FT - 1:
                                x_back(n - 1, 1)
                    down(n, par)

                x_a(0, 0)
                a_rows(0)
                step(0, 0, first=True)
                step(1, 1)
                with pe.Fori(1, N1 // 2) as s:
                    step(2 * s, 0)
                    step(2 * s + 1, 1)
                y_transposes(N1 - 1, 1)
                project(N1 - 1)
                pre_transposes(N1 - 1)
                branch_product(N1 - 1)
                x_back(N1 - 1, 0)
                x_back(N1 - 1, 1)


def kernel(**inputs):
    import numpy as np
    import concourse.bacc as bacc
    from concourse.bass_utils import run_bass_kernel_spmd as run

    def get(name):
        return np.asarray(inputs[name])

    def columns(v):
        return v.reshape(KT, P).T

    def slots_a(t, slots, tiles):
        return t.reshape(slots, tiles, P, -1).transpose(2, 0, 1, 3)

    a_gu = np.stack([get("L1_cond_A_gate")[0], get("L1_cond_A_up")[0]], 1)
    a_gu = slots_a(a_gu.transpose(0, 3, 1, 2), SLOTS1, KT).reshape(P, SLOTS1, -1)
    a_d = np.zeros((SLOTS1, FT * P, RANK), np.float32)
    a_d[:, :F] = get("L1_cond_A_down")[0].transpose(0, 2, 1)
    a_d = slots_a(a_d, SLOTS1, FT).reshape(P, SLOTS1, -1)
    a1 = np.concatenate([a_gu, a_d], 2)
    wd = np.zeros((PIECES * DT_PIECE * P, D), np.float32)
    wd[:F] = get("L1_cond_W_down").T
    rows = [get(n)[0].transpose(0, 2, 1) for n in ("L1_cond_B_gate", "L1_cond_B_up", "L1_cond_B_down")]
    x = get("x").reshape(TOK, D)
    arrays = {
        "xT": x.T,
        "slot0": get("itok_B_0_23").reshape(1, BATCH),
        "slot1": get("itok_B_2_6").reshape(1, BATCH),
        "w0T": get("L0_cond_W").T,
        "b0": columns(get("L0_cond_b")),
        "a0": slots_a(get("L0_cond_lora_As"), SLOTS0, KT).reshape(P, -1),
        "b0t": get("L0_cond_lora_Bs").reshape(SLOTS0 * RANK, D),
        "chan": columns(get("L0_ffn_channel_scale").reshape(D)),
        "qT": get("L0_ffn_qweight").T,
        "perm": columns(get("L0_ffn_q_perm")),
        "scT": get("L0_ffn_scales").T,
        "zrT": get("L0_ffn_zeros").T,
        "fbias": columns(get("L0_ffn_bias")),
        "wgT": get("L1_cond_W_gate").T,
        "wuT": get("L1_cond_W_up").T,
        "wdT": wd,
        "a1": a1.reshape(P, PIECES, -1).transpose(1, 0, 2).reshape(PIECES * P, -1),
        "b1t": np.concatenate(rows, 2).reshape(2 * SLOTS1 * RANK, B1W // 2),
        "proj": np.concatenate([get("L1_ffn_W_res"), get("L1_ffn_W_pre"), get("L1_ffn_W_post")], 0).T,
        "base": np.concatenate([get("L1_ffn_H_res_base").reshape(-1), get("L1_ffn_H_pre_base"),
                                get("L1_ffn_H_post_base")]).reshape(1, NPROJ),
        "gate": get("L1_ffn_gate").reshape(1, 1),
        "branch": get("L1_ffn_W_branch"),
    }
    nc = bacc.Bacc("TRN2", target_bir_lowering=False, num_devices=1)
    arrays = {"in_" + n: np.ascontiguousarray(v) for n, v in arrays.items()}
    aps = {n[3:]: nc.dram_tensor(n, v.shape, mybir.dt.from_np(v.dtype), kind="ExternalInput").ap()
           for n, v in arrays.items()}
    out = nc.dram_tensor("out", (TOK, D), F32, kind="ExternalOutput").ap()
    build(nc, aps, out)
    r = run(nc, [arrays], core_ids=[0])
    return r.results[0]["out"].reshape(BATCH, SEQ, D)
```

```python
from contextlib import ExitStack

import concourse.bass as bass
from concourse import mybir

F32 = mybir.dt.float32
F16 = mybir.dt.float16
I32 = mybir.dt.int32
U32 = mybir.dt.uint32
ALU = mybir.AluOpType
ACT = mybir.ActivationFunctionType
AX = mybir.AxisListType

P = 128
BATCH, SEQ, D = 64, 32, 512
TOK = BATCH * SEQ
KT = D // P
RANK = 16
SLOTS0, SLOTS1 = 32, 16
F = 1376
FT = -(-F // P)
FL = F - (FT - 1) * P
C0 = 512
N0 = TOK // C0
T0 = C0 // P
B0 = C0 // SEQ
G0 = B0 // 2
C1 = 256
N1 = TOK // C1
T1 = C1 // P
B1 = C1 // SEQ
G1 = B1 // 2
SP_A = 12
SP_AG, SP_BG = 3, 2
PAIR = 2 * SEQ
PIECES = 4
DT_PIECE = 3
A1W = KT * 2 * RANK + FT * RANK
GUW = KT * 2 * RANK
B1W = 2 * F + D
GU = 2 * F
NPROJ = 24
ROUNDS = 50
NT = TOK // P
GROUPS = ((0, 4), (4, 10), (10, 16))
CHAIN_STEPS = ((2, 3, 4), (5, 6, 7))
MIX_STEP = 5
LATE_POOL = 3
CHAIN_F = (1, 0, 0, 1, 2, 2, 2, 2, 3, 2, 2)
CHAIN_DOWN = 18
TAIL_BOTH = 12
RMS_EPS = 1.1920929e-07

SCALE = 256.0
INV = 1.0 / SCALE
LORA0 = 2.0 * INV
LORA1 = 0.5 * INV
PASSES = ((0, 0), (1, 0), (0, 1))


def wait(eng, sem, value):
    if not isinstance(value, int) or value > 0:
        eng.wait_ge(sem, value)


def build(nc, a, out):
    ctx = ExitStack()
    with ctx:
        def maker(stack):
            return lambda name, shape, dt: stack.enter_context(nc.sbuf_tensor(name, shape, dt))

        sb = maker(ctx)

        xT = sb("xT", [P, KT, TOK + C1], F32)
        ident32 = sb("ident32", [P, P], F32)
        ident16 = sb("ident16", [P, P], F16)
        mask0 = sb("mask0", [P, 4, RANK], F32)
        mask1 = sb("mask1", [P, 4, RANK], F32)
        slot0 = sb("slot0", [1, BATCH], I32)
        slot1 = sb("slot1", [1, BATCH + B1], I32)
        proj = sb("proj", [P, KT, NPROJ], F32)
        base = sb("base", [P, NPROJ], F32)
        gate = sb("gate", [P, 2], F32)
        branch = sb("branch", [P, P], F32)
        chan = sb("chan", [P, KT], F32)
        b0 = sb("b0", [P, KT], F32)
        b0s = sb("b0s", [P, KT, 2], F16)
        fbias = sb("fbias", [P, KT], F32)
        csum = sb("csum", [P, KT], F32)
        cvec = sb("cvec", [P, KT], F32)
        perm_i = sb("perm_i", [P, KT], I32)
        perm_f = sb("perm_f", [P, KT], F32)
        shift = sb("shift", [P, 1], I32)
        shift4 = sb("shift4", [P, 1], I32)

        setup = ExitStack()
        st = maker(setup)
        q = st("q", [P, KT, D], U32)
        q4 = st("q4", [P, KT, D], U32)
        sc = st("sc", [P, KT, D], F32)
        zr = st("zr", [P, KT, D], F32)
        w_in = st("w_in", [P, KT, D], F32)
        a0_in = st("a0_in", [P, SLOTS0, KT * RANK], F32)
        a0_out = st("a0_out", [P, SLOTS0, 2, KT * RANK], F16)
        b0_in = st("b0_in", [P, KT, D], F32)
        b0_out = st("b0_out", [P, 2, KT, D], F16)
        onehot = st("onehot", [P, KT, D], F16)
        col_i = st("col_i", [P, D], I32)
        setup.close()

        wg = sb("wg", [P, 2, KT, F], F16)
        wu = sb("wu", [P, 2, KT, F], F16)
        wd = sb("wd", [P, 2, PIECES * DT_PIECE, D], F16)

        layer0 = ExitStack()
        l0 = maker(layer0)
        sb_out = l0("sb_out", [P, 2, B1W // 2], F16)
        sa_out = l0("sa_out", [P, SLOTS1 // 4, 2, A1W], F16)
        s_g = l0("s_g", [P, F], F32)
        w0 = l0("w0", [P, 2, KT, D], F16)
        mw = l0("mw", [P, 2, KT, D], F16)
        xs = l0("xs", [P, 2, 2, KT, C0], F16)
        hs = l0("hs", [P, 2, KT, C0], F16)
        o_sb = l0("o_sb", [P, 3, C0], F32)
        a0g = l0("a0g", [P, B0, 2, KT * RANK], F16)
        b0g = l0("b0g", [P, G0, D], F16)
        t0_f = l0("t0_f", [P, T0 * 4, RANK], F32)
        t0_s = l0("t0_s", [P, T0 * 4, 4, RANK], F16)
        t0_t = l0("t0_t", [P, C0], F16)
        wq16 = xs[:, 1]
        s_u = l0("s_u", [P, F], F32)
        s_d = l0("s_d", [P, DT_PIECE, D], F32)
        s_a = l0("s_a", [P, SLOTS1 // 4, A1W], F32)
        s_b = l0("s_b", [P, B1W // 2], F32)
        layer0.close()

        a0_tab = nc.dram_tensor("a0_tab", [SLOTS0, P, 2 * KT * RANK], F16, kind="Internal")
        b0_tab = nc.dram_tensor("b0_tab", [SLOTS0, 2, RANK, D], F16, kind="Internal")
        a1_tab = nc.dram_tensor("a1_tab", [SLOTS1, P, 2 * A1W], F16, kind="Internal")
        b1_tab = nc.dram_tensor("b1_tab", [SLOTS1, 2, RANK, B1W], F16, kind="Internal")

        psum0 = ExitStack()

        def ps(name, shape, dt=F32, stack=psum0):
            return stack.enter_context(nc.psum_tensor(name, shape, dt))

        p_h = ps("p_h", [P, 4, D])
        p_t = ps("p_t", [P, 2 * T0 * 4, RANK])
        p_tt = ps("p_tt", [P, 2 * C0], F16)
        p_o = ps("p_o", [P, 2, D])
        psum0.close()

        with ExitStack() as sems0:
            def sem(name):
                return sems0.enter_context(nc.semaphore(name))

            ld_small, ld_q, ld_w, ld_a0, ld_b0, ld_const = (
                sem(n) for n in "ld_small ld_q ld_w ld_a0 ld_b0 ld_const".split())
            ld_x = [sem(f"ld_x{c}") for c in range(N0)]
            ld_g, ld_u, ld_d, ld_a1, ld_b1 = (sem(n) for n in "ld_g ld_u ld_d ld_a1 ld_b1".split())
            consts, z_ready = sem("consts"), sem("z_ready")
            deq = sem("deq")
            w_hi, w_lo = sem("w_hi"), sem("w_lo")
            m_ps, m_hi, m_lo = sem("m_ps"), sem("m_hi"), sem("m_lo")
            c_ps, c_done = sem("c_ps"), sem("c_done")
            wr_a0, wr_b0, wr_a1, wr_b1, got_a, got_a2, got_b = (
                sem(n) for n in "wr_a0 wr_b0 wr_a1 wr_b1 got_a got_a2 got_b".split())
            x_hi, x_lo, a_ps, t_f, t_hi, t_lo, tt_ps, tt_sb, base_done = (
                sem(n) for n in "x_hi x_lo a_ps t_f t_hi t_lo tt_ps tt_sb base_done".split())
            h_ps, h_hi, h_lo, o_ps, o_up, x1 = (sem(n) for n in "h_ps h_hi h_lo o_ps o_up x1".split())
            s_hi, s_lo = sem("s_hi"), sem("s_lo")

            block = sems0.enter_context(nc.Block())

            def gather_a(eng, c, batches, done):
                wait(eng, a_ps, c)
                for b in range(*batches):
                    s = eng.value_load(slot0[0:1, c * B0 + b:c * B0 + b + 1], min_val=0, max_val=SLOTS0 - 1)
                    eng.dma_start(a0g[:, b, :, :].rearrange("p h n -> p (h n)"),
                                  a0_tab[bass.ds(s, 1)].rearrange("a p n -> (a p) n")).then_inc(done, 16)

            @block.sync
            def _(sp):
                sp.dma_start(perm_i[:], a["perm"]).then_inc(ld_small, 16)
                sp.dma_start(slot0[:], a["slot0"]).then_inc(ld_small, 16)
                sp.dma_start(slot1[:, 0:BATCH], a["slot1"]).then_inc(ld_small, 16)
                sp.dma_start(chan[:], a["chan"]).then_inc(ld_small, 16)
                sp.dma_start(b0[:], a["b0"]).then_inc(ld_small, 16)
                sp.dma_start(fbias[:], a["fbias"]).then_inc(ld_small, 16)
                def load_x(c):
                    sp.dma_start(xT[:, :, c * C0:(c + 1) * C0],
                                 a["xT"].rearrange("(t p) n -> p t n", p=P)[:, :, c * C0:(c + 1) * C0]
                                 ).then_inc(ld_x[c], 16)

                sp.dma_start(a0_in[:], a["a0"].rearrange("p (s n) -> p s n", s=SLOTS0)).then_inc(ld_a0, 16)
                sp.dma_start(w_in[:], a["w0T"].rearrange("(t p) o -> p t o", p=P)).then_inc(ld_w, 16)
                load_x(0)
                sp.dma_start(b0_in[:], a["b0t"].rearrange("(t p) o -> p t o", p=P)).then_inc(ld_b0, 16)
                for t in range(KT):
                    words = a["qT"][t * 16:(t + 1) * 16, :]
                    sp.dma_start(q[:, t, :], words.unsqueeze(1).broadcast_to([16, 8, D])).then_inc(ld_q, 16)
                for table, dst in (("scT", sc), ("zrT", zr)):
                    halves = a[table].rearrange("(t h) o -> h t o", h=2)
                    for h in range(2):
                        sp.dma_start(dst[64 * h:64 * h + 64, :, :],
                                     halves[h].unsqueeze(0).broadcast_to([64, KT, D])).then_inc(ld_q, 16)
                sp.wait_ge(w_lo, 1)
                sp.dma_start(a0_tab.rearrange("s p n -> p s n"),
                             a0_out[:].rearrange("p s h n -> p s (h n)")).then_inc(wr_a0, 16)
                sp.wait_ge(w_lo, 3)
                for t in range(KT):
                    for part in range(2):
                        sp.dma_start(b0_tab[8 * t:8 * t + 8, part], b0_out[:, part, t, :]).then_inc(wr_b0, 16)

                load_x(1)
                sp.wait_ge(ld_small, 6 * 16)
                sp.wait_ge(wr_a0, 16)
                gather_a(sp, 0, (0, SP_A), got_a)
                for c in range(N0):
                    if c + 1 < N0:
                        gather_a(sp, c + 1, (0, SP_A), got_a)
                    if c + 2 < N0:
                        load_x(c + 2)
                    if c == 0:
                        for dst, src in ((proj[:], a["proj"].rearrange("(t p) n -> p t n", p=P)),
                                         (base[:], a["base"].broadcast_to([P, NPROJ])),
                                         (gate[:, 0:1], a["gate"].broadcast_to([P, 1])),
                                         (branch[:], a["branch"])):
                            sp.dma_start(dst, src).then_inc(ld_const, 16)
                sp.wait_ge(wr_a1, N0 * 16)
                sp.wait_ge(wr_b1, N0 * 2 * 16)
                for s, n in ((ld_q, 8), (ld_const, 4), (got_a, N0 * SP_A)):
                    sp.wait_ge(s, n * 16)

            @block.gpsimd
            def _(pool):
                pool.iota(shift4[:], [[0, 1]], base=0, channel_multiplier=4).then_inc(consts, 1)
                pool.iota(col_i[:], [[1, D]], base=0, channel_multiplier=0).then_inc(consts, 1)
                pool.memset(ident32[:], 0.0).then_inc(z_ready, 1)
                pool.memset(mask0[:], LORA0).then_inc(z_ready, 1)
                pool.memset(mask1[:], LORA1).then_inc(z_ready, 1)
                pool.memset(slot1[:, BATCH:BATCH + B1], 0).then_inc(z_ready, 1)
                pool.memset(xT[:, :, TOK:TOK + C1], 0.0).then_inc(z_ready, 1)
                pool.wait_ge(z_ready, 5)
                pool.affine_select(out=ident32[:], in_=ident32[:], compare_op=ALU.not_equal, fill=1.0, base=0,
                                   pattern=[[-1, P]], channel_multiplier=1).then_inc(z_ready, 1)
                for m in (mask0, mask1):
                    pool.affine_select(out=m[:], in_=m[:], compare_op=ALU.is_ge, fill=0.0, base=0,
                                       pattern=[[-SEQ, 4], [0, RANK]], channel_multiplier=1).then_inc(z_ready, 1)
                pool.wait_ge(z_ready, 8)
                pool.tensor_copy(ident16[:], ident32[:]).then_inc(consts, 1)
                for m in (mask0, mask1):
                    pool.affine_select(out=m[:], in_=m[:], compare_op=ALU.is_ge, fill=0.0, base=SEQ - 1,
                                       pattern=[[SEQ, 4], [0, RANK]], channel_multiplier=-1).then_inc(consts, 1)

                def gather_b(c):
                    for b in range(B0):
                        s = pool.value_load(slot0[0:1, bass.ds(c * B0 + b, 1)], min_val=0, max_val=SLOTS0 - 1)
                        if b == 0:
                            wait(pool, h_ps, c * KT)
                        pool.dma_start(b0g[64 * (b % 2):64 * (b % 2) + 64, b // 2, :],
                                     b0_tab[bass.ds(s, 1)].rearrange("a h r n -> a (h r) n")
                                     .broadcast_to([2, 2 * RANK, D])).then_inc(got_b, 16)

                def residual(c):
                    for o in range(KT):
                        pool.wait_ge(o_up, c * KT + o + 1)
                        xo = xT[:, o, c * C0:(c + 1) * C0]
                        pool.tensor_tensor(xo, xo, o_sb[:, (c * KT + o) % 3, :], ALU.add).then_inc(x1, 1)

                pool.wait_ge(ld_small, 6 * 16)
                pool.wait_ge(wr_a0, 16)
                gather_a(pool, 0, (SP_A, B0), got_a2)
                pool.wait_ge(wr_b0, 2 * KT * 16)
                gather_b(0)
                for c in range(N0):
                    if c + 1 < N0:
                        gather_a(pool, c + 1, (SP_A, B0), got_a2)
                        gather_b(c + 1)
                    residual(c)
                pool.wait_ge(got_a2, N0 * (B0 - SP_A) * 16)
                pool.wait_ge(got_b, BATCH * 16)

            @block.scalar
            def _(act):
                def hi(out, in_, done, scale=SCALE):
                    nc.scalar.activation(out, in_, ACT.Identity, scale=scale).then_inc(done, 1)

                def x_high(c):
                    act.wait_ge(ld_x[c], 16)
                    wait(act, base_done, c - 1)
                    hi(xs[:, c % 2, 0], xT[:, :, c * C0:(c + 1) * C0], x_hi, scale=1.0)

                act.wait_ge(ld_a0, 16)
                hi(a0_out[:, :, 0, :], a0_in[:], w_hi)
                act.wait_ge(ld_w, 16)
                hi(w0[:, 0], w_in[:], w_hi)
                x_high(0)
                act.wait_ge(ld_b0, 16)
                hi(b0_out[:, 0], b0_in[:], w_hi)
                act.wait_ge(ld_small, 6 * 16)
                hi(b0s[:, :, 0], b0[:], w_hi)
                act.wait_ge(deq, 5)
                hi(wq16[:, 0], sc[:], w_hi)

                def t_high(c):
                    act.wait_ge(t_f, c + 1)
                    wait(act, tt_ps, c)
                    for copy in range(2):
                        nc.scalar.copy(t0_s[:, :, copy, :], t0_f[:]).then_inc(t_hi, 1)

                def t_rows(c):
                    act.wait_ge(tt_ps, c + 1)
                    wait(act, h_ps, c * KT)
                    nc.scalar.copy(t0_t[:].rearrange("p (t n) -> p t n", t=T0),
                                   p_tt[:].rearrange("p (t n) -> p t n", t=T0)[:, :, 64:64 + P]).then_inc(tt_sb, 1)

                def load_pieces(c):
                    wait(act, s_lo, c * 5)
                    act.dma_start(s_a[:], a["a1"][c * P:(c + 1) * P, :]
                                 .rearrange("p (s n) -> p s n", n=A1W)).then_inc(ld_a1, 16)
                    act.dma_start(s_b[:], a["b1t"][c * P:(c + 1) * P, :]).then_inc(ld_b1, 16)
                    act.dma_start(s_g[:], a["wgT"][c * P:(c + 1) * P, :]).then_inc(ld_g, 16)
                    act.dma_start(s_u[:], a["wuT"][c * P:(c + 1) * P, :]).then_inc(ld_u, 16)
                    act.dma_start(s_d[:], a["wdT"][c * DT_PIECE * P:(c + 1) * DT_PIECE * P, :]
                                 .rearrange("(t p) n -> p t n", p=P)).then_inc(ld_d, 16)

                def store_pieces(c):
                    act.wait_ge(s_lo, c * 5 + 1)
                    act.dma_start(a1_tab[4 * c:4 * c + 4].rearrange("s p n -> p s n"),
                                 sa_out[:].rearrange("p s h n -> p s (h n)")).then_inc(wr_a1, 16)
                    act.wait_ge(s_lo, c * 5 + 2)
                    for part in range(2):
                        act.dma_start(b1_tab[4 * c:4 * c + 4, part].rearrange("s r (k n) -> s (r k) n", k=2),
                                      sb_out[:, part, :]).then_inc(wr_b1, 16)

                def piece(c, k):
                    ready, out, in_ = (
                        (ld_a1, sa_out[:, :, 0, :], s_a[:]),
                        (ld_b1, sb_out[:, 0, :], s_b[:]),
                        (ld_g, wg[:, 0, c:c + 1, :], s_g[:].unsqueeze(1)),
                        (ld_u, wu[:, 0, c:c + 1, :], s_u[:].unsqueeze(1)),
                        (ld_d, wd[:, 0, c * DT_PIECE:(c + 1) * DT_PIECE, :], s_d[:]))[k]
                    act.wait_ge(ready, c * 16 + 16)
                    if k == 0:
                        wait(act, wr_a1, c * 16)
                    if k == 1:
                        wait(act, wr_b1, c * 32)
                    hi(out, in_, s_hi)

                def out_up(c, o):
                    act.wait_ge(o_ps, c * KT + o + 1)
                    wait(act, x1, c * KT + o - 2)
                    nc.scalar.activation(o_sb[:, (c * KT + o) % 3, :], p_o[:, o % 2, :], ACT.Identity,
                                         bias=cvec[:, o:o + 1], scale=INV).then_inc(o_up, 1)

                for o in range(KT):
                    act.wait_ge(m_ps, o + 1)
                    hi(mw[:, 0, o, :], p_o[:, o % 2, :], m_hi, scale=chan[:, o:o + 1])
                x_high(1)
                act.wait_ge(wr_a0, 16)
                act.wait_ge(wr_b0, 2 * KT * 16)
                load_pieces(0)
                act.wait_ge(c_done, 2)
                t_high(0)
                t_rows(0)
                for c in range(N0):
                    for o in range(KT):
                        act.wait_ge(h_ps, c * KT + o + 1)
                        if o == 0:
                            wait(act, o_ps, c * KT)
                        hi(hs[:, 0, o, :], p_h[:, o, :], h_hi, scale=INV)
                    if 0 < c < N0 - 1:
                        t_high(c + 1)
                    piece(c, 0)
                    out_up(c, 0)
                    piece(c, 1)
                    out_up(c, 1)
                    if 0 < c < N0 - 1:
                        t_rows(c + 1)
                    out_up(c, 2)
                    piece(c, 2)
                    out_up(c, 3)
                    store_pieces(c)
                    if c == 0:
                        t_high(1)
                    if c + 2 < N0:
                        x_high(c + 2)
                    if c == 0:
                        t_rows(1)
                    piece(c, 3)
                    piece(c, 4)
                    if c + 1 < N0:
                        load_pieces(c + 1)

            @block.vector
            def _(dve):
                def lo(out, in_, high, done, scale=SCALE):
                    nc.vector.scalar_tensor_tensor(out, in_, scale, high, ALU.mult, ALU.subtract).then_inc(done, 1)

                dve.wait_ge(consts, 2)
                dve.wait_ge(ld_small, 6 * 16)
                nc.vector.tensor_scalar(shift[:], shift4[:], 31, None, ALU.bitwise_and).then_inc(deq, 1)
                nc.vector.tensor_copy(perm_f[:], perm_i[:]).then_inc(deq, 1)
                dve.wait_ge(deq, 2)
                dve.wait_ge(w_hi, 1)
                lo(a0_out[:, :, 1, :], a0_in[:], a0_out[:, :, 0, :], w_lo)
                dve.wait_ge(w_hi, 2)
                lo(w0[:, 1], w_in[:], w0[:, 0], w_lo)

                def x_low(c):
                    dve.wait_ge(x_hi, c + 1)
                    nc.vector.tensor_tensor(xs[:, c % 2, 1], xT[:, :, c * C0:(c + 1) * C0], xs[:, c % 2, 0],
                                            ALU.subtract).then_inc(x_lo, 1)

                x_low(0)
                for t in range(KT):
                    nc.vector.tensor_scalar(onehot[:, t, :], col_i[:], perm_f[:, t:t + 1], None,
                                            ALU.is_equal).then_inc(m_lo, 1)
                dve.wait_ge(w_hi, 3)
                lo(b0_out[:, 1], b0_in[:], b0_out[:, 0], w_lo)
                dve.wait_ge(w_hi, 4)
                lo(b0s[:, :, 1], b0[:], b0s[:, :, 0], w_lo)
                dve.wait_ge(ld_q, 8 * 16)
                nc.vector.tensor_scalar(q4[:], q[:], shift[:, 0:1].bitcast(U32), 15, ALU.logical_shift_right,
                                        ALU.bitwise_and).then_inc(deq, 1)
                dve.wait_ge(deq, 3)
                nc.vector.tensor_tensor(sc[:], q4[:], sc[:], ALU.mult).then_inc(deq, 1)
                dve.wait_ge(deq, 4)
                nc.vector.tensor_tensor(sc[:], sc[:], zr[:], ALU.add).then_inc(deq, 1)
                dve.wait_ge(w_hi, 5)
                dve.wait_ge(deq, 5)
                lo(wq16[:, 1], sc[:], wq16[:, 0], w_lo)
                for o in range(KT):
                    dve.wait_ge(m_hi, o + 1)
                    nc.vector.scalar_tensor_tensor(mw[:, 1, o, :], p_o[:, o % 2, :], chan[:, o:o + 1], mw[:, 0, o, :],
                                                   ALU.mult, ALU.subtract).then_inc(m_lo, 1)
                dve.wait_ge(c_ps, 1)
                nc.vector.tensor_reduce(csum[:], p_t[:, 0:KT, 0:2], AX.X, ALU.add).then_inc(c_done, 1)
                dve.wait_ge(c_done, 1)
                nc.vector.scalar_tensor_tensor(cvec[:], csum[:], INV * INV, fbias[:], ALU.mult,
                                               ALU.add).then_inc(c_done, 1)
                dve.wait_ge(consts, 5)

                def x_a_parts(c):
                    dve.wait_ge(a_ps, c + 1)
                    wait(dve, t_hi, 2 * c)
                    nc.vector.tensor_tensor(
                        t0_f[:].rearrange("p (t b) r -> p t b r", b=4),
                        p_t[:, 0:T0 * 4, :].rearrange("p (t b) r -> p t b r", b=4),
                        mask0[:].unsqueeze(1).broadcast_to([P, T0, 4, RANK]), ALU.mult).then_inc(t_f, 1)
                    dve.wait_ge(t_hi, 2 * c + 2)
                    dve.wait_ge(t_f, c + 1)
                    for copy in range(2):
                        nc.vector.tensor_tensor(t0_s[:, :, 2 + copy, :], t0_f[:], t0_s[:, :, 0, :],
                                                ALU.subtract).then_inc(t_lo, 1)

                def piece(c, k):
                    out, in_, high = (
                        (sa_out[:, :, 1, :], s_a[:], sa_out[:, :, 0, :]),
                        (sb_out[:, 1, :], s_b[:], sb_out[:, 0, :]),
                        (wg[:, 1, c:c + 1, :], s_g[:].unsqueeze(1), wg[:, 0, c:c + 1, :]),
                        (wu[:, 1, c:c + 1, :], s_u[:].unsqueeze(1), wu[:, 0, c:c + 1, :]),
                        (wd[:, 1, c * DT_PIECE:(c + 1) * DT_PIECE, :], s_d[:],
                         wd[:, 0, c * DT_PIECE:(c + 1) * DT_PIECE, :]))[k]
                    dve.wait_ge(s_hi, c * 5 + k + 1)
                    lo(out, in_, high, s_lo)

                x_a_parts(0)
                x_low(1)
                for c in range(N0):
                    for o in range(KT):
                        dve.wait_ge(h_hi, c * KT + o + 1)
                        lo(hs[:, 1, o, :], p_h[:, o, :], hs[:, 0, o, :], h_lo, scale=INV)
                    if 0 < c < N0 - 1:
                        x_a_parts(c + 1)
                    for k in range(3):
                        piece(c, k)
                    if c == 0:
                        x_a_parts(1)
                    if c + 2 < N0:
                        x_low(c + 2)
                    piece(c, 3)
                    piece(c, 4)

            @block.tensor
            def _(pe):
                def x_a(c):
                    pe.wait_ge(x_lo, c + 1)
                    pe.wait_ge(got_a, (c + 1) * SP_A * 16)
                    pe.wait_ge(got_a2, (c + 1) * (B0 - SP_A) * 16)
                    wait(pe, t_f, c)
                    for t in range(T0):
                        for n, (sx, sa) in enumerate(PASSES):
                            for i in range(KT):
                                mm = nc.tensor.matmul(
                                    p_t[:, 4 * t:4 * t + 4, :], xs[:, c % 2, sx, i, t * P:(t + 1) * P],
                                    a0g[:, 4 * t:4 * t + 4, sa, i * RANK:(i + 1) * RANK],
                                    start=(n == 0 and i == 0), stop=(n == 2 and i == KT - 1))
                    mm.then_inc(a_ps, 1)

                def transposes(c):
                    pe.wait_ge(t_lo, 2 * c + 2)
                    wait(pe, tt_sb, c)
                    for t in range(T0):
                        for g in range(2):
                            at = (2 * t + 1 - g) * P
                            mm = nc.tensor.transpose(
                                p_tt[:, at:at + P],
                                t0_s[:, 4 * t + 2 * g:4 * t + 2 * g + 2, :, :].rearrange("p b s r -> p (b s r)"),
                                ident16[:])
                    mm.then_inc(tt_ps, 1)

                def x_w(c, o):
                    wait(pe, h_lo, (c - 1) * KT + o + 1)
                    for n, (sw, sx) in enumerate(PASSES):
                        for i in range(KT):
                            mm = nc.tensor.matmul(p_h[:, o, :], w0[:, sw, i, o * P:(o + 1) * P],
                                                  xs[:, c % 2, sx, i, :],
                                                  start=(n == 0 and i == 0), stop=(n == 2 and i == KT - 1))
                    if o == KT - 1:
                        mm.then_inc(base_done, 1)

                def lora(c, o):
                    if o == 0:
                        pe.wait_ge(tt_sb, c + 1)
                        pe.wait_ge(got_b, (c + 1) * B0 * 16)
                    for g in range(G0):
                        cols = slice(g * PAIR, (g + 1) * PAIR)
                        rows = slice((g ^ 1) * PAIR, ((g ^ 1) + 1) * PAIR)
                        mm = nc.tensor.matmul(p_h[:, o, cols], b0g[:, g, o * P:(o + 1) * P], t0_t[:, rows],
                                              start=False, stop=True, skip_group_check=True)
                    mm.then_inc(h_ps, 1)

                def h_m(c, o):
                    wait(pe, o_up, c * KT + o - 1)
                    for n, (sw, sx) in enumerate(PASSES):
                        for i in range(KT):
                            mm = nc.tensor.matmul(p_o[:, o % 2, :], mw[:, sw, i, o * P:(o + 1) * P], hs[:, sx, i, :],
                                                  start=(n == 0 and i == 0), stop=(n == 2 and i == KT - 1))
                    mm.then_inc(o_ps, 1)

                pe.wait_ge(w_lo, 2)
                pe.wait_ge(x_lo, 1)
                for o in range(KT):
                    x_w(0, o)
                pe.wait_ge(w_lo, 5)
                pe.wait_ge(m_lo, KT)
                for i in range(KT):
                    if i >= 2:
                        pe.wait_ge(m_lo, KT + i - 1)
                    for part in range(2):
                        for t in range(KT):
                            mm = nc.tensor.matmul(p_o[:, i % 2, :], onehot[:, t, i * P:(i + 1) * P],
                                                  wq16[:, part, t, :],
                                                  start=(part == 0 and t == 0), stop=(part == 1 and t == KT - 1))
                    mm.then_inc(m_ps, 1)
                pe.wait_ge(m_lo, 2 * KT)
                for o in range(KT):
                    for part in range(2):
                        for i in range(KT):
                            mm = nc.tensor.matmul(p_t[:, o, 0:2], mw[:, part, i, o * P:(o + 1) * P], b0s[:, i, :],
                                                  start=(part == 0 and i == 0), stop=(part == 1 and i == KT - 1))
                mm.then_inc(c_ps, 1)
                pe.wait_ge(consts, 5)
                pe.wait_ge(c_done, 1)
                x_a(0)
                transposes(0)
                for c in range(N0):
                    for o in range(KT):
                        if c:
                            x_w(c, o)
                        if c == 1 and o == 1:
                            transposes(1)
                        if o:
                            lora(c, o - 1)
                    lora(c, KT - 1)
                    if 0 < c < N0 - 1:
                        x_a(c + 1)
                    pe.wait_ge(h_lo, (c + 1) * KT)
                    for o in range(KT):
                        h_m(c, o)
                        if o == 1 and 0 < c < N0 - 1:
                            transposes(c + 1)
                    if c == 0:
                        x_a(1)

        l1 = maker(ctx)
        xs1 = l1("xs1", [P, 2, 2, KT, C1], F16)
        acts = l1("acts", [P, 2, FT, C1], F16)
        sil = l1("sil", [P, 2, C1], F32)
        prod = l1("prod", [P, 2, C1], F32)
        y1 = l1("y1", [P, 2, T1, D], F32)
        yT = l1("yT", [P, T1, KT, P], F32)
        xc = l1("xc", [P, KT, C1], F32)
        ag = l1("ag", [P, B1, 2, GUW], F16)
        ad = l1("ad", [P, B1, 2, FT * RANK], F16)
        bg = l1("bg", [P, G1, GU], F16)
        bd = l1("bd", [P, G1, D], F16)
        ta_f = l1("ta_f", [P, T1 * 2 * 4, RANK], F32)
        ta_s = l1("ta_s", [P, T1 * 2 * 4, 4, RANK], F16)
        ta_t = l1("ta_t", [P, 2, T1 * 2, P], F16)
        td_f = l1("td_f", [P, T1 * 4, RANK], F32)
        td_s = l1("td_s", [P, T1 * 4, 4, RANK], F16)
        td_t = l1("td_t", [P, T1 * 2, P], F16)
        base_sb = l1("base_sb", [P, T1, D], F32)
        y_in = l1("y_in", [P, 2, D], F32)
        mix_sb = l1("mix_sb", [P, 2, D], F32)
        xpre = l1("xpre", [P, T1, P], F32)
        yb = l1("yb", [P, T1, P], F32)
        ssq = l1("ssq", [P, 2, T1], F32)
        sq_junk = l1("sq_junk", [P, T1, D], F16)
        ms = l1("ms", [P, T1], F32)
        lnms = l1("lnms", [P, T1], F32)
        rs0 = l1("rs0", [P, T1], F32)
        rs1 = l1("rs1", [P, T1], F32)
        rstd = l1("rstd", [P, T1], F32)
        lg = l1("lg", [P, T1 * 6, 4], F32)
        mx = l1("mx", [P, T1 * 6], F32)
        ex = l1("ex", [P, T1 * 6, 4], F32)
        rsum = l1("rsum", [P, T1 * 6], F32)
        rinv = l1("rinv", [P, T1 * 6], F32)
        lnr = l1("lnr", [P, T1 * 4], F32)
        hpp = l1("hpp", [P, T1, 2, 4], F32)
        lu = l1("lu", [P, T1, 4, 4], F32)
        cmax = l1("cmax", [P, T1, 4], F32)
        hr = l1("hr", [P, NT, 4, 4], F32)
        sums = l1("sums", [P, NT, 4], F32)
        inv = l1("inv", [P, NT, 4], F32)
        csums = l1("csums", [P, T1, 4], F32)
        cinv = l1("cinv", [P, T1, 4], F32)
        hg = l1("hg", [P, NT, 16], F32)
        term = y_in
        eye = l1("eye", [P, 16], F32)
        gsig = l1("gsig", [P, 4], F32)

        y_tok = nc.dram_tensor("y_tok", [TOK, D], F32, kind="Internal")
        base_tok = nc.dram_tensor("base_tok", [TOK, D], F32, kind="Internal")

        psum1 = ExitStack()
        p_gu = ps("p_gu", [P, 2, 2, C1], stack=psum1)
        p_y = ps("p_y", [P, T1, D], stack=psum1)
        p_a = ps("p_a", [P, D], stack=psum1)
        p_at = ps("p_at", [P, 2 * D], F16, stack=psum1)
        p_m1 = ps("p_m1", [P, D], stack=psum1)
        p_m2 = ps("p_m2", [P, D], stack=psum1)

        with ExitStack() as sems1:
            def sem(name):
                return sems1.enter_context(nc.semaphore(name))

            got_ag, got_ad, got_bg, got_bd = (sem(n) for n in "got_ag got_ad got_bg got_bd".split())
            got_first_a, got_first_b = sem("got_first_a"), sem("got_first_b")
            x_hi, x_lo = sem("x1_hi"), sem("x1_lo")
            ta_ps, ta_up, ta_hi, ta_lo, tat_ps, tat_sb = (
                sem(n) for n in "ta_ps ta_up ta_hi ta_lo tat_ps tat_sb".split())
            td_ps, td_up, td_hi, td_lo, tdt_ps, tdt_sb = (
                sem(n) for n in "td_ps td_up td_hi td_lo tdt_ps tdt_sb".split())
            gu_ps, sil_up, prods, act_hi, act_lo = (sem(n) for n in "gu_ps sil_up prods act_hi act_lo".split())
            y_ps, y_up, yt_ps, yt_sb, lg_ps = (sem(n) for n in "y_ps y_up yt_ps yt_sb lg_ps".split())
            to_act, from_act, chain = (sem(n) for n in "to_act from_act chain".split())
            round_step = [sem(f"round_step{h}") for h in range(2 * len(GROUPS))]
            xp_up, xp_ps, xp_sb, yb_ps, yb_sb = (sem(n) for n in "xp_up xp_ps xp_sb yb_ps yb_sb".split())
            xb_ps, xc_up, mixed = (sem(n) for n in "xb_ps xc_up mixed".split())
            y_kept = [sem(f"y_kept{p}") for p in range(2)]
            base_up, base_kept = sem("base_up"), sem("base_kept")
            mix_in = [sem(f"mix_in{b}") for b in range(2)]
            stored = [sem(f"stored{b}") for b in range(2)]
            tail_in = [sem(f"tail_in{g}") for g in range(2)]
            tail_out, hg_up, term_up, term_used = (sem(n) for n in "tail_out hg_up term_up term_used".split())
            gate_e, eye_up = sem("gate_e"), sem("eye_up")

            block = sems1.enter_context(nc.Block())

            def rows_of(f):
                return P if f < FT - 1 else FL


            def tail_y(t):
                t = (t - GROUPS[1][0]) % 8
                return xT[:, t // 4, t % 4 * D:(t % 4 + 1) * D]

            def tail_mix(t):
                t = (t - GROUPS[1][0]) % 8
                return xT[:, 2 + t // 4, t % 4 * D:(t % 4 + 1) * D]

            late_tiles = [*range(*GROUPS[1]), *range(GROUPS[2][1] - LATE_POOL, GROUPS[2][1])]

            def gather(eng, n, tables, pairs=(0, G1)):
                with eng.Fori(*pairs) as g:
                    for b in range(2):
                        s = eng.value_load(slot1[0:1, bass.ds(2 * g + (n * B1 + b), 1)],
                                           min_val=0, max_val=SLOTS1 - 1)
                        for dst, table, cols, done in tables:
                            eng.dma_start(dst(g, b), table(s, cols)).then_inc(done, 16)

            def slot_a(s, cols):
                return (a1_tab[bass.ds(s, 1)].rearrange("a p (h n) -> (a p) h n", h=2)[:, :, cols])

            def slot_b(s, cols):
                rows = b1_tab[bass.ds(s, 1)].rearrange("a h r n -> a (h r) n")[:, :, cols]
                return rows.broadcast_to([2, 2 * RANK, cols.stop - cols.start])

            def pair_rows(dst):
                return lambda g, b: dst[64 * b:64 * b + 64, bass.ds(g, 1), :].rearrange("p g n -> p (g n)")

            def batch(dst):
                return lambda g, b: dst[:, bass.ds(2 * g + b, 1), :, :].rearrange("p g h n -> p (g h) n")

            table_ag = (batch(ag), slot_a, slice(0, GUW), got_ag)
            table_ad = (batch(ad), slot_a, slice(GUW, A1W), got_ad)
            table_bg = (pair_rows(bg), slot_b, slice(0, GU), got_bg)
            table_bd = (pair_rows(bd), slot_b, slice(GU, B1W), got_bd)

            @block.sync
            def _(sp):
                def gather_ag(n):
                    wait(sp, ta_ps, n)
                    gather(sp, n, (table_ag,))

                def gather_down(n):
                    wait(sp, td_ps, n)
                    wait(sp, y_ps, n * T1)
                    gather(sp, n, (table_ad, table_bd))

                def gather_bg(n):
                    wait(sp, gu_ps, n * FT)
                    gather(sp, n, (table_bg,))

                def keep_y(n):
                    sp.wait_ge(y_up, 2 * T1 * (n + 1))
                    for t in range(T1):
                        sp.dma_start(y_tok[(n * T1 + t) * P:(n * T1 + t + 1) * P, :],
                                     y1[:, n % 2, t, :]).then_inc(y_kept[n % 2], 16)

                def keep_base(n):
                    sp.wait_ge(base_up, n + 1)
                    for t in range(T1):
                        sp.dma_start(base_tok[(n * T1 + t) * P:(n * T1 + t + 1) * P, :],
                                     base_sb[:, t, :]).then_inc(base_kept, 16)

                def mix_load(t):
                    b = t % 2
                    wait(sp, stored[b], t // 2 * 16)
                    sp.dma_start(y_in[:, b, :], y_tok[t * P:(t + 1) * P, :]).then_inc(mix_in[b], 16)
                    sp.dma_start(mix_sb[:, b, :], base_tok[t * P:(t + 1) * P, :]).then_inc(mix_in[b], 16)

                def mix_first():
                    in_dram(GROUPS[0][1])
                    mix_load(0)
                    mix_load(1)

                def mix_next(t):
                    sp.wait_ge(mixed, t + 1)
                    sp.dma_start(out[t * P:(t + 1) * P, :], mix_sb[:, t % 2, :]).then_inc(stored[t % 2], 16)
                    if t + 2 < GROUPS[0][1]:
                        mix_load(t + 2)

                def in_dram(end):
                    for p in range(2):
                        steps = len(range(p, -(-end // T1), 2))
                        sp.wait_ge(y_kept[p], steps * T1 * 16)
                    sp.wait_ge(base_kept, end * 16)

                def tail_load(first, end, done):
                    for t in range(first, end):
                        sp.dma_start(tail_y(t), y_tok[t * P:(t + 1) * P, :]).then_inc(done, 16)
                        sp.dma_start(tail_mix(t), base_tok[t * P:(t + 1) * P, :]).then_inc(done, 16)

                def tail_store(t, by, count):
                    sp.wait_ge(by, count)
                    sp.dma_start(out[t * P:(t + 1) * P, :], tail_mix(t)).then_inc(tail_out, 16)

                gather(sp, 0, (table_ag,), (0, SP_AG))
                gather(sp, 0, (table_bg,), (0, SP_BG))
                for n in range(N1):
                    if n:
                        keep_y(n - 1)
                    if n == MIX_STEP:
                        mix_first()
                    if n > MIX_STEP:
                        mix_next(2 * (n - 1 - MIX_STEP))
                        mix_next(2 * (n - 1 - MIX_STEP) + 1)
                    gather_ag(n + 1)
                    gather_down(n)
                    if n + 1 < N1:
                        gather_bg(n + 1)
                    if n:
                        keep_base(n - 1)
                keep_y(N1 - 1)
                (first, end), (_, last) = GROUPS[1:]
                sp.wait_ge(xc_up, N1)
                sp.wait_ge(x_hi, N1)
                sp.wait_ge(x_lo, N1)
                in_dram(end)
                tail_load(first, end, tail_in[0])
                for t in range(first, end):
                    tail_store(t, term_used, 4 * (t - first + 1))
                keep_base(N1 - 1)
                in_dram(last)
                sp.wait_ge(tail_out, (end - first) * 16)
                tail_load(end, last, tail_in[1])
                split = last - LATE_POOL
                for n in range(max(split - end, LATE_POOL)):
                    if n < split - end:
                        tail_store(end + n, mixed, GROUPS[0][1] + n + 1)
                    if n < LATE_POOL:
                        tail_store(split + n, term_used, 4 * (end - first + n + 1))
                sp.wait_ge(tail_out, (last - first) * 16)
                sp.wait_ge(got_ag, N1 * B1 * 16 + SP_AG * 32)
                for b in range(2):
                    sp.wait_ge(stored[b], GROUPS[0][1] // 2 * 16)

            @block.gpsimd
            def _(pool):
                gather(pool, 0, (table_ag[:3] + (got_first_a,),), (SP_AG, G1))
                gather(pool, 0, (table_bg[:3] + (got_first_b,),), (SP_BG, G1))
                pool.memset(eye[:], 0.0).then_inc(eye_up, 1)
                pool.wait_ge(eye_up, 1)
                pool.affine_select(out=eye[:].rearrange("p (i j) -> p i j", j=4),
                                   in_=eye[:].rearrange("p (i j) -> p i j", j=4), compare_op=ALU.not_equal,
                                   fill=1.0, base=0, pattern=[[1, 4], [-1, 4]],
                                   channel_multiplier=0).then_inc(eye_up, 1)

                def x_low(n, par):
                    pool.wait_ge(x_hi, n + 1)
                    pool.tensor_tensor(xs1[:, par, 1], xT[:, :, bass.ds(n * C1, C1)], xs1[:, par, 0],
                                       ALU.subtract).then_inc(x_lo, 1)

                def keep_x(n):
                    pool.tensor_copy(xc[:], xT[:, :, bass.ds(n * C1, C1)]).then_inc(xc_up, 1)

                def step(n, par, first=False, second=False):
                    for f in range(FT):
                        m = rows_of(f)
                        if f == 1 and not (first or second):
                            pool.wait_ge(xb_ps, (n - 1) * T1)
                        pool.wait_ge(act_hi, n * FT + f + 1)
                        pool.tensor_tensor(acts[0:m, 1, f, :], prod[0:m, (par * FT + f) % 2, :], acts[0:m, 0, f, :],
                                           ALU.subtract).then_inc(act_lo, 1)
                        if f == 3:
                            x_low(n + 1, 1 - par)
                        if f == 1 and not first:
                            keep_x(n - 1)

                pool.wait_ge(got_first_a, (G1 - SP_AG) * 32)
                pool.wait_ge(got_first_b, (G1 - SP_BG) * 32)
                step(0, 0, first=True)
                step(1, 1, second=True)
                with pool.Fori(1, N1 // 2) as s:
                    step(2 * s, 0)
                    step(2 * s + 1, 1)
                pool.wait_ge(xb_ps, (N1 - 1) * T1)
                keep_x(N1 - 1)
                for n, t in enumerate(late_tiles):
                    for k in range(4):
                        pool.wait_ge(term_up, n * 4 + k + 1)
                        if n or k:
                            pool.wait_ge(term_used, n * 4 + k)
                        pool.tensor_tensor(tail_mix(t), tail_mix(t), term[:, k % 2, :],
                                           ALU.add).then_inc(term_used, 1)

            @block.scalar
            def _(act):
                def split_x(n, par):
                    nc.scalar.copy(xs1[:, par, 0], xT[:, :, bass.ds(n * C1, C1)]).then_inc(x_hi, 1)

                def a_high(n):
                    act.wait_ge(ta_up, n + 1)
                    for copy in range(2):
                        if copy == 0:
                            wait(act, tat_ps, n)
                        nc.scalar.copy(ta_s[:, :, copy, :], ta_f[:]).then_inc(ta_hi, 1)

                def a_rows(n, par):
                    act.wait_ge(tat_ps, n + 1)
                    nc.scalar.copy(ta_t[:, par], p_at[:].rearrange("p (u n) -> p u n", u=2 * T1)
                                   [:, :, 64:64 + P]).then_inc(tat_sb, 1)

                def high(n, par, f):
                    m = rows_of(f)
                    act.wait_ge(prods, n * FT + f + 1)
                    if f == 0:
                        wait(act, y_ps, n * T1)
                    nc.scalar.copy(acts[0:m, 0, f, :], prod[0:m, (par * FT + f) % 2, :]).then_inc(act_hi, 1)

                def y_transposed(n):
                    act.wait_ge(yt_ps, n + 1)
                    wait(act, lg_ps, n)
                    for t, p in enumerate((p_m1, p_a)):
                        nc.scalar.copy(yT[:, t].rearrange("p k n -> p (k n)"), p[:]).then_inc(yt_sb, 1)

                def root(n):
                    act.wait_ge(to_act, 4 * n + 1)
                    nc.scalar.activation(lnms[:], ms[:], ACT.Ln).then_inc(from_act, 1)
                    act.wait_ge(from_act, 5 * n + 1)
                    nc.scalar.activation(rs0[:], lnms[:], ACT.Exp, scale=-0.5).then_inc(from_act, 1)

                def exps(n):
                    act.wait_ge(to_act, 4 * n + 2)
                    v = ex[:].rearrange("p (t k) j -> p t (k j)", t=T1)
                    w = lg[:].rearrange("p (t k) j -> p t (k j)", t=T1)
                    nc.scalar.activation(v[:, :, 0:16], w[:, :, 0:16], ACT.Exp, scale=10.0)
                    nc.scalar.activation(v[:, :, 16:24], w[:, :, 16:24], ACT.Exp).then_inc(from_act, 1)
                    act.wait_ge(to_act, 4 * n + 3)
                    nc.scalar.activation(lnr[:].rearrange("p (t k) -> p t k", t=T1),
                                         rsum[:].rearrange("p (t k) -> p t k", t=T1)[:, :, 0:4],
                                         ACT.Ln).then_inc(from_act, 1)
                    act.wait_ge(to_act, 4 * n + 4)
                    nc.scalar.activation(ex[:].rearrange("p (t k) j -> p t (k j)", t=T1)[:, :, 0:16],
                                         lu[:].rearrange("p t i j -> p t (i j)"), ACT.Exp).then_inc(from_act, 1)

                def x_pre_out(n):
                    act.wait_ge(xp_ps, n + 1)
                    wait(act, yb_ps, n)
                    nc.scalar.copy(xpre[:].rearrange("p t c -> p (t c)"), p_m2[:, 0:C1]).then_inc(xp_sb, 1)

                def y_out(n):
                    act.wait_ge(yb_ps, n + 1)
                    wait(act, base_up, n)
                    nc.scalar.copy(yb[:].rearrange("p t c -> p (t c)"), p_m2[:, C1:2 * C1]).then_inc(yb_sb, 1)

                def step(n, par, first=False):
                    for f in range(FT):
                        m = rows_of(f)
                        act.wait_ge(gu_ps, n * FT + f + 1)
                        wait(act, prods, n * FT + f - 1)
                        nc.scalar.activation(sil[0:m, (par * FT + f) % 2, :],
                                             p_gu[0:m, (par * FT + f) % 2, 0, :], ACT.Silu, scale=INV).then_inc(sil_up, 1)
                        if f:
                            high(n, par, f - 1)
                        if not first:
                            if f == 0:
                                y_transposed(n - 1)
                            if f == 1:
                                act.preload_act_table_set("natural_log_exp_and_others")
                                root(n - 1)
                                exps(n - 1)
                                act.preload_act_table_set("silu_and_others")
                            if f == 6:
                                x_pre_out(n - 1)
                            if f == 8:
                                y_out(n - 1)
                        if f == 2:
                            split_x(n + 1, 1 - par)
                        if f == 8:
                            a_high(n + 1)
                    high(n, par, FT - 1)
                    a_rows(n + 1, 1 - par)
                    act.wait_ge(td_up, n + 1)
                    for copy in range(2):
                        if copy == 0:
                            wait(act, tdt_ps, n)
                        nc.scalar.copy(td_s[:, :, copy, :], td_f[:]).then_inc(td_hi, 1)
                    act.wait_ge(tdt_ps, n + 1)
                    nc.scalar.copy(td_t[:].rearrange("p u n -> p (u n)"), p_at[:, 0:D]).then_inc(tdt_sb, 1)
                    for t in range(T1):
                        act.wait_ge(y_ps, n * T1 + t + 1)
                        if t == 0:
                            wait(act, y_up, 2 * T1 * n)
                            wait(act, y_kept[par], (n - par) * T1 * 8)
                        nc.scalar.activation(y1[:, par, t, :], p_y[:, t, :], ACT.Identity, scale=INV).then_inc(y_up, 1)
                        nc.scalar.activation(sq_junk[:, t, :], p_y[:, t, :], ACT.Square, scale=INV,
                                             accum_out=ssq[:, par, t:t + 1]).then_inc(y_up, 1)

                nc.scalar.activation(gsig[:, 0:1], gate[:, 0:1], ACT.Exp, scale=-1.0).then_inc(gate_e, 1)
                split_x(0, 0)
                a_high(0)
                a_rows(0, 0)
                step(0, 0, first=True)
                step(1, 1)
                with act.Fori(1, N1 // 2) as s:
                    step(2 * s, 0)
                    step(2 * s + 1, 1)
                act.preload_act_table_set("natural_log_exp_and_others")
                root(N1 - 1)
                y_transposed(N1 - 1)
                exps(N1 - 1)
                x_pre_out(N1 - 1)
                y_out(N1 - 1)
                for n, t in enumerate(late_tiles):
                    late = t >= GROUPS[2][0]
                    act.wait_ge(hg_up, 2 + late)
                    act.wait_ge(tail_in[late], (GROUPS[1 + late][1] - GROUPS[1 + late][0]) * 32)
                    for k in range(4):
                        wait(act, term_used, n * 4 + k - 1)
                        for i in range(4):
                            last = nc.scalar.activation(
                                term[:, k % 2, i * P:(i + 1) * P], tail_y(t)[:, k * P:(k + 1) * P], ACT.Identity,
                                scale=hg[:, t, 4 * i + k:4 * i + k + 1])
                        last.then_inc(term_up, 1)

            @block.vector
            def _(dve):
                count = [0]

                def link(ins):
                    count[0] += 1
                    ins.then_inc(chain, 1)
                    dve.wait_ge(chain, count[0])

                def restart():
                    dve.sem_clear(chain)
                    count[0] = 0

                def take_a(n):
                    dve.wait_ge(ta_ps, n + 1)
                    wait(dve, ta_hi, 2 * n)
                    nc.vector.tensor_tensor(
                        ta_f[:].rearrange("p (u b) r -> p u (b r)", b=4),
                        p_a[:, 0:C1].rearrange("p (u m) -> p u m", u=2 * T1),
                        mask1[:].rearrange("p b r -> p (b r)").unsqueeze(1).broadcast_to([P, 2 * T1, 4 * RANK]),
                        ALU.mult).then_inc(ta_up, 1)

                def low_a(n):
                    dve.wait_ge(ta_hi, 2 * n + 2)
                    for copy in range(2):
                        nc.vector.tensor_tensor(ta_s[:, :, 2 + copy, :], ta_f[:], ta_s[:, :, 0, :],
                                                ALU.subtract).then_inc(ta_lo, 1)

                def logits(m, par):
                    link(nc.vector.tensor_scalar(rs1[:], rs0[:], 1.0, None, ALU.mult))
                    link(nc.vector.tensor_tensor(rs1[:], rs0[:], rs0[:], ALU.mult))
                    link(nc.vector.tensor_tensor(rs1[:], rs1[:], ms[:], ALU.mult))
                    link(nc.vector.tensor_scalar(rs1[:], rs1[:], -0.5, 1.5, ALU.mult, ALU.add))
                    link(nc.vector.tensor_tensor(rstd[:], rs0[:], rs1[:], ALU.mult))
                    dve.wait_ge(lg_ps, m + 1)
                    for t in range(T1):
                        last = nc.vector.scalar_tensor_tensor(
                            lg[:].rearrange("p (t k) j -> p t (k j)", t=T1)[:, t, :],
                            p_m2[:, t * NPROJ:(t + 1) * NPROJ], rstd[:, t:t + 1], base[:], ALU.mult, ALU.add)
                    link(last)
                    link(nc.vector.tensor_reduce(mx[:], lg[:], AX.X, ALU.max))
                    nc.vector.tensor_tensor(lg[:], lg[:], mx[:].unsqueeze(2).broadcast_to([P, T1 * 6, 4]),
                                            ALU.subtract).then_inc(to_act, 1)
                    dve.wait_ge(from_act, 5 * m + 3)
                    nc.vector.tensor_reduce(rsum[:], ex[:], AX.X, ALU.add).then_inc(to_act, 1)
                    dve.wait_ge(to_act, 4 * m + 3)
                    link(nc.vector.reciprocal(rinv[:], rsum[:]))
                    link(nc.vector.tensor_tensor(
                        hpp[:], ex[:].rearrange("p (t k) j -> p t k j", t=T1)[:, :, 4:6, :],
                        rinv[:].rearrange("p (t k) -> p t k", t=T1)[:, :, 4:6].unsqueeze(3)
                        .broadcast_to([P, T1, 2, 4]), ALU.mult))
                    dve.wait_ge(from_act, 5 * m + 4)
                    for t in range(T1):
                        last = nc.vector.scalar_tensor_tensor(
                            lu[:, t], lg[:, 6 * t:6 * t + 4, :], 10.0,
                            lnr[:, 4 * t:4 * t + 4].unsqueeze(2).broadcast_to([P, 4, 4]), ALU.mult, ALU.subtract)
                    link(last)
                    link(nc.vector.tensor_reduce(cmax[:], lu[:].rearrange("p t i j -> p t j i"), AX.X, ALU.max))
                    nc.vector.tensor_tensor(lu[:], lu[:], cmax[:].unsqueeze(2).broadcast_to([P, T1, 4, 4]),
                                            ALU.subtract).then_inc(to_act, 1)
                    dve.wait_ge(from_act, 5 * m + 5)
                    e2 = ex[:].rearrange("p (t k) j -> p t k j", t=T1)[:, :, 0:4, :]
                    link(nc.vector.tensor_reduce(csums[:], e2.rearrange("p t i j -> p t j i"), AX.X, ALU.add))
                    link(nc.vector.reciprocal(cinv[:], csums[:]))
                    link(nc.vector.tensor_tensor(hr[:, m * T1:(m + 1) * T1], e2,
                                                 cinv[:].unsqueeze(2).broadcast_to([P, T1, 4, 4]), ALU.mult))

                def mean_square(m, par):
                    dve.wait_ge(y_up, 2 * T1 * (m + 1))
                    nc.vector.tensor_scalar(ms[:], ssq[:, par, :], 1.0 / D, RMS_EPS, ALU.mult,
                                            ALU.add).then_inc(to_act, 1)
                    dve.wait_ge(from_act, 5 * m + 2)

                def half_rounds(group):
                    tiles = slice(*group)
                    h = hr[:, tiles]
                    shape = [P, group[1] - group[0], 4, 4]
                    for r in range(2 * (ROUNDS - 1)):
                        rows = r % 2 == 0
                        yield nc.vector.tensor_reduce(
                            sums[:, tiles], h if rows else h.rearrange("p t i j -> p t j i"), AX.X, ALU.add)
                        yield nc.vector.reciprocal(inv[:, tiles], sums[:, tiles])
                        yield nc.vector.tensor_tensor(
                            h, h, inv[:, tiles].unsqueeze(3 if rows else 2).broadcast_to(shape), ALU.mult)

                halves = [half for a, e in GROUPS for half in ((a, (a + e) // 2), ((a + e) // 2, e))]
                rounds = [half_rounds(half) for half in halves]
                issued = [0] * len(halves)
                whole = 6 * (ROUNDS - 1)

                def advance(groups, k, beside=()):
                    which = [h for g in groups for h in (2 * g, 2 * g + 1) if issued[h] < whole]
                    for _ in range(min(3 * k, whole - min((issued[h] for h in which), default=whole))):
                        for h in which:
                            if issued[h]:
                                dve.wait_ge(round_step[h], issued[h])
                            next(rounds[h]).then_inc(round_step[h], 1)
                            issued[h] += 1
                        next(iter(beside), None)
                    for h in which:
                        dve.wait_ge(round_step[h], issued[h])

                def pre_streams(m, par):
                    wait(dve, yb_ps, m)
                    for k in range(4):
                        for t in range(T1):
                            s_k = y1[:, par, t, k * P:(k + 1) * P]
                            if k == 0:
                                ins = nc.vector.tensor_scalar(xpre[:, t, :], s_k, hpp[:, t, 0, 0:1], None, ALU.mult)
                            else:
                                ins = nc.vector.scalar_tensor_tensor(xpre[:, t, :], s_k, hpp[:, t, 0, k:k + 1],
                                                                     xpre[:, t, :], ALU.mult, ALU.add)
                            if k == 3 and t == T1 - 1:
                                ins.then_inc(xp_up, 1)
                            yield ins if k < 3 and t == T1 - 1 else None

                def x_pre(m, par):
                    finish(pre_streams(m, par))

                def base_of(m):
                    dve.wait_ge(yb_sb, m + 1)
                    dve.wait_ge(xb_ps, m * T1 + T1)
                    wait(dve, base_kept, m * T1 * 16)
                    for t, back in enumerate((p_m1, p_m2)):
                        for i in range(4):
                            last = nc.vector.scalar_tensor_tensor(
                                base_sb[:, t, i * P:(i + 1) * P], yb[:, t, :], hpp[:, t, 1, i:i + 1],
                                back[:, i * P:(i + 1) * P], ALU.mult, ALU.add)
                    last.then_inc(base_up, 1)

                def gated(group):
                    n = group[1] - group[0]
                    nc.vector.scalar_tensor_tensor(
                        hg[:, slice(*group)], hr[:, slice(*group)].rearrange("p t i j -> p t (i j)"), gsig[:, 2:3],
                        eye[:].unsqueeze(1).broadcast_to([P, n, 16]), ALU.mult, ALU.add).then_inc(hg_up, 1)
                    dve.wait_ge(hg_up, GROUPS.index(group) + 1)

                def mixing(tiles, place):
                    for t in tiles:
                        y_t, mix_t = place(t)
                        for k in range(4):
                            for i in range(4):
                                o = mix_t[:, i * P:(i + 1) * P]
                                ins = nc.vector.scalar_tensor_tensor(
                                    o, y_t[:, k * P:(k + 1) * P], hg[:, t, 4 * i + k:4 * i + k + 1], o,
                                    ALU.mult, ALU.add)
                                if k == 3 and i == 3:
                                    ins.then_inc(mixed, 1)
                                yield ins if i == 3 and k < 3 else None

                def buffered(t):
                    dve.wait_ge(mix_in[t % 2], (t // 2 + 1) * 32)
                    return y_in[:, t % 2, :], mix_sb[:, t % 2, :]

                def in_tail(t):
                    return tail_y(t), tail_mix(t)

                def finish(turns):
                    for ins in turns:
                        if ins is not None:
                            link(ins)

                def step(n):
                    par = n % 2
                    restart()
                    for f in range(FT):
                        m = rows_of(f)
                        dve.wait_ge(sil_up, n * FT + f + 1)
                        wait(dve, act_lo, n * FT + f - 1)
                        nc.vector.scalar_tensor_tensor(prod[0:m, (par * FT + f) % 2, :],
                                                       p_gu[0:m, (par * FT + f) % 2, 1, :], INV,
                                                       sil[0:m, (par * FT + f) % 2, :], ALU.mult,
                                                       ALU.mult).then_inc(prods, 1)
                        if n:
                            if f == 1:
                                mean_square(n - 1, 1 - par)
                                logits(n - 1, 1 - par)
                            if f == 3:
                                x_pre(n - 1, 1 - par)
                        chain_slot(n, f)
                        if f == 7:
                            take_a(n + 1)
                        if f == 9:
                            low_a(n + 1)
                    if n:
                        base_of(n - 1)
                    dve.wait_ge(td_ps, n + 1)
                    wait(dve, td_hi, 2 * n)
                    nc.vector.tensor_tensor(
                        td_f[:].rearrange("p (u b) r -> p u (b r)", b=4),
                        p_a[:, 0:P].rearrange("p (u m) -> p u m", u=T1),
                        mask1[:].rearrange("p b r -> p (b r)").unsqueeze(1).broadcast_to([P, T1, 4 * RANK]),
                        ALU.mult).then_inc(td_up, 1)
                    dve.wait_ge(td_hi, 2 * n + 2)
                    for copy in range(2):
                        nc.vector.tensor_tensor(td_s[:, :, 2 + copy, :], td_f[:], td_s[:, :, 0, :],
                                                ALU.subtract).then_inc(td_lo, 1)
                    chain_slot(n, FT)

                beside_step = {MIX_STEP + n: mixing((2 * n, 2 * n + 1), buffered)
                               for n in range(GROUPS[0][1] // 2)}

                def chain_slot(n, f):
                    if n == MIX_STEP and f == 0:
                        advance((0,), 2 * ROUNDS)
                        gated(GROUPS[0])
                    k = CHAIN_DOWN if f == FT else CHAIN_F[f]
                    for g, steps in enumerate(CHAIN_STEPS):
                        if n in steps and (f >= 2 or n > steps[0]):
                            advance((g,), k, beside_step.get(n, ()))
                    if n in beside_step and f == FT:
                        finish(beside_step[n])

                dve.wait_ge(x_hi, 1)
                nc.vector.tensor_tensor(xs1[:, 0, 1], xT[:, :, 0:C1], xs1[:, 0, 0], ALU.subtract).then_inc(x_lo, 1)
                take_a(0)
                low_a(0)
                restart()
                dve.wait_ge(gate_e, 1)
                dve.wait_ge(eye_up, 2)
                link(nc.vector.tensor_scalar(gsig[:, 1:2], gsig[:, 0:1], 1.0, None, ALU.add))
                link(nc.vector.reciprocal(gsig[:, 2:3], gsig[:, 1:2]))
                link(nc.vector.tensor_scalar(gsig[:, 3:4], gsig[:, 2:3], -1.0, 1.0, ALU.mult, ALU.add))
                link(nc.vector.tensor_scalar(eye[:], eye[:], gsig[:, 3:4], None, ALU.mult))
                for n in range(N1):
                    step(n)
                restart()
                mean_square(N1 - 1, 1)
                logits(N1 - 1, 1)
                advance((1, 2), TAIL_BOTH, pre_streams(N1 - 1, 1))
                base_of(N1 - 1)
                advance((1, 2), (whole - issued[2]) // 3)
                gated(GROUPS[1])
                advance((2,), 2 * ROUNDS)
                gated(GROUPS[2])
                dve.wait_ge(tail_in[1], (GROUPS[2][1] - GROUPS[2][0]) * 32)
                finish(mixing(range(GROUPS[2][0], GROUPS[2][1] - LATE_POOL), in_tail))

            @block.tensor
            def _(pe):
                def x_a(n, par):
                    pe.wait_ge(x_lo, n + 1)
                    pe.wait_ge(got_ag, n * (B1 * 16) + SP_AG * 32)
                    wait(pe, td_up, n - 1)
                    for t in range(T1):
                        for k, (sx, sa) in enumerate(PASSES):
                            for i in range(KT):
                                mm = nc.tensor.matmul(
                                    p_a[:, t * P:(t + 1) * P], xs1[:, par, sx, i, t * P:(t + 1) * P],
                                    ag[:, 4 * t:4 * t + 4, sa, i * 2 * RANK:(i + 1) * 2 * RANK]
                                    .rearrange("p b (a r) -> p a b r", a=2),
                                    start=(k == 0 and i == 0), stop=(k == 2 and i == KT - 1))
                    mm.then_inc(ta_ps, 1)

                def a_rows(n):
                    pe.wait_ge(ta_lo, 2 * n + 2)
                    wait(pe, tdt_sb, n - 1)
                    for u in range(2 * T1):
                        for g in range(2):
                            at = (2 * u + 1 - g) * P
                            mm = nc.tensor.transpose(
                                p_at[:, at:at + P],
                                ta_s[:, 4 * u + 2 * g:4 * u + 2 * g + 2, :, :].rearrange("p b s r -> p (b s r)"),
                                ident16[:])
                    mm.then_inc(tat_ps, 1)

                def gate_up(n, par, f):
                    m = rows_of(f)
                    bank = (par * FT + f) % 2
                    wait(pe, prods, n * FT + f - 1)
                    for tab, w in enumerate((wg, wu)):
                        for k, (sw, sx) in enumerate(PASSES):
                            for i in range(KT):
                                nc.tensor.matmul(p_gu[0:m, bank, tab, :], w[:, sw, i, f * P:f * P + m],
                                                 xs1[:, par, sx, i, :], start=(k == 0 and i == 0),
                                                 stop=(k == 2 and i == KT - 1))
                        for t in range(T1):
                            for g in range(2):
                                at = t * P + g * PAIR
                                col = tab * F + f * P
                                mm = nc.tensor.matmul(
                                    p_gu[0:m, bank, tab, at:at + PAIR],
                                    bg[:, 2 * t + g, col:col + m],
                                    ta_t[:, par, 2 * t + tab, (1 - g) * PAIR:(2 - g) * PAIR],
                                    start=False, stop=True, skip_group_check=True)
                    mm.then_inc(gu_ps, 1)

                def y_transposes(m, par):
                    pe.wait_ge(y_up, 2 * T1 * (m + 1))
                    wait(pe, base_up, m)
                    for t, p in enumerate((p_m1, p_a)):
                        for i in range(KT):
                            mm = nc.tensor.transpose(p[:, i * P:(i + 1) * P], y1[:, par, t, i * P:(i + 1) * P],
                                                     ident32[:])
                    mm.then_inc(yt_ps, 1)

                def project(m):
                    pe.wait_ge(yt_sb, 2 * m + 2)
                    for t in range(T1):
                        for i in range(KT):
                            mm = nc.tensor.matmul(p_m2[:, t * NPROJ:(t + 1) * NPROJ], yT[:, t, i, :], proj[:, i, :],
                                                  start=(i == 0), stop=(i == KT - 1))
                    mm.then_inc(lg_ps, 1)

                def pre_transposes(m):
                    pe.wait_ge(xp_up, m + 1)
                    for t in range(T1):
                        mm = nc.tensor.transpose(p_m2[:, t * P:(t + 1) * P], xpre[:, t, :], ident32[:])
                    mm.then_inc(xp_ps, 1)

                def branch_product(m):
                    pe.wait_ge(xp_sb, m + 1)
                    for t in range(T1):
                        mm = nc.tensor.matmul(p_m2[:, C1 + t * P:C1 + (t + 1) * P], xpre[:, t, :], branch[:],
                                              start=True, stop=True)
                    mm.then_inc(yb_ps, 1)

                def x_back(m, t):
                    if t == 0:
                        pe.wait_ge(xc_up, m + 1)
                    else:
                        pe.wait_ge(yb_sb, m + 1)
                    for i in range(KT):
                        mm = nc.tensor.transpose((p_m1, p_m2)[t][:, i * P:(i + 1) * P],
                                                 xc[:, i, t * P:(t + 1) * P], ident32[:])
                    mm.then_inc(xb_ps, 1)

                def down(n, par):
                    def act_w(t, i):
                        m = rows_of(i)
                        for k, (sx, sw) in enumerate(PASSES):
                            nc.tensor.matmul(p_y[:, t, :], acts[0:m, sx, i, t * P:(t + 1) * P],
                                             wd[0:m, sw, i, :], start=(i == 0 and k == 0), stop=False)

                    wait(pe, y_up, 2 * T1 * n)
                    for i in range(FT - 1):
                        pe.wait_ge(act_lo, n * FT + i + 1)
                        act_w(0, i)
                    a_rows(n + 1)
                    pe.wait_ge(got_ad, (n + 1) * (B1 * 16))
                    pe.wait_ge(ta_up, n + 2)
                    pe.wait_ge(act_lo, (n + 1) * FT)
                    for t in range(T1):
                        for i in range(FT):
                            m = rows_of(i)
                            for k, (sx, sa) in enumerate(PASSES):
                                mm = nc.tensor.matmul(
                                    p_a[:, t * 64:(t + 1) * 64], acts[0:m, sx, i, t * P:(t + 1) * P],
                                    ad[0:m, 4 * t:4 * t + 4, sa, i * RANK:(i + 1) * RANK],
                                    start=(i == 0 and k == 0), stop=(i == FT - 1 and k == 2))
                    mm.then_inc(td_ps, 1)
                    act_w(0, FT - 1)
                    for i in range(FT):
                        act_w(1, i)
                        if i == 7:
                            pe.wait_ge(td_lo, 2 * n + 2)
                            pe.wait_ge(tat_sb, n + 2)
                            for u in range(2 * T1):
                                mm = nc.tensor.transpose(
                                    p_at[:, u * P:(u + 1) * P],
                                    td_s[:, 2 * u:2 * u + 2, :, :].rearrange("p b s r -> p (b s r)"), ident16[:])
                            mm.then_inc(tdt_ps, 1)
                    pe.wait_ge(tdt_sb, n + 1)
                    pe.wait_ge(got_bd, (n + 1) * (B1 * 16))
                    for t in range(T1):
                        for g in range(2):
                            mm = nc.tensor.matmul(p_y[:, t, :], td_t[:, 2 * t + g, :], bd[:, 2 * t + g, :],
                                                  start=False, stop=(g == 1))
                        mm.then_inc(y_ps, 1)

                def step(n, par, first=False):
                    pe.wait_ge(tat_sb, n + 1)
                    pe.wait_ge(got_bg, n * (B1 * 16) + SP_BG * 32)
                    for f in range(FT):
                        gate_up(n, par, f)
                        if f == 6:
                            x_a(n + 1, 1 - par)
                        if not first:
                            if f == 0:
                                y_transposes(n - 1, 1 - par)
                            if f == 1:
                                project(n - 1)
                            if f == 5:
                                pre_transposes(n - 1)
                            if f == 7:
                                branch_product(n - 1)
                            if f == 8:
                                x_back(n - 1, 0)
                            if f == FT - 1:
                                x_back(n - 1, 1)
                    down(n, par)

                pe.wait_ge(got_first_a, (G1 - SP_AG) * 32)
                x_a(0, 0)
                a_rows(0)
                pe.wait_ge(got_first_b, (G1 - SP_BG) * 32)
                step(0, 0, first=True)
                step(1, 1)
                with pe.Fori(1, N1 // 2) as s:
                    step(2 * s, 0)
                    step(2 * s + 1, 1)
                y_transposes(N1 - 1, 1)
                project(N1 - 1)
                pre_transposes(N1 - 1)
                branch_product(N1 - 1)
                x_back(N1 - 1, 0)
                x_back(N1 - 1, 1)


def kernel(**inputs):
    import numpy as np
    import concourse.bacc as bacc
    from concourse.bass_utils import run_bass_kernel_spmd as run

    def get(name):
        return np.asarray(inputs[name])

    def columns(v):
        return v.reshape(KT, P).T

    def slots_a(t, slots, tiles):
        return t.reshape(slots, tiles, P, -1).transpose(2, 0, 1, 3)

    a_gu = np.stack([get("L1_cond_A_gate")[0], get("L1_cond_A_up")[0]], 1)
    a_gu = slots_a(a_gu.transpose(0, 3, 1, 2), SLOTS1, KT).reshape(P, SLOTS1, -1)
    a_d = np.zeros((SLOTS1, FT * P, RANK), np.float32)
    a_d[:, :F] = get("L1_cond_A_down")[0].transpose(0, 2, 1)
    a_d = slots_a(a_d, SLOTS1, FT).reshape(P, SLOTS1, -1)
    a1 = np.concatenate([a_gu, a_d], 2)
    wd = np.zeros((PIECES * DT_PIECE * P, D), np.float32)
    wd[:F] = get("L1_cond_W_down").T
    rows = [get(n)[0].transpose(0, 2, 1) for n in ("L1_cond_B_gate", "L1_cond_B_up", "L1_cond_B_down")]
    x = get("x").reshape(TOK, D)
    arrays = {
        "xT": x.T,
        "slot0": get("itok_B_0_23").reshape(1, BATCH),
        "slot1": get("itok_B_2_6").reshape(1, BATCH),
        "w0T": get("L0_cond_W").T,
        "b0": columns(get("L0_cond_b")),
        "a0": slots_a(get("L0_cond_lora_As"), SLOTS0, KT).reshape(P, -1),
        "b0t": get("L0_cond_lora_Bs").reshape(SLOTS0 * RANK, D),
        "chan": columns(get("L0_ffn_channel_scale").reshape(D)),
        "qT": get("L0_ffn_qweight").T,
        "perm": columns(get("L0_ffn_q_perm")),
        "scT": get("L0_ffn_scales").T,
        "zrT": get("L0_ffn_zeros").T,
        "fbias": columns(get("L0_ffn_bias")),
        "wgT": get("L1_cond_W_gate").T,
        "wuT": get("L1_cond_W_up").T,
        "wdT": wd,
        "a1": a1.reshape(P, PIECES, -1).transpose(1, 0, 2).reshape(PIECES * P, -1),
        "b1t": np.concatenate(rows, 2).reshape(2 * SLOTS1 * RANK, B1W // 2),
        "proj": np.concatenate([get("L1_ffn_W_res"), get("L1_ffn_W_pre"), get("L1_ffn_W_post")], 0).T,
        "base": np.concatenate([get("L1_ffn_H_res_base").reshape(-1), get("L1_ffn_H_pre_base"),
                                get("L1_ffn_H_post_base")]).reshape(1, NPROJ),
        "gate": get("L1_ffn_gate").reshape(1, 1),
        "branch": get("L1_ffn_W_branch"),
    }
    nc = bacc.Bacc("TRN2", target_bir_lowering=False, num_devices=1)
    arrays = {"in_" + n: np.ascontiguousarray(v) for n, v in arrays.items()}
    aps = {n[3:]: nc.dram_tensor(n, v.shape, mybir.dt.from_np(v.dtype), kind="ExternalInput").ap()
           for n, v in arrays.items()}
    out = nc.dram_tensor("out", (TOK, D), F32, kind="ExternalOutput").ap()
    build(nc, aps, out)
    r = run(nc, [arrays], core_ids=[0])
    return r.results[0]["out"].reshape(BATCH, SEQ, D)
```
